# Optimizing a Trainium2 kernel written in Bass

```python
import numpy as np
import jax
import jax.numpy as jnp

def _softmax(x, axis=-1):
    return jax.nn.softmax(x, axis=axis)

def _gelu(x):
    return jax.nn.gelu(x, approximate=True)

def _silu(x):
    return jax.nn.silu(x)

def _sigmoid(x):
    return jax.nn.sigmoid(x)

def _layernorm(x, axis=-1, eps=1e-05):
    m = jnp.mean(x, axis=axis, keepdims=True)
    v = jnp.var(x, axis=axis, keepdims=True)
    return (x - m) / jnp.sqrt(v + eps)

def _scatter_add(tgt, idx, src, axis=0):
    return tgt.at[idx].add(src)

def _segment_sum(src, seg, n):
    return jax.ops.segment_sum(src, seg, n)
kernel_name = 'mk_adaln_d1_jaxref_r8_646481'

def setup_inputs(seed: int=0):
    np.random.seed(seed)
    _w = jnp.asarray

    def _L0_attn_setup():
        import jax, jax.numpy as jnp
        import numpy as np
        B, N, E, H = (1, 512, 256, 16)
        D = E // H
        DEGREE = 4
        LN_EPS = 1e-05
        ROPE_BASE = 10000.0

        def rope_cos_sin(n, d):
            inv_freq = 1.0 / ROPE_BASE ** (jnp.arange(0, d, 2, dtype=jnp.float32) / d)
            t = jnp.arange(n, dtype=jnp.float32)[:, None] * inv_freq[None, :]
            return (jnp.cos(t), jnp.sin(t))

        def apply_rope(x, cos, sin):
            x1, x2 = jnp.split(x, 2, axis=-1)
            c = cos[None, :, None, :]
            s = sin[None, :, None, :]
            return jnp.concatenate([x1 * c - x2 * s, x1 * s + x2 * c], axis=-1)

        def layernorm(x, scale, bias, eps=LN_EPS):
            m = jnp.mean(x, axis=-1, keepdims=True)
            v = jnp.var(x, axis=-1, keepdims=True)
            return (x - m) * jax.lax.rsqrt(v + eps) * scale + bias

        def polynomial_attention(q, k, v, degree, is_causal):
            a = jnp.einsum('bhnd,bhmd->bhnm', q, k) ** degree
            if is_causal:
                a = jnp.tril(a)
            denom = jnp.sum(a, axis=-1, keepdims=True)
            return jnp.einsum('bhnm,bhmd->bhnd', a / denom, v)
        key = jax.random.key(seed)
        k0, k1, k2 = jax.random.split(key, 3)
        x = jax.random.normal(k0, (B, N, E), dtype=jnp.float32)
        w_qkv = jax.random.normal(k1, (E, 3 * E), dtype=jnp.float32) * (1.0 / np.sqrt(E))
        w_out = jax.random.normal(k2, (E, E), dtype=jnp.float32) * (1.0 / np.sqrt(E))
        ln_scale = jnp.ones((D,), dtype=jnp.float32)
        ln_bias = jnp.zeros((D,), dtype=jnp.float32)
        return {'x': x, 'w_qkv': w_qkv, 'w_out': w_out, 'ln_scale': ln_scale, 'ln_bias': ln_bias}
    _L0_attn_in = _L0_attn_setup()

    def _L0_ffn_setup():
        import jax, jax.numpy as jnp
        import numpy as np
        B, S, H = (2, 64, 256)
        E, I, K = (64, 176, 6)
        NS = 2
        SH_I = I * NS
        key = jax.random.key(seed)
        ks = jax.random.split(key, 6)
        s = 0.02
        return {'hidden_states': jax.random.normal(ks[0], (B, S, H), jnp.float32), 'gate_w': jax.random.normal(ks[1], (E, H), jnp.float32) * s, 'experts_w1': jax.random.normal(ks[2], (E, I, H), jnp.float32) * s, 'experts_w2': jax.random.normal(ks[3], (E, H, I), jnp.float32) * s, 'shared_gate_up': jax.random.normal(ks[4], (2 * SH_I, H), jnp.float32) * s, 'shared_down': jax.random.normal(ks[5], (H, SH_I), jnp.float32) * s}
    _L0_ffn_in = _L0_ffn_setup()
    _L0_c = _w((lambda *s: np.random.randn(*s).astype(np.float32) * 0.05)(8, 256))
    _L0_wmod = _w((lambda *s: np.random.randn(*s).astype(np.float32) * 0.05)(256, 6 * 256) * 256 ** (-0.5))
    _d = {'L0_attn_x': _L0_attn_in['x'], 'L0_attn_w_qkv': _L0_attn_in['w_qkv'], 'L0_attn_w_out': _L0_attn_in['w_out'], 'L0_attn_ln_scale': _L0_attn_in['ln_scale'], 'L0_attn_ln_bias': _L0_attn_in['ln_bias'], 'L0_ffn_gate_w': _L0_ffn_in['gate_w'], 'L0_ffn_experts_w1': _L0_ffn_in['experts_w1'], 'L0_ffn_experts_w2': _L0_ffn_in['experts_w2'], 'L0_ffn_shared_gate_up': _L0_ffn_in['shared_gate_up'], 'L0_ffn_shared_down': _L0_ffn_in['shared_down'], 'L0_c': _L0_c, 'L0_wmod': _L0_wmod}
    _x0 = _d['L0_attn_x']
    _d['L0_attn_x'] = jax.random.normal(jax.random.fold_in(jax.random.key(seed), 1), (8, 256, 256), dtype=_x0.dtype)
    del _x0
    return _d

def reference(L0_attn_x, L0_attn_w_qkv, L0_attn_w_out, L0_attn_ln_scale, L0_attn_ln_bias, L0_ffn_gate_w, L0_ffn_experts_w1, L0_ffn_experts_w2, L0_ffn_shared_gate_up, L0_ffn_shared_down, L0_c, L0_wmod):

    def _L0_attn_ref(x, w_qkv, w_out, ln_scale, ln_bias):
        import jax, jax.numpy as jnp
        import numpy as np
        B, N, E, H = (1, 512, 256, 16)
        D = E // H
        DEGREE = 4
        LN_EPS = 1e-05
        ROPE_BASE = 10000.0

        def rope_cos_sin(n, d):
            inv_freq = 1.0 / ROPE_BASE ** (jnp.arange(0, d, 2, dtype=jnp.float32) / d)
            t = jnp.arange(n, dtype=jnp.float32)[:, None] * inv_freq[None, :]
            return (jnp.cos(t), jnp.sin(t))

        def apply_rope(x, cos, sin):
            x1, x2 = jnp.split(x, 2, axis=-1)
            c = cos[None, :, None, :]
            s = sin[None, :, None, :]
            return jnp.concatenate([x1 * c - x2 * s, x1 * s + x2 * c], axis=-1)

        def layernorm(x, scale, bias, eps=LN_EPS):
            m = jnp.mean(x, axis=-1, keepdims=True)
            v = jnp.var(x, axis=-1, keepdims=True)
            return (x - m) * jax.lax.rsqrt(v + eps) * scale + bias

        def polynomial_attention(q, k, v, degree, is_causal):
            a = jnp.einsum('bhnd,bhmd->bhnm', q, k) ** degree
            if is_causal:
                a = jnp.tril(a)
            denom = jnp.sum(a, axis=-1, keepdims=True)
            return jnp.einsum('bhnm,bhmd->bhnd', a / denom, v)
        b, n, e = x.shape
        proj = x @ w_qkv
        q, k, v = jnp.split(proj, 3, axis=-1)
        q = q.reshape(b, n, H, D)
        k = k.reshape(b, n, H, D)
        v = v.reshape(b, n, H, D)
        cos, sin = rope_cos_sin(n, D)
        q = apply_rope(q, cos, sin)
        k = apply_rope(k, cos, sin)
        q = q.transpose(0, 2, 1, 3)
        k = k.transpose(0, 2, 1, 3)
        v = v.transpose(0, 2, 1, 3)
        q = layernorm(q, ln_scale, ln_bias)
        k = layernorm(k, ln_scale, ln_bias)
        out = polynomial_attention(q, k, v, DEGREE, True)
        out = out.transpose(0, 2, 1, 3).reshape(b, n, e)
        out = out @ w_out
        return out

    def _L0_ffn_ref(hidden_states, gate_w, experts_w1, experts_w2, shared_gate_up, shared_down):
        import jax, jax.numpy as jnp
        import numpy as np
        B, S, H = (2, 64, 256)
        E, I, K = (64, 176, 6)
        NS = 2
        SH_I = I * NS
        orig_shape = hidden_states.shape
        x = hidden_states.reshape(-1, orig_shape[-1])
        router_logits = x @ gate_w.T
        probs = jax.nn.softmax(router_logits, axis=-1)
        topk_w, topk_idx = jax.lax.top_k(probs, K)
        topk_w = topk_w / jnp.sum(topk_w, axis=-1, keepdims=True)
        combine = jnp.sum(jax.nn.one_hot(topk_idx, E, dtype=x.dtype) * topk_w[..., None], axis=1)
        h = jax.nn.silu(jnp.einsum('th,eih->tei', x, experts_w1))
        y = jnp.einsum('tei,ehi->teh', h, experts_w2)
        routed_out = jnp.einsum('teh,te->th', y, combine)
        gu = x @ shared_gate_up.T
        g, u = jnp.split(gu, 2, axis=-1)
        shared_out = jax.nn.silu(g) * u @ shared_down.T
        return (routed_out + shared_out).reshape(orig_shape)
    x = L0_attn_x
    mod = (_silu(L0_c) @ L0_wmod).reshape(L0_c.shape[0], 6, 1, -1)
    sa, ca, ga, sb, cb, gb = (mod[:, 0], mod[:, 1], mod[:, 2], mod[:, 3], mod[:, 4], mod[:, 5])
    ga = (2 * (ga >= 0) - 1) * jnp.maximum(jnp.abs(ga), 0.25)
    gb = (2 * (gb >= 0) - 1) * jnp.maximum(jnp.abs(gb), 0.25)
    h = _layernorm(x, axis=-1) * (1 + ca) + sa
    x = x + ga * _L0_attn_ref(h, L0_attn_w_qkv, L0_attn_w_out, L0_attn_ln_scale, L0_attn_ln_bias)
    h = _layernorm(x, axis=-1) * (1 + cb) + sb
    x = x + gb * _L0_ffn_ref(h, L0_ffn_gate_w, L0_ffn_experts_w1, L0_ffn_experts_w2, L0_ffn_shared_gate_up, L0_ffn_shared_down)
    return x

_drawn_inputs = setup_inputs


def setup_inputs(seed=0):
    import zlib

    import numpy as np

    out = dict(_drawn_inputs(seed))
    spreads = {'L0_attn_ln_scale': (1.0, 0.2), 'L0_attn_ln_bias': (0.0, 0.671)}
    factors = {'L0_ffn_gate_w': 8.0,
     'L0_ffn_experts_w1': 8.0,
     'L0_ffn_experts_w2': 8.0,
     'L0_ffn_shared_gate_up': 8.0,
     'L0_ffn_shared_down': 8.0}
    for name, (base, spread) in spreads.items():
        noise = np.random.default_rng([zlib.crc32(name.encode()), seed]).standard_normal(out[name].shape)
        drawn = base * np.exp(spread * noise) if base else spread * noise
        out[name] = jnp.asarray(drawn.astype(out[name].dtype))
    for name, factor in factors.items():
        out[name] = (out[name] * factor).astype(out[name].dtype)
    return out
```

```python
from contextlib import ExitStack

import concourse.bass as bass
from concourse import mybir

ALU = mybir.AluOpType
ACT = mybir.ActivationFunctionType
F32 = mybir.dt.float32
F16 = mybir.dt.float16
I32 = mybir.dt.int32
U32 = mybir.dt.uint32
AX_X = mybir.AxisListType.X

P = 128
B, N, E = 8, 256, 256
TOK = B * N
TILES = TOK // P
EC = E // P
HEADS, D = 16, 16
QK = 2 * E // P
GROUP = 512
TURNS = TOK // GROUP
TPG = GROUP // P
BPG = GROUP // N
NEXP, INNER, TOPK = 64, 176, 6
IC = 2
IP = INNER // IC
ROUTED_TILES = (TOK * TOPK + NEXP * (P - 1)) // P
RING = 4
SLOT_TILES = -(-ROUTED_TILES // RING) * RING
SHARED = 352
SH_CHUNKS = [(0, 128), (128, 128), (256, 96)]
EPS = 1e-5

CST = {}
_at = 0
for _name, _n in (("ident", P), ("centre", P), ("centre_swap", P), ("var", P), ("cos", N), ("sin", N),
                  ("even", 1), ("odd", 1), ("eps", 1), ("token", TILES), ("steps", TOK // P),
                  ("sel", B * P)):
    CST[_name] = (_at, _at + _n)
    _at += _n
NCST = _at
HST = {}
_at = 0
for _name, _n in (("before", P), ("ones", P), ("exp_before", NEXP), ("exp_upto", NEXP),
                  ("tiles", SLOT_TILES), ("slots", P)):
    HST[_name] = (_at, _at + _n)
    _at += _n
NHST = _at


def build(nc, x, w_qkv, w_out, ln_cols, gate_t, w1_t, w2_t, gu_t, down_t, c_t, wmod, cst, hst, out):
    with ExitStack() as ctx:
        def sb(name, shape, dt=F32):
            return ctx.enter_context(nc.sbuf_tensor(name, shape, dt))

        def sem(name):
            return ctx.enter_context(nc.semaphore(name))

        h2_dram = nc.dram_tensor("h2_rows", [TOK, E], F32, kind="Internal").ap()
        y_dram = nc.dram_tensor("expert_rows", [SLOT_TILES * P, E], F32, kind="Internal").ap()

        PS = ctx.enter_context(nc.psum_tensor("PS", [P, 8, 512], F32))

        cs = sb("cs", [P, NCST])
        hs = sb("hs", [P, NHST], F16)
        ln_col = sb("ln_col", [P, 2])
        ln_mask = sb("ln_mask", [P, 4])
        wqkv_sb = sb("wqkv_sb", [P, EC, 3 * E])
        wout_sb = sb("wout_sb", [P, EC, E])
        gate_sb = sb("gate_sb", [P, EC, NEXP])
        gu_sb = sb("gu_sb", [P, EC, 2 * SHARED])
        down_sb = sb("down_sb", [P, len(SH_CHUNKS), E])
        mod_col = sb("mod_col", [P, 2, EC, B])
        rows = sb("rows", [B, 4, E])
        mod_row = sb("mod_row", [P, B * 4 * E])
        x_all = sb("x_all", [P, TILES * E])
        h2T_all = sb("h2T_all", [P, EC, TOK])
        lg = sb("lg", [P, TILES * NEXP])
        mx = sb("mx", [P, TILES])
        zs = sb("zs", [P, TILES])
        p8 = sb("p8", [P, TILES, 8])
        slot_i = sb("slot_i", [P, TILES * 8], I32)
        slot_g = sb("slot_g", [P, TILES * 8], I32)
        slot_s = sb("slot_s", [P, TILES * 8], I32)
        col_g = sb("col_g", [P, TILES * 8])
        col_s = sb("col_s", [P, TILES * 8])
        tok_of = sb("tok_of", [P, SLOT_TILES], U32)
        n_col = sb("n_col", [NEXP, 1])
        n_cmp = sb("n_cmp", [NEXP, TILES])
        t_col = sb("t_col", [NEXP, 1])
        t_col16 = sb("t_col16", [NEXP, 1], F16)
        t_wide = sb("t_wide", [NEXP, P], F16)
        e_end = sb("e_end", [NEXP, 1])
        e_cmp = sb("e_cmp", [NEXP, SLOT_TILES], F16)
        e_row = sb("e_row", [1, SLOT_TILES])
        e_of = sb("e_of", [1, SLOT_TILES], I32)
        wk = sb("wk", [P, TOPK, TILES])
        early_stack = ExitStack()

        def early(name, shape, dt=F32):
            return early_stack.enter_context(nc.sbuf_tensor(name, shape, dt))

        modulation_stack = ExitStack()

        def modulation(name, shape, dt=F32):
            return modulation_stack.enter_context(nc.sbuf_tensor(name, shape, dt))

        wmod_sb = modulation("wmod_sb", [P, EC, 6 * E])
        cT = modulation("cT", [P, EC, B])
        silu_c = modulation("silu_c", [P, EC, B])
        rneg = modulation("rneg", [B, 2, E])
        rsgn = modulation("rsgn", [B, 2, E])
        modulation_stack.close()
        mod_now = early("mod_now", [P, 2, EC, BPG])
        st = early("st", [P, TPG, 6])
        mv = early("mv", [P, TPG, 2])
        sd = early("sd", [P, TPG])
        rstd = early("rstd", [P, TPG])
        xn = early("xn", [P, TPG, E])
        hT = early("hT", [P, EC, GROUP])
        rc = early("rc", [P, 2, GROUP])
        rs = early("rs", [P, 2, GROUP])
        sq = early("sq", [P, 2, GROUP])
        qsd = early("qsd", [P, 2, GROUP])
        qrs = early("qrs", [P, 2, GROUP])
        cn = early("cn", [P, 2, GROUP])
        q_even = early("q_even", [P, 2, GROUP])
        q_odd = early("q_odd", [P, 2, GROUP])
        kk = early("kk", [P, 2, GROUP])
        va = early("va", [P, TPG, HEADS, D + 1])
        s2 = early("s2", [P, 3, 2, 384])
        s4 = early("s4", [P, 3, 2, 384])
        rden = early("rden", [P, 2 * 8])
        o_sb = early("o_sb", [P, TPG, E])
        oT = early("oT", [P, 2, EC, P])
        gated = early("gated", [P, BPG, 2 * E])
        h2 = early("h2", [P, TPG, E])
        h2T = early("h2T", [P, EC, GROUP])
        early_stack.close()
        def late(name, shape, dt=F32):
            return ctx.enter_context(nc.sbuf_tensor(name, shape, dt))

        sh_all = late("sh_all", [P, TILES * E])
        ex = late("ex", [P, TILES, NEXP])
        pr = late("pr", [P, TILES, NEXP + 2])
        rep = late("rep", [P, TILES, NEXP + 2])
        comb = late("comb", [P, TILES, NEXP])
        pos1 = late("pos1", [P, TILES, NEXP])
        mask = late("mask", [P, TILES, NEXP], F16)
        cum = late("cum", [P, TILES, NEXP], F16)
        slot8 = late("slot8", [P, TILES, 8])
        hot_s = late("hot_s", [P, 2, TOPK, P], F16)
        hot_g = late("hot_g", [P, 2, TOPK, SLOT_TILES], F16)
        sg = late("sg", [P, 2, GROUP])
        su = late("su", [P, 2, GROUP])
        sact = late("sact", [P, len(SH_CHUNKS), GROUP])
        ti = late("ti", [P, RING], U32)
        xg = late("xg", [P, RING, E])
        xgT = late("xgT", [P, 2, EC, P])
        w1b = late("w1b", [P, RING, EC, INNER])
        w2b = late("w2b", [IP, RING, IC, E])
        hx = late("hx", [IP, 2, IC, P])
        yb = late("yb", [P, RING, E])
        ki = late("ki", [P, 2, TOPK], U32)
        yg = late("yg", [P, 2, TOPK, E])
        acc = late("acc", [P, 2, E])

        def C(name, rows_=P):
            a, b = CST[name]
            return cs[0:rows_, a:b]

        def H(name, rows_=P):
            a, b = HST[name]
            return hs[0:rows_, a:b]

        ident = C("ident")

        s_w = sem("weights_loaded")
        s_cst = sem("constants_loaded")
        s_x = sem("x_loaded")
        s_set = sem("buffers_set")
        s_silu = sem("silu_c_ready")
        s_modp = sem("mod_product")
        s_modc = sem("mod_columns")
        s_rowp = sem("rows_product")
        s_rows = sem("rows_ready")
        s_bc = sem("rows_broadcast")
        s_bce = sem("broadcast_copied")
        s_chain = sem("vector_steps")
        s_achain = sem("scalar_steps")
        s_turn = sem("vector_turn_steps")
        s_mv = sem("moments")
        s_sd = sem("deviation")
        s_xn = sem("normed")
        s_xnT = sem("normed_turned")
        s_now = sem("mod_now_ready")
        s_hT = sem("h_ready")
        s_proj = sem("qk_projected")
        s_rope = sem("rope_products")
        s_cent = sem("centred")
        s_sq = sem("squared")
        s_var = sem("variance")
        s_qsd = sem("head_deviation")
        s_cn = sem("head_normed")
        s_fa = sem("q_even_ready")
        s_fp = sem("q_odd_or_k_ready")
        s_v = sem("v_projected")
        s_va = sem("v_copied")
        s_sc = sem("scores")
        s_s2 = sem("scores_squared")
        s_msk = sem("scores_masked")
        s_s4 = sem("scores_fourth")
        s_av = sem("attended")
        s_on = sem("attention_normed")
        s_ot = sem("attention_turned")
        s_oT = sem("attention_turned_copied")
        s_ao = sem("attention_projected")
        s_mv2 = sem("moments2")
        s_sd2 = sem("deviation2")
        s_h2 = sem("h2_ready")
        s_h2d = sem("h2_stored")
        s_h2t = sem("h2_turned")
        s_h2T = sem("h2_turned_copied")
        s_h2k = sem("h2_turned_kept")
        s_lgp = sem("logits_product")
        s_lg = sem("logits_ready")
        s_ls = sem("logits_less_max")
        s_ex = sem("exp_ready")
        s_mask = sem("masks_ready")
        s_n = sem("expert_counts")
        s_t = sem("expert_tiles")
        s_pos = sem("positions")
        s_e = sem("expert_of_tile_sum")
        s_ec = sem("expert_compared")
        s_end = sem("expert_ends")
        s_eo = sem("expert_of_tile")
        s_hot = sem("one_hots")
        s_hotm = sem("one_hots_used")
        s_tok = sem("token_of_slot")
        s_gp = sem("shared_gate_product")
        s_up = sem("shared_up_product")
        s_sg = sem("shared_gate_copied")
        s_su = sem("shared_up_copied")
        s_sa = sem("shared_act")
        s_sp = sem("shared_down_product")
        s_sh = sem("shared_copied")
        s_ti = sem("tile_indices")
        s_xg = [sem(f"rows_gathered{i}") for i in range(RING)]
        s_w1 = [sem(f"w1_loaded{i}") for i in range(RING)]
        s_w2 = [sem(f"w2_loaded{i}") for i in range(RING)]
        s_yd = [sem(f"rows_stored{i}") for i in range(RING)]
        s_xt = sem("rows_turned")
        s_xT = sem("rows_turned_copied")
        s_m1 = sem("inner_product")
        s_hx = sem("inner_silu")
        s_m2 = sem("outer_product")
        s_yb = sem("outer_copied")
        s_ystored = sem("all_rows_stored")
        s_slots = sem("slots_ready")
        s_ki = sem("choice_indices")
        s_yg = [sem(f"choices_gathered{i}") for i in range(2)]
        s_acc = sem("choices_summed")
        s_fin = sem("rows_final")
        s_out = [sem(f"out_stored{i}") for i in range(2)]
        s_wait = sem("waited")

        def then(eng, semaphore, value):
            eng.wait_ge(semaphore, value)
            eng.sem_inc(s_wait, 1)

        def project_out(pe, t, j):
            pe.wait_ge(s_oT, 4 * j + t + 1)
            for c in range(EC):
                last = nc.tensor.matmul(PS[:, 2 + t // 2, (t % 2) * E:(t % 2 + 1) * E], oT[:, t % 2, c, :],
                                        wout_sb[:, c, :], start=(c == 0), stop=(c == EC - 1))
            last.then_inc(s_ao, 1)

        def heads_norm(dve, j, idx, next_):
            v = nc.vector
            bb, f = idx // 2, idx % 2
            dve.wait_ge(s_av, 16 * j + 4 * idx + 4)
            o = PS[:, 6 + f, 0:2 * 8 * (D + 1)].rearrange("p (m d) -> p m d", d=D + 1)
            next_(v.reciprocal(rden[:, :], o[:, :, D]))
            v.tensor_tensor(o_sb[:, 2 * bb:2 * bb + 2, f * P:(f + 1) * P].rearrange("p t (h d) -> p t h d", d=D),
                            o[:, :, 0:D].rearrange("p (t h) d -> p t h d", t=2),
                            rden[:, :].rearrange("p (t h) -> p t h", t=2).unsqueeze(3).broadcast_to([P, 2, 8, D]),
                            ALU.mult).then_inc(s_on, 1)

        N_W = 9
        block = ctx.enter_context(nc.Block())

        @block.sync
        def _(sp):
            sp.dma_start(cT[:, :, :], c_t.rearrange("(c p) b -> p c b", p=P)).then_inc(s_w, 16)
            sp.dma_start(wmod_sb[:, :, :], wmod.rearrange("(c p) n -> p c n", p=P)).then_inc(s_w, 16)
            sp.dma_start(cs[:, :], cst).then_inc(s_cst, 16)
            sp.dma_start(x_all[:, :].rearrange("p (t f) -> p t f", f=E),
                         x.rearrange("(t p) f -> p t f", p=P)).then_inc(s_x, 16)
            sp.dma_start(wqkv_sb[:, :, :], w_qkv.rearrange("(c p) n -> p c n", p=P)).then_inc(s_w, 16)
            sp.dma_start(ln_col[:, :], ln_cols).then_inc(s_w, 16)
            sp.dma_start(wout_sb[:, :, :], w_out.rearrange("(c p) n -> p c n", p=P)).then_inc(s_w, 16)
            sp.dma_start(gate_sb[:, :, :], gate_t.rearrange("(c p) n -> p c n", p=P)).then_inc(s_w, 16)
            sp.dma_start(hs[:, :], hst).then_inc(s_cst, 16)
            sp.dma_start(gu_sb[:, :, :], gu_t.rearrange("(c p) n -> p c n", p=P)).then_inc(s_w, 16)
            sp.dma_start(down_sb[:, 0:2, :], down_t[0:2 * P].rearrange("(c p) n -> p c n", p=P)).then_inc(s_w, 16)
            sp.dma_start(down_sb[0:SHARED - 2 * P, 2, :], down_t[2 * P:SHARED]).then_inc(s_w, 16)
            with sp.Fori(0, TURNS) as j:
                then(sp, s_h2, 2 * j + 2)
                sp.dma_start(h2_dram[bass.ds(j * GROUP, GROUP), :].rearrange("(t p) f -> p t f", p=P),
                             h2[:, :, :]).then_inc(s_h2d, 16)
            sp.wait_ge(s_eo, 1)
            sp.wait_ge(s_h2d, 16 * TURNS + 16)
            sp.wait_ge(s_h2k, TURNS)

            def load(tile, rnd, slot):
                e = sp.value_load(e_of[0:1, bass.ds(tile, 1)] if rnd is not None else e_of[0:1, tile:tile + 1],
                                  min_val=0, max_val=NEXP - 1)
                if rnd is not None:
                    then(sp, s_m1, tile - RING + 1)
                sp.dma_start(w1b[:, slot, :, :], w1_t[bass.ds(e, 1)].rearrange("a (c p) i -> p (a c) i", p=P))\
                    .then_inc(s_w1[slot], 16)
                if rnd is not None:
                    then(sp, s_m2, tile - RING + 1)
                sp.dma_start(w2b[:, slot, :, :], w2_t[bass.ds(e, 1)].rearrange("a (c p) h -> p (a c) h", p=IP))\
                    .then_inc(s_w2[slot], 16)

            for slot in range(RING):
                load(slot, None, slot)
            with sp.Fori(1, SLOT_TILES // RING) as r:
                for slot in range(RING):
                    load(r * RING + slot, r, slot)
            with sp.Fori(0, TILES // 2) as r:
                for b in range(2):
                    then(sp, s_fin, 2 * r + b + 1)
                    sp.dma_start(out[bass.ds((2 * r + b) * P, P), :], acc[:, b, :]).then_inc(s_out[b], 16)
            for b in range(2):
                sp.wait_ge(s_out[b], 16 * (TILES // 2))

        @block.tensor
        def _(pe):
            mm = nc.tensor.matmul

            pe.wait_ge(s_silu, 1)
            pe.wait_ge(s_w, 16 * N_W)
            pe.wait_ge(s_cst, 32)
            for kind in range(2):
                for c in range(EC):
                    at = (kind * EC + c) * B
                    for k in range(EC):
                        last = mm(PS[:, 0, at:at + B], wmod_sb[:, k, kind * E + c * P:kind * E + (c + 1) * P],
                                  silu_c[:, k, :], start=(k == 0), stop=(k == EC - 1))
            last.then_inc(s_modp, 1)
            for half in range(2):
                for k in range(EC):
                    last = mm(PS[0:B, 1 + half, :], silu_c[:, k, :],
                              wmod_sb[:, k, (2 + 2 * half) * E:(4 + 2 * half) * E], start=(k == 0), stop=(k == EC - 1))
            last.then_inc(s_rowp, 1)
            pe.wait_ge(s_rows, 1)
            pe.wait_ge(s_modc, 1)
            sel = C("sel", B)
            for b in range(B):
                for half in range(2):
                    n = 2 * b + half
                    if n >= 4:
                        pe.wait_ge(s_bce, n - 3)
                    mm(PS[:, 4 + n % 4, :], sel[:, b * P:(b + 1) * P],
                       rows[:, 2 * half:2 * half + 2, :].rearrange("b k f -> b (k f)"),
                       start=True, stop=True).then_inc(s_bc, 1)
            pe.wait_ge(s_bce, 2 * B)

            with pe.Fori(0, TURNS) as j:
                for t in range(TPG):
                    pe.wait_ge(s_xn, TPG * j + t + 1)
                    for c in range(EC):
                        last = nc.tensor.transpose(PS[:, t // 2, c * N + t % 2 * P:c * N + (t % 2 + 1) * P], xn[:, t, c * P:(c + 1) * P], ident)
                    last.then_inc(s_xnT, 1)

                def proj(u):
                    if u >= 2:
                        pe.wait_ge(s_rope, 4 * j + u - 1)
                    for k in range(EC):
                        last = mm(PS[:, 2 + u % 2, :], wqkv_sb[:, k, u * P:(u + 1) * P], hT[:, k, :],
                                  start=(k == 0), stop=(k == EC - 1))
                    last.then_inc(s_proj, 1)

                def values(t):
                    for k in range(EC):
                        last = mm(PS[:, t // 2, (t % 2) * E:(t % 2 + 1) * E], hT[:, k, t * P:(t + 1) * P],
                                  wqkv_sb[:, k, 2 * E:3 * E], start=(k == 0), stop=(k == EC - 1))
                    last.then_inc(s_v, 1)

                def centre(u):
                    pe.wait_ge(s_rope, 4 * j + u + 1)
                    if u >= 2:
                        pe.wait_ge(s_cn, 4 * j + u - 1)
                    mm(PS[:, 4 + u % 2, :], C("centre"), rc[:, u % 2, :], start=True, stop=False)
                    mm(PS[:, 4 + u % 2, :], C("centre_swap"), rs[:, u % 2, :], start=False, stop=True)\
                        .then_inc(s_cent, 1)

                def variance(u):
                    pe.wait_ge(s_sq, 4 * j + u + 1)
                    if u >= 2:
                        pe.wait_ge(s_qsd, 4 * j + u - 1)
                    mm(PS[:, 6 + u % 2, :], C("var"), sq[:, u % 2, :], start=True, stop=True).then_inc(s_var, 1)

                pe.wait_ge(s_hT, 4 * j + 4)
                proj(0)
                proj(1)
                values(0)
                values(1)
                centre(0)
                proj(2)
                values(2)
                variance(0)
                centre(1)
                proj(3)
                values(3)
                variance(1)
                for u in (2, 3):
                    centre(u)
                    variance(u)

                def unit(n):
                    bb, f, par, half = n // 8, n // 4 % 2, n // 2 % 2, n % 2
                    return bb, f, par, half

                def scores(n):
                    bb, f, par, half = unit(n)
                    if n >= 3:
                        pe.wait_ge(s_s2, 16 * j + n - 2)
                    q = q_odd if par else q_even
                    at = bb * N
                    for key in range(2):
                        for r in range(2):
                            g = 32 * (2 * half + r)
                            bank = 2 * (n % 3) + r
                            if key == 0:
                                last = mm(PS[:, bank, :].rearrange("p (a n) -> p a n", a=2)[:, :, 0:P],
                                          kk[g:g + 32, f, at:at + P], q[g:g + 32, f, at:at + N],
                                          start=True, stop=True)
                            else:
                                last = mm(PS[:, bank, P:2 * P], kk[g:g + 32, f, at + P:at + N],
                                          q[g:g + 32, f, at + P:at + N], start=True, stop=True)
                    last.then_inc(s_sc, 1)

                def attend(n):
                    bb, f, par, half = unit(n)
                    pe.wait_ge(s_s4, 16 * j + n + 1)
                    if n % 4 == 0 and n >= 8:
                        pe.wait_ge(s_on, 4 * j + n // 4 - 1)
                    o = PS[:, 6 + f, 0:2 * 8 * (D + 1)].rearrange("p (t h d) -> p t h d", t=2, h=8)
                    for r in range(2):
                        h8 = 2 * (2 * half + r) + par
                        v0, v1 = (va[:, 2 * bb + m, 8 * f + h8, :] for m in range(2))
                        a = s4[:, n % 3, r, :]
                        mm(o[:, 0, h8, :], a[:, 0:P], v0, start=True, stop=True)
                        mm(o[:, 1, h8, :], a[:, 2 * P:3 * P], v0, start=True, stop=False)
                        last = mm(o[:, 1, h8, :], a[:, P:2 * P], v1, start=False, stop=True)
                    last.then_inc(s_av, 1)

                pe.wait_ge(s_set, 2)
                pe.wait_ge(s_va, 2 * j + 2)
                pe.wait_ge(s_fa, 2 * j + 2)
                pe.wait_ge(s_fp, 4 * j + 4)
                scores(0)
                scores(1)
                for n in range(16):
                    if n + 2 < 16:
                        scores(n + 2)
                    attend(n)

                for t in range(TPG):
                    if t % 2 == 0:
                        pe.wait_ge(s_on, 4 * j + t + 2)
                    if t >= 2:
                        pe.wait_ge(s_oT, 4 * j + t - 1)
                    for c in range(EC):
                        last = nc.tensor.transpose(PS[:, t % 2, c * P:(c + 1) * P], o_sb[:, t, c * P:(c + 1) * P], ident)
                    last.then_inc(s_ot, 1)
                    if t >= 1:
                        project_out(pe, t - 1, j)
                project_out(pe, TPG - 1, j)

                for t in range(TPG):
                    if t % 2 == 0:
                        pe.wait_ge(s_h2, 2 * j + t // 2 + 1)
                    for c in range(EC):
                        last = nc.tensor.transpose(PS[:, 4 + c, t * P:(t + 1) * P], h2[:, t, c * P:(c + 1) * P], ident)
                last.then_inc(s_h2t, 1)
                pe.wait_ge(s_h2T, j + 1)
                for t in range(TPG):
                    for k in range(EC):
                        last = mm(PS[:, 6, t * NEXP:(t + 1) * NEXP], h2T[:, k, t * P:(t + 1) * P], gate_sb[:, k, :],
                                  start=(k == 0), stop=(k == EC - 1))
                last.then_inc(s_lgp, 1)

            pe.wait_ge(s_mask, 1)
            for i in range(TILES):
                last = mm(PS[0:NEXP, 0, 0:1], mask[:, i, :], H("ones")[:, 0:1], start=(i == 0), stop=(i == TILES - 1))
            last.then_inc(s_n, 1)
            pe.wait_ge(s_mask, 2)
            pe.wait_ge(s_t, 1)
            for half in range(2):
                tt = slice(8 * half, 8 * half + 8)
                o = PS[:, 1 + half, :]
                mm(o, H("before"), mask[:, tt, :].rearrange("p t e -> p (t e)"), start=True, stop=False)
                mm(o, H("ones"), cum[:, tt, :].rearrange("p t e -> p (t e)"), start=False, stop=False)
                last = mm(o, t_wide[:, :], H("exp_before", NEXP).unsqueeze(1).broadcast_to([NEXP, 8, NEXP]),
                          start=False, stop=True)
            last.then_inc(s_pos, 1)
            mm(PS[0:NEXP, 3, 0:1], H("exp_upto", NEXP), t_col16[:, :], start=True, stop=True).then_inc(s_end, 1)
            pe.wait_ge(s_ec, 1)
            mm(PS[0:1, 4, 0:SLOT_TILES], H("ones", NEXP)[:, 0:1], e_cmp[:, :], start=True, stop=True).then_inc(s_e, 1)

            pe.wait_ge(s_h2k, TURNS)
            with pe.Fori(0, TURNS) as j:
                for i, (c0, cn_) in enumerate(SH_CHUNKS):
                    n = 3 * j + i
                    for which, (bank, done, used) in enumerate(((5, s_gp, s_sg), (6, s_up, s_su))):
                        if i >= 1:
                            pe.wait_ge(used, n)
                        w0 = which * SHARED + c0
                        for k in range(EC):
                            last = mm(PS[0:cn_, bank, :], gu_sb[:, k, w0:w0 + cn_],
                                      h2T_all[:, k, bass.ds(j * GROUP, GROUP)], start=(k == 0), stop=(k == EC - 1))
                        last.then_inc(done, 1)
                pe.wait_ge(s_sa, 3 * j + 3)
                for t in range(TPG):
                    if t >= 1:
                        pe.wait_ge(s_sh, 4 * j + t)
                    for i, (c0, cn_) in enumerate(SH_CHUNKS):
                        last = mm(PS[:, 7, 0:E], sact[0:cn_, i, t * P:(t + 1) * P], down_sb[0:cn_, i, :],
                                  start=(i == 0), stop=(i == len(SH_CHUNKS) - 1))
                    last.then_inc(s_sp, 1)
                pe.wait_ge(s_sh, 4 * j + 4)

            def collect(n, b, first=False, final=False):
                pe.wait_ge(s_hot, n + 1)
                for k in range(TOPK):
                    last = mm(PS[:, 3, 0:SLOT_TILES], hot_s[:, b, k, :], hot_g[:, b, k, :],
                              start=(first and k == 0), stop=(final and k == TOPK - 1))
                last.then_inc(s_hotm, 1)

            collect(0, 0, first=True)
            collect(1, 1)
            with pe.Fori(1, TILES // 2 - 1) as r:
                for b in range(2):
                    collect(2 * r + b, b)
            collect(TILES - 2, 0)
            collect(TILES - 1, 1, final=True)

            def turn(tile, rnd, slot):
                pe.wait_ge(s_xg[slot], 16 * (rnd + 1))
                b = slot % 2
                for c in range(EC):
                    last = nc.tensor.transpose(PS[:, b, c * P:(c + 1) * P], xg[:, slot, c * P:(c + 1) * P], ident)
                last.then_inc(s_xt, 1)

            def inner(tile, rnd, slot):
                b = slot % 2
                pe.wait_ge(s_xT, tile + 1)
                pe.wait_ge(s_w1[slot], 16 * (rnd + 1))
                for i in range(IC):
                    for c in range(EC):
                        last = mm(PS[0:IP, 4 + b, i * P:(i + 1) * P], w1b[:, slot, c, i * IP:(i + 1) * IP],
                                  xgT[:, b, c, :], start=(c == 0), stop=(c == EC - 1))
                last.then_inc(s_m1, 1)

            def outer(tile, rnd, slot, first=False):
                b = slot % 2
                pe.wait_ge(s_hx, tile + 1)
                pe.wait_ge(s_w2[slot], 16 * (rnd + 1))
                if not first:
                    pe.wait_ge(s_yb, tile - 1)
                for i in range(IC):
                    last = mm(PS[:, 6 + b, 0:E], hx[:, b, i, :], w2b[:, slot, i, :],
                              start=(i == 0), stop=(i == IC - 1))
                last.then_inc(s_m2, 1)

            turn(0, 0, 0)
            turn(1, 0, 1)
            inner(0, 0, 0)
            LOOPS = SLOT_TILES // RING - 1
            def step(g, q, r, **kw):
                turn(g + 1, q + (r + 1) // RING, (r + 1) % RING)
                inner(g, q + r // RING, r % RING)
                outer(g - 1, q + (r - 1) // RING, (r - 1) % RING, **kw)
            for g in (1, 2):
                step(g, 0, g, first=True)
            with pe.Fori(0, LOOPS) as q:
                for r in range(3, 3 + RING):
                    step(RING * q + r, q, r)
            g = SLOT_TILES - 1
            inner(g, g // RING, g % RING)
            outer(g - 1, (g - 1) // RING, (g - 1) % RING)
            outer(g, g // RING, g % RING)

        @block.scalar
        def _(act):
            a = nc.scalar.activation
            act.wait_ge(s_w, 16 * N_W)
            act.wait_ge(s_cst, 32)
            a(silu_c[:, :, :], cT[:, :, :], ACT.Silu).then_inc(s_silu, 1)
            for n in range(2 * B):
                act.wait_ge(s_bc, n + 1)
                a(mod_row[:, n * 2 * E:(n + 1) * 2 * E], PS[:, 4 + n % 4, :], ACT.Copy).then_inc(s_bce, 1)
            eps = C("eps")
            with act.Fori(0, TURNS) as j:
                act.wait_ge(s_mv, j + 1)
                a(sd[:, :], mv[:, :, 1], ACT.Sqrt, bias=eps).then_inc(s_sd, 1)
                act.wait_ge(s_now, j + 1)
                for bb in range(BPG):
                    act.wait_ge(s_xnT, 4 * j + 2 * bb + 2)
                    for c in range(EC):
                        a(hT[:, c, bb * N:(bb + 1) * N], PS[:, bb, c * N:(c + 1) * N], ACT.Identity,
                          bias=mod_now[:, 0, c, bb:bb + 1], scale=mod_now[:, 1, c, bb:bb + 1]).then_inc(s_hT, 1)

                def squares(u):
                    act.wait_ge(s_cent, 4 * j + u + 1)
                    if u >= 2:
                        act.wait_ge(s_var, 4 * j + u - 1)
                    a(sq[:, u % 2, :], PS[:, 4 + u % 2, :], ACT.Square).then_inc(s_sq, 1)

                def deviation(u):
                    act.wait_ge(s_var, 4 * j + u + 1)
                    if u >= 2:
                        act.wait_ge(s_cn, 4 * j + u - 1)
                    a(qsd[:, u % 2, :], PS[:, 6 + u % 2, :], ACT.Sqrt, bias=eps).then_inc(s_qsd, 1)

                def even(u):
                    act.wait_ge(s_cn, 4 * j + u + 1)
                    a(q_even[:, u, :], cn[:, u % 2, :], ACT.Identity,
                      scale=ln_mask[:, 0:1], bias=ln_mask[:, 1:2]).then_inc(s_fa, 1)

                def copy_v(i):
                    act.wait_ge(s_v, 4 * j + 2 * i + 2)
                    a(va[:, 2 * i:2 * i + 2, :, 0:D].rearrange("p t h d -> p (t h) d"),
                      PS[:, i, :].rearrange("p (h d) -> p h d", d=D), ACT.Copy).then_inc(s_va, 1)

                copy_v(0)
                squares(0)
                deviation(0)
                squares(1)
                even(0)
                copy_v(1)
                deviation(1)
                squares(2)
                even(1)
                deviation(2)
                squares(3)
                deviation(3)

                for n in range(16):
                    act.wait_ge(s_sc, 16 * j + n + 1)
                    if n >= 3:
                        act.wait_ge(s_s4, 16 * j + n - 2)
                    a(s2[:, n % 3, :, :], PS[:, 2 * (n % 3):2 * (n % 3) + 2, 0:384], ACT.Square).then_inc(s_s2, 1)

                for t in range(TPG):
                    act.wait_ge(s_ot, 4 * j + t + 1)
                    if t >= 2:
                        act.wait_ge(s_ao, 4 * j + t - 1)
                    a(oT[:, t % 2, :, :].rearrange("p c n -> p (c n)"), PS[:, t % 2, 0:E], ACT.Copy).then_inc(s_oT, 1)
                for bb in range(BPG):
                    act.wait_ge(s_mv2, 2 * j + bb + 1)
                    a(sd[:, 2 * bb:2 * bb + 2], mv[:, 2 * bb:2 * bb + 2, 1], ACT.Sqrt, bias=eps).then_inc(s_sd2, 1)
                act.wait_ge(s_h2t, j + 1)
                a(h2T[:, :, :], PS[:, 4:6, :], ACT.Copy).then_inc(s_h2T, 1)
                act.wait_ge(s_lgp, j + 1)
                a(lg[:, bass.ds(j * TPG * NEXP, TPG * NEXP)], PS[:, 6, 0:TPG * NEXP], ACT.Copy).then_inc(s_lg, 1)

            act.wait_ge(s_ls, 1)
            a(ex[:, :, :], ex[:, :, :], ACT.Exp).then_inc(s_ex, 1)

            with act.Fori(0, TURNS) as j:
                for i, (c0, cn_) in enumerate(SH_CHUNKS):
                    n = 3 * j + i
                    act.wait_ge(s_gp, n + 1)
                    if i >= 2:
                        act.wait_ge(s_sa, n - 1)
                    a(sg[0:cn_, i % 2, :], PS[0:cn_, 5, :], ACT.Silu).then_inc(s_sg, 1)
                    act.wait_ge(s_up, n + 1)
                    a(su[0:cn_, i % 2, :], PS[0:cn_, 6, :], ACT.Copy).then_inc(s_su, 1)
                for t in range(TPG):
                    act.wait_ge(s_sp, 4 * j + t + 1)
                    a(sh_all[:, bass.ds((4 * j + t) * E, E)], PS[:, 7, 0:E], ACT.Copy).then_inc(s_sh, 1)

            def silu(tile, slot, first=False):
                b = slot % 2
                act.wait_ge(s_m1, tile + 1)
                if not first:
                    act.wait_ge(s_m2, tile - 1)
                a(hx[:, b, :, :].rearrange("p i n -> p (i n)"), PS[0:IP, 4 + b, 0:IC * P], ACT.Silu).then_inc(s_hx, 1)

            def store(tile, slot):
                act.wait_ge(s_yb, tile + 1)
                act.dma_start(y_dram[bass.ds(tile * P, P), :], yb[:, slot, :]).then_inc(s_yd[slot], 16)

            silu(0, 0, first=True)
            silu(1, 1, first=True)
            silu(2, 2)
            store(0, 0)
            with act.Fori(0, SLOT_TILES // RING - 1) as q:
                for r in range(3, 3 + RING):
                    silu(RING * q + r, r % RING)
                    store(RING * q + r - 2, (r - 2) % RING)
            g = SLOT_TILES - 1
            silu(g, g % RING)
            for t in (g - 2, g - 1, g):
                store(t, t % RING)
            for slot in range(RING):
                act.wait_ge(s_yd[slot], 16 * (SLOT_TILES // RING))
            act.sem_inc(s_ystored, 1)

        @block.vector
        def _(dve):
            v = nc.vector
            steps = [0]

            def link(ins):
                steps[0] += 1
                ins.then_inc(s_chain, 1)
                dve.wait_ge(s_chain, steps[0])

            dve.sem_inc(s_h2d, 16)
            dve.wait_ge(s_w, 16 * N_W)
            dve.wait_ge(s_cst, 32)
            v.tensor_scalar(ln_mask[:, 0:2], ln_col[:, :], C("even"), None, ALU.mult)
            v.tensor_scalar(ln_mask[:, 2:4], ln_col[:, :], C("odd"), None, ALU.mult).then_inc(s_set, 1)
            dve.wait_ge(s_modp, 1)
            both = PS[:, 0, 0:2 * EC * B]
            v.tensor_copy(mod_col[:, 0, :, :].rearrange("p c b -> p (c b)"), both[:, 0:EC * B])
            v.tensor_scalar(mod_col[:, 1, :, :].rearrange("p c b -> p (c b)"), both[:, EC * B:2 * EC * B], 1.0, None,
                            ALU.add).then_inc(s_modc, 1)
            dve.wait_ge(s_rowp, 1)
            v.tensor_copy(rows[:, 0:2, :].rearrange("b k f -> b (k f)"), PS[0:B, 1, :])
            v.tensor_scalar(rows[:, 2, :], PS[0:B, 2, 0:E], 1.0, None, ALU.add)
            link(v.tensor_copy(rows[:, 3, :], PS[0:B, 2, E:2 * E]))
            gates = rows[:, 0:4:3, :]
            v.tensor_scalar(rneg[:, :, :], gates, -1.0, None, ALU.mult)
            link(v.tensor_scalar(rsgn[:, :, :], gates, 0.0, 2.0, ALU.is_ge, ALU.mult))
            link(v.tensor_tensor(rneg[:, :, :], gates, rneg[:, :, :], ALU.max))
            link(v.tensor_scalar(rneg[:, :, :], rneg[:, :, :], 0.25, None, ALU.max))
            link(v.tensor_scalar(rsgn[:, :, :], rsgn[:, :, :], -1.0, None, ALU.add))
            v.tensor_tensor(gates, rsgn[:, :, :], rneg[:, :, :], ALU.mult).then_inc(s_rows, 1)
            dve.wait_ge(s_x, 16)
            dve.wait_ge(s_modc, 1)
            dve.wait_ge(s_bce, 2 * B)
            v.memset(va[:, :, :, D:D + 1].rearrange("p t h d -> p (t h) d"), 1.0).then_inc(s_set, 1)

            PER = 22
            with dve.Fori(0, TURNS) as j:
                done = [0]

                def next_(ins):
                    done[0] += 1
                    ins.then_inc(s_turn, 1)
                    dve.wait_ge(s_turn, j * PER + done[0])

                def moments(ts):
                    for t in ts:
                        ins = v.bn_stats(st[:, t, :], x_all[:, bass.ds((TPG * j + t) * E, E)])
                    done[0] += 1
                    ins.then_inc(s_turn, 1)
                    then(dve, s_turn, j * PER + done[0])
                    for t in ts:
                        ins = v.bn_aggr(mv[:, t, :], st[:, t, :])
                    return ins

                moments(range(TPG)).then_inc(s_mv, 1)
                v.tensor_copy(mod_now[:, :, :, :].rearrange("p k c b -> p (k c) b"),
                              mod_col[:, :, :, :].rearrange("p k c b -> p (k c) b")[:, :, bass.ds(BPG * j, BPG)])\
                    .then_inc(s_now, 1)
                dve.wait_ge(s_sd, j + 1)
                next_(v.reciprocal(rstd[:, :], sd[:, :]))
                for t in range(TPG):
                    v.tensor_scalar(xn[:, t, :], x_all[:, bass.ds((TPG * j + t) * E, E)], mv[:, t, 0:1],
                                    rstd[:, t:t + 1], ALU.subtract, ALU.mult).then_inc(s_xn, 1)
                cos = C("cos").unsqueeze(1).broadcast_to([P, BPG, N])
                sin = C("sin").unsqueeze(1).broadcast_to([P, BPG, N])

                def two(ap):
                    return ap.rearrange("p (b n) -> p b n", b=BPG)

                def rope(u):
                    dve.wait_ge(s_proj, 4 * j + u + 1)
                    if u >= 2:
                        dve.wait_ge(s_cent, 4 * j + u - 1)
                    v.tensor_tensor(two(rc[:, u % 2, :]), two(PS[:, 2 + u % 2, :]), cos, ALU.mult)
                    v.tensor_tensor(two(rs[:, u % 2, :]), two(PS[:, 2 + u % 2, :]), sin, ALU.mult).then_inc(s_rope, 1)

                def norm(u):
                    dve.wait_ge(s_qsd, 4 * j + u + 1)
                    next_(v.reciprocal(qrs[:, u % 2, :], qsd[:, u % 2, :]))
                    if u >= 2:
                        dve.wait_ge(s_fp, 4 * j + u - 1)
                        dve.wait_ge(s_fa, 2 * j + u - 1)
                    v.tensor_tensor(cn[:, u % 2, :], PS[:, 4 + u % 2, :], qrs[:, u % 2, :], ALU.mult).then_inc(s_cn, 1)

                rope(0)
                rope(1)
                rope(2)
                norm(0)
                rope(3)
                for u in (1, 2, 3):
                    norm(u)

                for n in range(16):
                    dve.wait_ge(s_msk, 16 * j + n + 1)
                    if n >= 3:
                        dve.wait_ge(s_av, 16 * j + n - 2)
                    flat = "p r n -> p (r n)"
                    v.tensor_tensor(s4[:, n % 3, :, :].rearrange(flat), s2[:, n % 3, :, :].rearrange(flat),
                                    s2[:, n % 3, :, :].rearrange(flat), ALU.mult).then_inc(s_s4, 1)
                    if n % 4 == 1 and n >= 4:
                        heads_norm(dve, j, n // 4 - 1, next_)
                heads_norm(dve, j, 3, next_)

                for bb in range(BPG):
                    mrow = (BPG * j + bb) * 4 * E

                    def row(kind):
                        return mod_row[:, bass.ds(mrow + kind * E, E)].unsqueeze(1).broadcast_to([P, 2, E])

                    def tiles(ap):
                        return ap.rearrange("p (t f) -> p t f", t=2)

                    xs = tiles(x_all[:, bass.ds((TPG * j + 2 * bb) * E, 2 * E)])
                    dve.wait_ge(s_ao, 4 * j + 2 * bb + 2)
                    next_(v.tensor_tensor(tiles(gated[:, bb, :]), tiles(PS[:, 2 + bb, :]), row(0), ALU.mult))
                    v.tensor_tensor(xs, tiles(gated[:, bb, :]), xs, ALU.add).then_inc(s_turn, 1)
                    done[0] += 1
                    then(dve, s_turn, j * PER + done[0])
                    moments((2 * bb, 2 * bb + 1)).then_inc(s_mv2, 1)
                    dve.wait_ge(s_sd2, 2 * j + bb + 1)
                    next_(v.reciprocal(rstd[:, 2 * bb:2 * bb + 2], sd[:, 2 * bb:2 * bb + 2]))
                    if bb == 0:
                        dve.wait_ge(s_h2d, 16 * j + 16)
                    for t in (2 * bb, 2 * bb + 1):
                        ins = v.tensor_scalar(h2[:, t, :], x_all[:, bass.ds((TPG * j + t) * E, E)], mv[:, t, 0:1],
                                              rstd[:, t:t + 1], ALU.subtract, ALU.mult)
                    hh = h2[:, 2 * bb:2 * bb + 2, :]
                    ins.then_inc(s_turn, 1)
                    done[0] += 1
                    dve.wait_ge(s_turn, j * PER + done[0])
                    next_(v.tensor_tensor(hh, hh, row(2), ALU.mult))
                    v.tensor_tensor(hh, hh, row(1), ALU.add).then_inc(s_h2, 1)
                assert done[0] == PER, done[0]

            dve.wait_ge(s_lg, TURNS)
            v.memset(pr[:, :, NEXP:NEXP + 1], 8.0)
            v.memset(pr[:, :, NEXP + 1:NEXP + 2], 9.0)
            v.memset(cum[:, 0, :], 0.0)
            wide = [P, TILES, NEXP]
            lg3 = lg[:, :].rearrange("p (t e) -> p t e", t=TILES)
            link(v.tensor_reduce(mx[:, :], lg3, AX_X, ALU.max))
            v.tensor_tensor(ex[:, :, :], lg3, mx[:, :].unsqueeze(2).broadcast_to(wide), ALU.subtract).then_inc(s_ls, 1)
            dve.wait_ge(s_ex, 1)
            link(v.tensor_reduce(zs[:, :], ex[:, :, :], AX_X, ALU.add))
            link(v.reciprocal(mx[:, :], zs[:, :]))
            probs = pr[:, :, 0:NEXP]
            link(v.tensor_tensor(probs, ex[:, :, :], mx[:, :].unsqueeze(2).broadcast_to(wide), ALU.mult))
            for i in range(TILES):
                ins = v.max(p8[:, i, :], pr[:, i, 0:NEXP])
            link(ins)
            v.memset(p8[:, :, TOPK:TOPK + 1], 8.0)
            link(v.memset(p8[:, :, TOPK + 1:8], 9.0))
            for i in range(TILES):
                ins = v.match_replace(rep[:, i, :], p8[:, i, :], pr[:, i, :], -1.0)
            link(ins)
            v.tensor_scalar(mask[:, :, :], rep[:, :, 0:NEXP], -1.0, None, ALU.is_equal).then_inc(s_mask, 1)
            dve.wait_ge(s_mask, 1)
            for i in range(1, TILES):
                ins = v.tensor_tensor(cum[:, i, :], cum[:, i - 1, :], mask[:, i - 1, :], ALU.add)
                if i < TILES - 1:
                    link(ins)
            ins.then_inc(s_mask, 1)
            dve.wait_ge(s_n, 1)
            link(v.tensor_copy(n_col[:, :], PS[0:NEXP, 0, 0:1]))
            link(v.tensor_scalar(n_cmp[:, :], C("steps", NEXP), n_col[:, 0:1], None, ALU.is_lt))
            link(v.tensor_reduce(t_col[:, :], n_cmp[:, :], AX_X, ALU.add))
            v.tensor_copy(t_col16[:, :], t_col[:, :])
            v.tensor_scalar(t_wide[:, :], H("ones", NEXP), t_col[:, 0:1], float(P), ALU.mult, ALU.mult)\
                .then_inc(s_t, 1)
            dve.wait_ge(s_end, 1)
            link(v.tensor_copy(e_end[:, :], PS[0:NEXP, 3, 0:1]))
            v.tensor_scalar(e_cmp[:, :], H("tiles", NEXP), e_end[:, 0:1], None, ALU.is_ge).then_inc(s_ec, 1)
            dve.wait_ge(s_e, 1)
            link(v.tensor_scalar(e_row[:, :], PS[0:1, 4, 0:SLOT_TILES], float(NEXP - 1), None, ALU.min))
            v.tensor_copy(e_of[:, :], e_row[:, :]).then_inc(s_eo, 1)
            for half in range(2):
                tt = slice(8 * half, 8 * half + 8)
                ins = v.scalar_tensor_tensor(out=pos1[:, tt, :].rearrange("p t e -> p (t e)"), in0=PS[:, 1 + half, :],
                                             scalar=1.0, in1=mask[:, tt, :].rearrange("p t e -> p (t e)"),
                                             op0=ALU.add, op1=ALU.mult)
            link(ins)
            for i in range(TILES):
                ins = v.max(slot8[:, i, :], pos1[:, i, :])
            link(ins)
            v.tensor_scalar(slot_i[:, :], slot8[:, :, :].rearrange("p t k -> p (t k)"), -1.0, 0.0,
                            ALU.add, ALU.max).then_inc(s_slots, 1)
            dve.wait_ge(s_slots, 1)
            v.tensor_scalar(slot_g[:, :], slot_i[:, :], 7, None, ALU.arith_shift_right)
            link(v.tensor_scalar(slot_s[:, :], slot_i[:, :], P - 1, None, ALU.bitwise_and))
            v.tensor_copy(col_g[:, :], slot_g[:, :])
            link(v.tensor_copy(col_s[:, :], slot_s[:, :]))
            t0 = CST["token"][0]

            def one_hots(i, b, first=False):
                if not first:
                    dve.wait_ge(s_hotm, i - 1)
                for k in range(TOPK):
                    at = bass.ds(i * 8 + k, 1)
                    v.tensor_scalar(hot_s[:, b, k, :], H("slots"), col_s[:, at], None, ALU.is_equal)
                    ins = v.tensor_scalar(hot_g[:, b, k, :], H("tiles"), col_g[:, at], cs[:, bass.ds(i + t0, 1)],
                                          ALU.is_equal, ALU.mult)
                ins.then_inc(s_hot, 1)

            one_hots(0, 0, first=True)
            one_hots(1, 1, first=True)
            with dve.Fori(1, TILES // 2) as r:
                for b in range(2):
                    one_hots(2 * r + b, b)
            dve.wait_ge(s_hotm, TILES)
            v.tensor_copy(tok_of[:, :], PS[:, 3, 0:SLOT_TILES]).then_inc(s_tok, 1)

            def copy_x(tile, slot, first=False):
                b = slot % 2
                dve.wait_ge(s_xt, tile + 1)
                if not first:
                    dve.wait_ge(s_m1, tile - 1)
                v.tensor_copy(xgT[:, b, :, :].rearrange("p c n -> p (c n)"), PS[:, b, 0:E]).then_inc(s_xT, 1)

            def copy_y(tile, rnd, slot, first=False):
                b = slot % 2
                dve.wait_ge(s_m2, tile + 1)
                if not first:
                    dve.wait_ge(s_yd[slot], 16 * rnd)
                v.tensor_copy(yb[:, slot, :], PS[:, 6 + b, 0:E]).then_inc(s_yb, 1)

            copy_x(0, 0, first=True)
            copy_x(1, 1, first=True)
            for g in range(1, RING + 1):
                copy_x(g + 1, (g + 1) % RING)
                copy_y(g - 1, 0, g - 1, first=True)
            with dve.Fori(1, SLOT_TILES // RING - 1) as q:
                for r in range(1, 1 + RING):
                    copy_x(RING * q + r + 1, (r + 1) % RING)
                    copy_y(RING * q + r - 1, q, r - 1)
            g = SLOT_TILES - RING
            for r in range(1, 1 + RING):
                if g + r + 1 < SLOT_TILES:
                    copy_x(g + r + 1, (r + 1) % RING)
                copy_y(g + r - 1, g // RING, r - 1)

            link(v.tensor_tensor(comb[:, :, :], mask[:, :, :], probs, ALU.mult))
            link(v.tensor_reduce(zs[:, :], comb[:, :, :], AX_X, ALU.add))
            link(v.reciprocal(mx[:, :], zs[:, :]))
            link(v.tensor_tensor(comb[:, :, :], comb[:, :, :], mx[:, :].unsqueeze(2).broadcast_to(wide), ALU.mult))
            for k in range(TOPK):
                link(v.tensor_tensor(ex[:, :, :], pos1[:, :, :],
                                     slot8[:, :, k:k + 1].broadcast_to(wide), ALU.is_equal))
                link(v.tensor_tensor(ex[:, :, :], ex[:, :, :], comb[:, :, :], ALU.mult))
                link(v.tensor_reduce(wk[:, k, :], ex[:, :, :], AX_X, ALU.add))

            def combine(i, rnd, b, chain, first=False):
                dve.wait_ge(s_yg[b], 16 * TOPK * (rnd + 1))
                if not first:
                    dve.wait_ge(s_out[b], 16 * rnd)
                for k in range(TOPK):
                    src = sh_all[:, bass.ds(i * E, E)] if k == 0 else acc[:, b, :]
                    ins = v.scalar_tensor_tensor(out=acc[:, b, :], in0=yg[:, b, k, :],
                                                 scalar=wk[:, k, bass.ds(i, 1)], in1=src,
                                                 op0=ALU.mult, op1=ALU.add)
                    if k < TOPK - 1:
                        chain(ins)
                ins.then_inc(s_acc, 1)
                dve.wait_ge(s_acc, i + 1)
                chain(v.tensor_tensor(acc[:, b, :], acc[:, b, :], mod_row[:, bass.ds((4 * rnd + 3) * E, E)],
                                      ALU.mult))
                v.tensor_tensor(acc[:, b, :], acc[:, b, :], x_all[:, bass.ds(i * E, E)], ALU.add)\
                    .then_inc(s_fin, 1)

            combine(0, 0, 0, link, first=True)
            combine(1, 0, 1, link, first=True)
            before = steps[0]
            with dve.Fori(1, TILES // 2) as r:
                count = [0]

                def linked(ins):
                    count[0] += 1
                    ins.then_inc(s_chain, 1)
                    dve.wait_ge(s_chain, (r - 1) * 2 * TOPK + before + count[0])

                for b in range(2):
                    combine(2 * r + b, r, b, linked)
                assert count[0] == 2 * TOPK

        @block.gpsimd
        def _(pool):
            g = nc.gpsimd
            pool.wait_ge(s_set, 2)
            with pool.Fori(0, TURNS) as j:
                for u in range(4):
                    then(pool, s_cn, 4 * j + u + 1)
                    dst = q_odd[:, u, :] if u < 2 else kk[:, u - 2, :]
                    col = ln_mask[:, 2:4] if u < 2 else ln_col[:, 0:2]
                    g.tensor_scalar(dst, cn[:, u % 2, :], col[:, 0:1], col[:, 1:2], ALU.mult, ALU.add)\
                        .then_inc(s_fp, 1)
                for n in range(16):
                    then(pool, s_s2, 16 * j + n + 1)
                    m = s2[:, n % 3, :, 0:2 * P].rearrange("p r (a n) -> p r a n", a=2)
                    g.affine_select(out=m, in_=m, pattern=[[0, 2], [0, 2], [1, P]], compare_op=ALU.is_ge, fill=0.0,
                                    base=0, channel_multiplier=-1).then_inc(s_msk, 1)
                then(pool, s_h2T, j + 1)
                g.tensor_copy(h2T_all[:, :, bass.ds(j * GROUP, GROUP)], h2T[:, :, :]).then_inc(s_h2k, 1)

            with pool.Fori(0, TURNS) as j:
                for i, (c0, cn_) in enumerate(SH_CHUNKS):
                    n = 3 * j + i
                    then(pool, s_sg, n + 1)
                    then(pool, s_su, n + 1)
                    b = (3 * 0 + i) % 2
                    g.tensor_tensor(sact[0:cn_, i, :], sg[0:cn_, b, :], su[0:cn_, b, :], ALU.mult).then_inc(s_sa, 1)

            pool.wait_ge(s_tok, 1)
            pool.wait_ge(s_h2d, 16 * TURNS + 16)

            def gather(index, slot):
                g.indirect_dma_start(out=xg[:, slot, :], out_offset=None, in_=h2_dram,
                                     in_offset=bass.IndirectOffsetOnAxis(ap=index, axis=0)).then_inc(s_xg[slot], 16)

            for slot in range(RING):
                gather(tok_of[:, slot:slot + 1], slot)
            with pool.Fori(1, SLOT_TILES // RING) as r:
                for slot in range(RING):
                    tile = RING * r + slot
                    then(pool, s_xt, tile - RING + 1)
                    g.tensor_copy(ti[:, slot:slot + 1], tok_of[:, bass.ds(tile, 1)]).then_inc(s_ti, 1)
                    then(pool, s_ti, tile - RING + 1)
                    gather(ti[:, slot:slot + 1], slot)

            pool.wait_ge(s_ystored, 1)
            pool.wait_ge(s_slots, 1)
            idx = slot_i[:, :].bitcast(U32)

            def choices(i, b):
                g.tensor_copy(ki[:, b, :], idx[:, bass.ds(8 * i, TOPK)]).then_inc(s_ki, 1)
                then(pool, s_ki, i + 1)
                for k in range(TOPK):
                    g.indirect_dma_start(out=yg[:, b, k, :], out_offset=None, in_=y_dram,
                                         in_offset=bass.IndirectOffsetOnAxis(ap=ki[:, b, k:k + 1], axis=0))\
                        .then_inc(s_yg[b], 16)

            choices(0, 0)
            choices(1, 1)
            with pool.Fori(1, TILES // 2) as r:
                for b in range(2):
                    then(pool, s_acc, 2 * r + b - 1)
                    choices(2 * r + b, b)


def constants():
    import numpy as np
    cst = np.zeros((P, NCST), np.float32)

    def put(name, a):
        lo, _ = CST[name]
        a = np.asarray(a, np.float32)
        cst[0:a.shape[0], lo:lo + a.shape[1]] = a

    head = np.arange(P) // D
    same = (head[:, None] == head[None, :]).astype(np.float32)
    centre = np.eye(P, dtype=np.float32) - same / np.float32(D)
    swap = np.arange(P) ^ (D // 2)
    put("ident", np.eye(P))
    put("centre", centre)
    put("centre_swap", centre[swap])
    put("var", same / np.float32(D))
    inv = (np.float32(1.0) / np.float32(10000.0) ** (np.arange(0, D, 2, dtype=np.float32) / np.float32(D))).astype(np.float32)
    ang = np.arange(N, dtype=np.float32)[None, :] * inv[:, None]
    half = np.arange(P) % (D // 2)
    first = (np.arange(P) % D < D // 2)[:, None]
    put("cos", np.cos(ang)[half])
    put("sin", np.where(first, np.sin(ang)[half], -np.sin(ang)[half]))
    put("even", (head % 2 == 0)[:, None])
    put("odd", (head % 2 == 1)[:, None])
    put("eps", np.full((P, 1), EPS))
    put("token", np.arange(P)[:, None] + P * np.arange(TILES)[None, :])
    put("steps", np.tile(P * np.arange(TOK // P)[None, :], (P, 1)))
    put("sel", np.repeat(np.eye(B), P, axis=1))
    hst = np.zeros((P, NHST), np.float16)

    def put16(name, a):
        lo, _ = HST[name]
        a = np.asarray(a, np.float16)
        hst[0:a.shape[0], lo:lo + a.shape[1]] = a

    put16("before", np.triu(np.ones((P, P)), 1))
    put16("ones", np.ones((P, P)))
    put16("exp_before", np.triu(np.ones((NEXP, NEXP)), 1))
    put16("exp_upto", np.triu(np.ones((NEXP, NEXP)), 0))
    put16("tiles", np.tile(np.arange(SLOT_TILES)[None, :], (P, 1)))
    put16("slots", np.tile(np.arange(P)[None, :], (P, 1)))
    return cst, hst


def kernel(L0_attn_x, L0_attn_w_qkv, L0_attn_w_out, L0_attn_ln_scale, L0_attn_ln_bias, L0_ffn_gate_w,
           L0_ffn_experts_w1, L0_ffn_experts_w2, L0_ffn_shared_gate_up, L0_ffn_shared_down, L0_c, L0_wmod):
    import numpy as np
    import concourse.bacc as bacc
    from concourse.bass_utils import run_bass_kernel_spmd

    def lay(a):
        return np.ascontiguousarray(a)

    cst, hst = constants()
    ln = np.stack([np.tile(np.asarray(L0_attn_ln_scale), P // D), np.tile(np.asarray(L0_attn_ln_bias), P // D)], axis=1)
    arrays = {
        "x": lay(L0_attn_x).reshape(TOK, E),
        "w_qkv": lay(L0_attn_w_qkv),
        "w_out": lay(L0_attn_w_out),
        "ln_cols": lay(ln),
        "gate_t": lay(np.asarray(L0_ffn_gate_w).T),
        "w1_t": lay(np.asarray(L0_ffn_experts_w1).transpose(0, 2, 1)),
        "w2_t": lay(np.asarray(L0_ffn_experts_w2).transpose(0, 2, 1)),
        "gu_t": lay(np.asarray(L0_ffn_shared_gate_up).T),
        "down_t": lay(np.asarray(L0_ffn_shared_down).T),
        "c_t": lay(np.asarray(L0_c).T),
        "wmod": lay(L0_wmod),
        "cst": cst,
        "hst": hst,
    }
    nc = bacc.Bacc("TRN2", target_bir_lowering=False, num_devices=1)
    args = [nc.dram_tensor(name, a.shape, mybir.dt.from_np(a.dtype), kind="ExternalInput").ap()
            for name, a in arrays.items()]
    out = nc.dram_tensor("out", (TOK, E), F32, kind="ExternalOutput").ap()
    build(nc, *args, out)
    r = run_bass_kernel_spmd(nc, [arrays], core_ids=[0])
    return r.results[0]["out"].reshape(B, N, E)
```

```python
from contextlib import ExitStack

import concourse.bass as bass
from concourse import mybir

ALU = mybir.AluOpType
ACT = mybir.ActivationFunctionType
F32 = mybir.dt.float32
F32R = mybir.dt.float32r
F16 = mybir.dt.float16
I32 = mybir.dt.int32
U32 = mybir.dt.uint32
AX_X = mybir.AxisListType.X

P = 128
B, N, E = 8, 256, 256
TOK = B * N
TILES = TOK // P
EC = E // P
HEADS, D = 16, 16
QK = 2 * E // P
GROUP = 512
TURNS = TOK // GROUP
S_RING, A_RING = 4, 3
UNITS = 16
TPG = GROUP // P
BPG = GROUP // N
NEXP, INNER, TOPK = 64, 176, 6
IC = 2
IP = INNER // IC
ROUTED_TILES = (TOK * TOPK + NEXP * (P - 1)) // P
RING = 4
SLOT_TILES = -(-ROUTED_TILES // RING) * RING
SHARED = 352
SH_CHUNKS = [(0, 128), (128, 128), (256, 96)]
EPS = 1e-5

CST = {}
_at = 0
for _name, _n in (("ident", P), ("centre", P), ("centre_swap", P), ("var", P), ("cos", N), ("sin", N),
                  ("even", 1), ("odd", 1), ("eps", 1), ("token", TILES), ("steps", TOK // P)):
    CST[_name] = (_at, _at + _n)
    _at += _n
NCST = _at
HST = {}
_at = 0
for _name, _n in (("before", P), ("ones", P), ("exp_before", NEXP), ("exp_upto", NEXP),
                  ("tiles", SLOT_TILES), ("slots", P)):
    HST[_name] = (_at, _at + _n)
    _at += _n
NHST = _at


def build(nc, x, w_qkv, w_out, ln_cols, gate_t, w1_t, w2_t, gu_t, down_t, c_t, wmod, cst, hst, out):
    with ExitStack() as ctx:
        def sb(name, shape, dt=F32):
            return ctx.enter_context(nc.sbuf_tensor(name, shape, dt))

        def sem(name):
            return ctx.enter_context(nc.semaphore(name))

        rows_dram = nc.dram_tensor("modulation_rows", [B, 4 * E], F32, kind="Internal").ap()
        h2_dram = nc.dram_tensor("h2_rows", [TOK, E], F32, kind="Internal").ap()
        y_dram = nc.dram_tensor("expert_rows", [SLOT_TILES * P, E], F32, kind="Internal").ap()

        PS = ctx.enter_context(nc.psum_tensor("PS", [P, 8, 512], F32))

        cs = sb("cs", [P, NCST])
        hs = sb("hs", [P, NHST], F16)
        ln_col = sb("ln_col", [P, 2])
        wqkv_sb = sb("wqkv_sb", [P, EC, 3 * E])
        wout_sb = sb("wout_sb", [P, EC, E])
        gate_sb = sb("gate_sb", [P, EC, NEXP])
        mod_col = sb("mod_col", [P, 2, EC, B])
        x_all = sb("x_all", [P, TILES * E])
        h2T_all = sb("h2T_all", [P, EC, TOK])
        lg = sb("lg", [P, TILES * NEXP])
        mx = sb("mx", [P, TILES])
        zs = sb("zs", [P, TILES])
        p8 = sb("p8", [P, TILES, 8])
        slot_i = sb("slot_i", [P, TILES * 8], I32)
        slot_g = sb("slot_g", [P, TILES * 8], I32)
        slot_s = sb("slot_s", [P, TILES * 8], I32)
        col_g = sb("col_g", [P, TILES * 8])
        col_s = sb("col_s", [P, TILES * 8])
        tok_of = sb("tok_of", [P, SLOT_TILES], U32)
        n_col = sb("n_col", [NEXP, 1])
        n_cmp = sb("n_cmp", [NEXP, TILES])
        t_col = sb("t_col", [NEXP, 1])
        t_col16 = sb("t_col16", [NEXP, 1], F16)
        t_wide = sb("t_wide", [NEXP, P], F16)
        e_end = sb("e_end", [NEXP, 1])
        e_cmp = sb("e_cmp", [NEXP, SLOT_TILES], F16)
        e_row = sb("e_row", [1, SLOT_TILES])
        e_of = sb("e_of", [1, SLOT_TILES], I32)
        wk = sb("wk", [P, TOPK, TILES])
        early_stack = ExitStack()

        def early(name, shape, dt=F32):
            return early_stack.enter_context(nc.sbuf_tensor(name, shape, dt))

        modulation_stack = ExitStack()

        def modulation(name, shape, dt=F32):
            return modulation_stack.enter_context(nc.sbuf_tensor(name, shape, dt))

        rows = modulation("rows", [B, 4, E])
        gate_size = modulation("gate_size", [B, 2, E])
        gate_sign = modulation("gate_sign", [B, 2, E])
        wmod_sb = modulation("wmod_sb", [P, EC, 6 * E])
        modulation_stack.close()
        h2 = early("h2", [P, TPG, E])
        gated = early("gated", [P, BPG, 2 * E])
        s2 = early("s2", [P, S_RING, 2, 384])
        cT = early("cT", [P, EC, B])
        silu_c = early("silu_c", [P, EC, B])
        mod_row = early("mod_row", [P, BPG, 4 * E])
        mod_now = early("mod_now", [P, 2, EC, BPG])
        st = early("st", [P, TPG, 6])
        mv = early("mv", [P, TPG, 2])
        sd = early("sd", [P, TPG])
        rstd = early("rstd", [P, TPG])
        xn = early("xn", [P, TPG, E])
        hT = early("hT", [P, EC, GROUP])
        rc = early("rc", [P, 2, GROUP])
        rs = early("rs", [P, 2, GROUP])
        sq = early("sq", [P, 2, GROUP])
        qsd = early("qsd", [P, 2, GROUP])
        qrs = early("qrs", [P, GROUP])
        scaled = early("scaled", [P, GROUP])
        q_sum = early("q_sum", [P, GROUP])
        q_hi = early("q_hi", [P, 2, GROUP], F32R)
        q_lo = early("q_lo", [P, 2, GROUP], F32R)
        k_hi = early("k_hi", [P, 2, GROUP], F32R)
        k_lo = early("k_lo", [P, 2, GROUP], F32R)
        k_stack = early("k_stack", [P, 4, 2, GROUP], F32R)
        q_stack = early("q_stack", [P, 4, 2, GROUP], F32R)
        kk = early("kk", [P, 2, GROUP])
        v_sb = early("v_sb", [P, TPG, HEADS, D])
        va = early("va", [P, TPG, HEADS, 2, D + 1], F32R)
        a_hi = early("a_hi", [P, A_RING, 2, 384], F32R)
        a_lo = early("a_lo", [P, A_RING, 2, 384], F32R)
        rows_av = early("rows_av", [2 * (D + 1), 2, 2, N])
        av = early("av", [P, 2 * 4, D + 1])
        rden = early("rden", [P, 2 * 4])
        o_sb = early("o_sb", [P, TPG, E])
        oT = early("oT", [P, 2, EC, P])
        h2T = s2[:, 0:2, :, :].rearrange("p s r n -> p (s r n)")[:, 0:EC * GROUP].rearrange("p (c n) -> p c n", c=EC)
        early_stack.close()
        def late(name, shape, dt=F32):
            return ctx.enter_context(nc.sbuf_tensor(name, shape, dt))

        yg = late("yg", [P, 2, TOPK, E])
        ex = late("ex", [P, TILES, NEXP])
        pr = late("pr", [P, TILES, NEXP + 2])
        rep = late("rep", [P, TILES, NEXP + 2])
        comb = late("comb", [P, TILES, NEXP])
        pos1 = late("pos1", [P, TILES, NEXP])
        mask = late("mask", [P, TILES, NEXP], F16)
        cum = late("cum", [P, TILES, NEXP], F16)
        slot8 = late("slot8", [P, TILES, 8])
        hot_s = late("hot_s", [P, 2, TOPK, P], F16)
        hot_g = late("hot_g", [P, 2, TOPK, SLOT_TILES], F16)
        gu_sb = late("gu_sb", [P, EC, 2 * SHARED])
        down_sb = late("down_sb", [P, len(SH_CHUNKS), E])
        sg = late("sg", [P, 2, GROUP])
        sact = late("sact", [P, len(SH_CHUNKS), GROUP])
        ti = late("ti", [P, RING], U32)
        xg = late("xg", [P, RING, E])
        xgT = late("xgT", [P, 2, EC, P])
        w1b = late("w1b", [P, RING, EC, INNER])
        w2b = late("w2b", [IP, RING, IC, E])
        hx = late("hx", [IP, 2, IC, P])
        yb = late("yb", [P, RING, E])
        ki = late("ki", [P, 2, TOPK], U32)
        acc = late("acc", [P, 2, E])
        gate_row = late("gate_row", [P, B, E])

        def C(name, rows_=P):
            a, b = CST[name]
            return cs[0:rows_, a:b]

        def H(name, rows_=P):
            a, b = HST[name]
            return hs[0:rows_, a:b]

        ident = C("ident")

        s_wm = sem("modulation_weights_loaded")
        s_w = sem("weights_loaded")
        s_ws = sem("shared_weights_loaded")
        s_cst = sem("constants_loaded")
        s_x = sem("x_loaded")
        s_set = sem("buffers_set")
        s_silu = sem("silu_c_ready")
        s_modp = sem("mod_product")
        s_modc = sem("mod_columns")
        s_rowp = sem("rows_product")
        s_rowr = sem("rows_product_read")
        s_rows = sem("rows_ready")
        s_rowd = sem("rows_stored_in_dram")
        s_bc = sem("rows_broadcast")
        s_gr = sem("gate_rows_broadcast")
        s_xr = sem("rest_of_x_loaded")
        s_pchain = sem("pool_steps")
        s_chain = sem("vector_steps")
        s_achain = sem("scalar_steps")
        s_turn = sem("vector_turn_steps")
        s_mv = sem("moments")
        s_sd = sem("deviation")
        s_xn = sem("normed")
        s_xnT = sem("normed_turned")
        s_now = sem("mod_now_ready")
        s_hT = sem("h_ready")
        s_proj = sem("qk_projected")
        s_rope = sem("rope_products")
        s_cent = sem("centred")
        s_sq = sem("squared")
        s_var = sem("variance")
        s_qsd = sem("head_deviation")
        s_fin = sem("centred_read")
        s_scale = sem("q_scaled")
        s_qh = sem("q_high_ready")
        s_ql = sem("q_low_ready")
        s_kk = sem("k_ready")
        s_kh = sem("k_high_ready")
        s_kl = sem("k_low_ready")
        s_qst = sem("q_stacked")
        s_kst = [sem(f"k_stacked{i}") for i in range(4)]
        s_vh = sem("v_high_ready")
        s_hi = sem("weights_high")
        s_lo = sem("weights_low")
        s_av4 = sem("attended_read")
        s_v = sem("v_projected")
        s_va = sem("v_copied")
        s_sc = sem("scores")
        s_s2 = sem("scores_squared")
        s_msk = sem("scores_masked")
        s_s4 = sem("scores_fourth")
        s_av = sem("attended")
        s_avc = sem("attended_copied")
        s_back = sem("attended_turned_back")
        s_on = sem("attention_normed")
        s_ot = sem("attention_turned")
        s_oT = sem("attention_turned_copied")
        s_ao = sem("attention_projected")
        s_mv2 = sem("moments2")
        s_sd2 = sem("deviation2")
        s_h2 = sem("h2_ready")
        s_h2d = sem("h2_stored")
        s_h2t = sem("h2_turned")
        s_h2T = sem("h2_turned_copied")
        s_h2k = sem("h2_turned_kept")
        s_lgp = sem("logits_product")
        s_lg = sem("logits_ready")
        s_ls = sem("logits_less_max")
        s_ex = sem("exp_ready")
        s_mask = sem("masks_ready")
        s_n = sem("expert_counts")
        s_t = sem("expert_tiles")
        s_pos = sem("positions")
        s_e = sem("expert_of_tile_sum")
        s_ec = sem("expert_compared")
        s_end = sem("expert_ends")
        s_eo = sem("expert_of_tile")
        s_hot = sem("one_hots")
        s_hotm = sem("one_hots_used")
        s_tok = sem("token_of_slot")
        s_gp = sem("shared_gate_and_up")
        s_sg = sem("shared_gate_copied")
        s_sa = sem("shared_act")
        s_sp = sem("shared_down_product")
        s_ti = sem("tile_indices")
        s_xg = [sem(f"rows_gathered{i}") for i in range(RING)]
        s_w1 = [sem(f"w1_loaded{i}") for i in range(RING)]
        s_w2 = [sem(f"w2_loaded{i}") for i in range(RING)]
        s_yd = [sem(f"rows_stored{i}") for i in range(RING)]
        s_xt = sem("rows_turned")
        s_xT = sem("rows_turned_copied")
        s_m1 = sem("inner_product")
        s_hx = sem("inner_silu")
        s_m2 = sem("outer_product")
        s_yb = sem("outer_copied")
        s_ystored = sem("all_rows_stored")
        s_slots = sem("slots_ready")
        s_ki = sem("choice_indices")
        s_yg = [sem(f"choices_gathered{i}") for i in range(2)]
        s_acc = sem("choices_summed")
        s_final = sem("rows_final")
        s_out = [sem(f"out_stored{i}") for i in range(2)]
        s_wait = sem("waited")

        def then(eng, semaphore, value):
            eng.wait_ge(semaphore, value)
            eng.sem_inc(s_wait, 1)

        def project_out(pe, t, j):
            pe.wait_ge(s_oT, 4 * j + t + 1)
            for c in range(EC):
                last = nc.tensor.matmul(PS[:, 2 + t // 2, (t % 2) * E:(t % 2 + 1) * E], oT[:, t % 2, c, :],
                                        wout_sb[:, c, :], start=(c == 0), stop=(c == EC - 1))
            last.then_inc(s_ao, 1)

        def heads_norm(dve, j, idx, next_):
            v = nc.vector
            bb, i, _ = unit(2 * idx)
            dve.wait_ge(s_back, UNITS * j + 2 * idx + 2)
            if idx >= 1:
                dve.wait_ge(s_on, 8 * j + idx)
            o = PS[:, 6 + idx % 2, 0:2 * 4 * 2 * (D + 1)].rearrange("p (m a d) -> p m d a", a=2, d=D + 1)
            v.tensor_reduce(av[:, :, :], o, AX_X, ALU.add).then_inc(s_av4, 1)
            dve.wait_ge(s_av4, 8 * j + idx + 1)
            next_(v.reciprocal(rden[:, :], av[:, :, D]))
            dst = o_sb[:, 2 * bb:2 * bb + 2, :].rearrange("p t (g i d) -> p t g i d", i=4, d=D)
            v.tensor_tensor(dst[:, :, :, i, :], av[:, :, 0:D].rearrange("p (t g) d -> p t g d", t=2),
                            rden[:, :].rearrange("p (t g) -> p t g", t=2).unsqueeze(3).broadcast_to([P, 2, 4, D]),
                            ALU.mult).then_inc(s_on, 1)

        def unit(n):
            return n // 8, n // 2 % 4, n % 2

        N_W = 5
        block = ctx.enter_context(nc.Block())

        @block.sync
        def _(sp):
            sp.dma_start(cT[:, :, :], c_t.rearrange("(c p) b -> p c b", p=P)).then_inc(s_wm, 16)
            sp.dma_start(wmod_sb[:, :, :], wmod.rearrange("(c p) n -> p c n", p=P)).then_inc(s_wm, 16)
            x_tiles = x_all[:, :].rearrange("p (t f) -> p t f", f=E)
            sp.dma_start(x_tiles[:, 0:TPG, :], x[0:GROUP, :].rearrange("(t p) f -> p t f", p=P)).then_inc(s_x, 16)
            sp.dma_start(cs[:, :], cst).then_inc(s_cst, 16)
            sp.dma_start(wqkv_sb[:, :, :], w_qkv.rearrange("(c p) n -> p c n", p=P)).then_inc(s_w, 16)
            sp.dma_start(ln_col[:, :], ln_cols).then_inc(s_w, 16)
            sp.dma_start(wout_sb[:, :, :], w_out.rearrange("(c p) n -> p c n", p=P)).then_inc(s_w, 16)
            sp.dma_start(gate_sb[:, :, :], gate_t.rearrange("(c p) n -> p c n", p=P)).then_inc(s_w, 16)
            sp.dma_start(hs[:, :], hst).then_inc(s_w, 16)
            sp.dma_start(x_tiles[:, TPG:TILES, :], x[GROUP:TOK, :].rearrange("(t p) f -> p t f", p=P)).then_inc(s_xr, 16)
            sp.wait_ge(s_rows, 1)
            sp.dma_start(rows_dram.rearrange("b (k f) -> b k f", k=4), rows[:, :, :]).then_inc(s_rowd, 16)
            sp.wait_ge(s_rowd, 16)
            with sp.Fori(0, TURNS) as j:
                sp.dma_start(mod_row[:, :, :].rearrange("p b f -> p (b f)"),
                             rows_dram[bass.ds(BPG * j, BPG), :].rearrange("b f -> (b f)").unsqueeze(0)
                             .broadcast_to([P, BPG * 4 * E])).then_inc(s_bc, 16)

                def stack(dst, parts, i, semaphore):
                    for head in (i, i + 4):
                        for n, part in enumerate(parts):
                            row = 64 * (head // 4) + D * n
                            sp.dma_start(dst[row:row + D, i, :, :].bitcast(F32),
                                         part[head * D:(head + 1) * D, :, :].bitcast(F32))\
                                .then_inc(semaphore, 16)

                then(sp, s_qh, 2 * j + 2)
                then(sp, s_ql, 2 * j + 2)
                for i in range(4):
                    stack(q_stack, (q_hi, q_hi, q_lo), i, s_qst)
                then(sp, s_kh, 2 * j + 2)
                then(sp, s_kl, 2 * j + 2)
                for i in range(4):
                    stack(k_stack, (k_hi, k_lo, k_hi), i, s_kst[i])
                then(sp, s_h2, 2 * j + 2)
                sp.dma_start(h2_dram[bass.ds(j * GROUP, GROUP), :].rearrange("(t p) f -> p t f", p=P),
                             h2[:, :, :]).then_inc(s_h2d, 16)
            sp.wait_ge(s_eo, 1)
            sp.wait_ge(s_h2d, 16 * TURNS + 16)
            sp.wait_ge(s_h2k, TURNS)

            sp.dma_start(gu_sb[:, :, :], gu_t.rearrange("(c p) n -> p c n", p=P)).then_inc(s_ws, 16)
            sp.dma_start(down_sb[:, 0:2, :], down_t[0:2 * P].rearrange("(c p) n -> p c n", p=P)).then_inc(s_ws, 16)
            sp.dma_start(down_sb[0:SHARED - 2 * P, 2, :], down_t[2 * P:SHARED]).then_inc(s_ws, 16)

            sp.dma_start(gate_row[:, :, :], rows_dram[:, 3 * E:4 * E].unsqueeze(0).broadcast_to([P, B, E]))\
                .then_inc(s_gr, 16)

            def load(tile, rnd, slot):
                e = sp.value_load(e_of[0:1, bass.ds(tile, 1)] if rnd is not None else e_of[0:1, tile:tile + 1],
                                  min_val=0, max_val=NEXP - 1)
                if rnd is not None:
                    then(sp, s_m1, tile - RING + 1)
                sp.dma_start(w1b[:, slot, :, :], w1_t[bass.ds(e, 1)].rearrange("a (c p) i -> p (a c) i", p=P))\
                    .then_inc(s_w1[slot], 16)
                if rnd is not None:
                    then(sp, s_m2, tile - RING + 1)
                sp.dma_start(w2b[:, slot, :, :], w2_t[bass.ds(e, 1)].rearrange("a (c p) h -> p (a c) h", p=IP))\
                    .then_inc(s_w2[slot], 16)

            for slot in range(RING):
                load(slot, None, slot)
            with sp.Fori(1, SLOT_TILES // RING) as r:
                for slot in range(RING):
                    load(r * RING + slot, r, slot)
            with sp.Fori(0, TILES // 2) as r:
                for b in range(2):
                    then(sp, s_final, 2 * r + b + 1)
                    sp.dma_start(out[bass.ds((2 * r + b) * P, P), :], acc[:, b, :]).then_inc(s_out[b], 16)
            for b in range(2):
                sp.wait_ge(s_out[b], 16 * (TILES // 2))

        @block.tensor
        def _(pe):
            mm = nc.tensor.matmul

            pe.wait_ge(s_silu, 1)
            pe.wait_ge(s_wm, 16 * 2)
            for kind in range(2):
                for c in range(EC):
                    at = (kind * EC + c) * B
                    for k in range(EC):
                        last = mm(PS[:, 0, at:at + B], wmod_sb[:, k, kind * E + c * P:kind * E + (c + 1) * P],
                                  silu_c[:, k, :], start=(k == 0), stop=(k == EC - 1))
            last.then_inc(s_modp, 1)
            for half in range(2):
                for k in range(EC):
                    last = mm(PS[0:B, 6 + half, :], silu_c[:, k, :],
                              wmod_sb[:, k, (2 + 2 * half) * E:(4 + 2 * half) * E], start=(k == 0), stop=(k == EC - 1))
            last.then_inc(s_rowp, 1)
            pe.wait_ge(s_modc, 1)
            pe.wait_ge(s_cst, 16)
            pe.wait_ge(s_w, 16 * N_W)

            with pe.Fori(0, TURNS) as j:
                for t in range(TPG):
                    pe.wait_ge(s_xn, TPG * j + t + 1)
                    for c in range(EC):
                        last = nc.tensor.transpose(PS[:, t // 2, c * N + t % 2 * P:c * N + (t % 2 + 1) * P], xn[:, t, c * P:(c + 1) * P], ident)
                    last.then_inc(s_xnT, 1)

                def proj(u):
                    if u >= 2:
                        pe.wait_ge(s_rope, 4 * j + u - 1)
                    for k in range(EC):
                        last = mm(PS[:, 2 + u % 2, :], wqkv_sb[:, k, u * P:(u + 1) * P], hT[:, k, :],
                                  start=(k == 0), stop=(k == EC - 1))
                    last.then_inc(s_proj, 1)

                def values(t):
                    for k in range(EC):
                        last = mm(PS[:, t // 2, (t % 2) * E:(t % 2 + 1) * E], hT[:, k, t * P:(t + 1) * P],
                                  wqkv_sb[:, k, 2 * E:3 * E], start=(k == 0), stop=(k == EC - 1))
                    last.then_inc(s_v, 1)

                def centre(u):
                    pe.wait_ge(s_rope, 4 * j + u + 1)
                    if u >= 2:
                        pe.wait_ge(s_fin, 4 * j + u - 1)
                    mm(PS[:, 4 + u % 2, :], C("centre"), rc[:, u % 2, :], start=True, stop=False)
                    mm(PS[:, 4 + u % 2, :], C("centre_swap"), rs[:, u % 2, :], start=False, stop=True)\
                        .then_inc(s_cent, 1)

                def variance(u):
                    if u == 0:
                        pe.wait_ge(s_rowr, 1)
                    pe.wait_ge(s_sq, 4 * j + u + 1)
                    if u >= 2:
                        pe.wait_ge(s_qsd, 4 * j + u - 1)
                    mm(PS[:, 6 + u % 2, :], C("var"), sq[:, u % 2, :], start=True, stop=True).then_inc(s_var, 1)

                pe.wait_ge(s_hT, 4 * j + 4)
                proj(0)
                proj(1)
                values(0)
                values(1)
                centre(0)
                proj(2)
                values(2)
                variance(0)
                centre(1)
                proj(3)
                values(3)
                variance(1)
                for u in (2, 3):
                    centre(u)
                    variance(u)

                def scores(n):
                    bb, i, f = unit(n)
                    if bb == 0 and f == 0:
                        pe.wait_ge(s_kst[i], 16 * 6 * (j + 1))
                    if n >= 2:
                        pe.wait_ge(s_s2, UNITS * j + n - 1)
                    at = bb * N
                    for r in range(2):
                        rows_ = slice(64 * r, 64 * r + 3 * D)
                        bank = PS[:, 2 * (n % 2) + r, :]
                        for key in range(2):
                            first = at + key * P
                            o = bank[:, P:2 * P] if key else bank.rearrange("p (a n) -> p a n", a=2)[:, :, 0:P]
                            last = mm(o, k_stack[rows_, i, f, first:first + P], q_stack[rows_, i, f, first:at + N],
                                      start=True, stop=True)
                    last.then_inc(s_sc, 1)

                def attend(n):
                    bb, i, f = unit(n)
                    pe.wait_ge(s_lo, UNITS * j + n + 1)
                    if n >= 2:
                        pe.wait_ge(s_avc, UNITS * j + n - 1)
                    for r in range(2):
                        v0, v1 = (va[:, 2 * bb + m, 8 * f + i + 4 * r, :, :].rearrange("p a d -> p (a d)")
                                  for m in range(2))
                        o = PS[0:2 * (D + 1), 4 + n % 2, r * N:(r + 1) * N]
                        hi, lo = (a[:, n % A_RING, r, :] for a in (a_hi, a_lo))

                        def all_queries(a):
                            return bass.AP(a.tensor, a.offset, [list(a.ap[0]), [2 * P, 2], [1, P]])

                        mm(o, v0, all_queries(hi), start=True, stop=False)
                        mm(o[:, P:2 * P], v1, hi[:, P:2 * P], start=False, stop=False)
                        mm(o[:, P:2 * P], v1, lo[:, P:2 * P], start=False, stop=False)
                        last = mm(o, v0, all_queries(lo), start=False, stop=True)
                    last.then_inc(s_av, 1)

                def turn_back(n):
                    f = n % 2
                    then(pe, s_avc, UNITS * j + n + 1)
                    if n % 2 == 0 and n >= 4:
                        then(pe, s_av4, 8 * j + n // 2 - 1)
                    o = PS[:, 6 + n // 2 % 2, 0:2 * 4 * 2 * (D + 1)].rearrange("p (t h d) -> p t h d", t=2, h=4)
                    for r in range(2):
                        for t in range(2):
                            last = nc.tensor.transpose(o[:, t, 2 * f + r, :], rows_av[:, n % 2, r, t * P:(t + 1) * P],
                                                       C("ident", 2 * (D + 1))[:, 0:2 * (D + 1)])
                    last.then_inc(s_back, 1)

                pe.wait_ge(s_va, 2 * j + 2)
                pe.wait_ge(s_qst, 16 * 24 * (j + 1))
                for n in range(UNITS + 4):
                    if n < UNITS:
                        scores(n)
                    if 3 <= n < UNITS + 3:
                        attend(n - 3)
                    if n >= 4:
                        turn_back(n - 4)

                for t in range(TPG):
                    if t % 2 == 0:
                        pe.wait_ge(s_on, 8 * j + 2 * t + 4)
                    if t >= 2:
                        pe.wait_ge(s_oT, 4 * j + t - 1)
                    for c in range(EC):
                        last = nc.tensor.transpose(PS[:, t % 2, c * P:(c + 1) * P], o_sb[:, t, c * P:(c + 1) * P], ident)
                    last.then_inc(s_ot, 1)
                    if t >= 1:
                        project_out(pe, t - 1, j)
                project_out(pe, TPG - 1, j)

                for t in range(TPG):
                    if t % 2 == 0:
                        pe.wait_ge(s_h2, 2 * j + t // 2 + 1)
                    for c in range(EC):
                        last = nc.tensor.transpose(PS[:, 4 + c, t * P:(t + 1) * P], h2[:, t, c * P:(c + 1) * P], ident)
                last.then_inc(s_h2t, 1)
                pe.wait_ge(s_h2T, j + 1)
                for t in range(TPG):
                    for k in range(EC):
                        last = mm(PS[:, 6, t * NEXP:(t + 1) * NEXP], h2T[:, k, t * P:(t + 1) * P], gate_sb[:, k, :],
                                  start=(k == 0), stop=(k == EC - 1))
                last.then_inc(s_lgp, 1)

            pe.wait_ge(s_mask, 1)
            for i in range(TILES):
                last = mm(PS[0:NEXP, 0, 0:1], mask[:, i, :], H("ones")[:, 0:1], start=(i == 0), stop=(i == TILES - 1))
            last.then_inc(s_n, 1)
            pe.wait_ge(s_mask, 2)
            pe.wait_ge(s_t, 1)
            for half in range(2):
                tt = slice(8 * half, 8 * half + 8)
                o = PS[:, 1 + half, :]
                mm(o, H("before"), mask[:, tt, :].rearrange("p t e -> p (t e)"), start=True, stop=False)
                mm(o, H("ones"), cum[:, tt, :].rearrange("p t e -> p (t e)"), start=False, stop=False)
                last = mm(o, t_wide[:, :], H("exp_before", NEXP).unsqueeze(1).broadcast_to([NEXP, 8, NEXP]),
                          start=False, stop=True)
            last.then_inc(s_pos, 1)
            mm(PS[0:NEXP, 3, 0:1], H("exp_upto", NEXP), t_col16[:, :], start=True, stop=True).then_inc(s_end, 1)
            pe.wait_ge(s_ec, 1)
            mm(PS[0:1, 4, 0:SLOT_TILES], H("ones", NEXP)[:, 0:1], e_cmp[:, :], start=True, stop=True).then_inc(s_e, 1)

            def collect(n, b, first=False, final=False):
                pe.wait_ge(s_hot, n + 1)
                for k in range(TOPK):
                    last = mm(PS[:, 3, 0:SLOT_TILES], hot_s[:, b, k, :], hot_g[:, b, k, :],
                              start=(first and k == 0), stop=(final and k == TOPK - 1))
                last.then_inc(s_hotm, 1)

            collect(0, 0, first=True)
            collect(1, 1)
            with pe.Fori(1, TILES // 2 - 1) as r:
                for b in range(2):
                    collect(2 * r + b, b)
            collect(TILES - 2, 0)
            collect(TILES - 1, 1, final=True)

            def turn(tile, rnd, slot):
                pe.wait_ge(s_xg[slot], 16 * (rnd + 1))
                b = slot % 2
                for c in range(EC):
                    last = nc.tensor.transpose(PS[:, b, c * P:(c + 1) * P], xg[:, slot, c * P:(c + 1) * P], ident)
                last.then_inc(s_xt, 1)

            def inner(tile, rnd, slot):
                b = slot % 2
                pe.wait_ge(s_xT, tile + 1)
                pe.wait_ge(s_w1[slot], 16 * (rnd + 1))
                for i in range(IC):
                    for c in range(EC):
                        last = mm(PS[0:IP, 4 + b, i * P:(i + 1) * P], w1b[:, slot, c, i * IP:(i + 1) * IP],
                                  xgT[:, b, c, :], start=(c == 0), stop=(c == EC - 1))
                last.then_inc(s_m1, 1)

            def outer(tile, rnd, slot, first=False):
                b = slot % 2
                pe.wait_ge(s_hx, tile + 1)
                pe.wait_ge(s_w2[slot], 16 * (rnd + 1))
                if not first:
                    pe.wait_ge(s_yb, tile - 1)
                for i in range(IC):
                    last = mm(PS[:, 6 + b, 0:E], hx[:, b, i, :], w2b[:, slot, i, :],
                              start=(i == 0), stop=(i == IC - 1))
                last.then_inc(s_m2, 1)

            turn(0, 0, 0)
            turn(1, 0, 1)
            inner(0, 0, 0)
            LOOPS = SLOT_TILES // RING - 1
            def step(g, q, r, **kw):
                turn(g + 1, q + (r + 1) // RING, (r + 1) % RING)
                inner(g, q + r // RING, r % RING)
                outer(g - 1, q + (r - 1) // RING, (r - 1) % RING, **kw)
            for g in (1, 2):
                step(g, 0, g, first=True)
            with pe.Fori(0, LOOPS) as q:
                for r in range(3, 3 + RING):
                    step(RING * q + r, q, r)
            g = SLOT_TILES - 1
            inner(g, g // RING, g % RING)
            outer(g - 1, (g - 1) // RING, (g - 1) % RING)
            outer(g, g // RING, g % RING)

            pe.wait_ge(s_ws, 16 * 3)
            pe.wait_ge(s_h2k, TURNS)
            pe.wait_ge(s_yb, SLOT_TILES)

            def shared(j, first=False):
                for i, (c0, cn_) in enumerate(SH_CHUNKS):
                    n = 3 * j + i
                    if i >= 2 or not first:
                        pe.wait_ge(s_sa, n - 1)
                    for which in range(2):
                        w0 = which * SHARED + c0
                        for k in range(EC):
                            last = mm(PS[0:cn_, 2 * (i % 2) + which, :], gu_sb[:, k, w0:w0 + cn_],
                                      h2T_all[:, k, bass.ds(j * GROUP, GROUP)], start=(k == 0), stop=(k == EC - 1))
                    last.then_inc(s_gp, 1)
                pe.wait_ge(s_sa, 3 * j + 3)
                for t in range(TPG):
                    if not first:
                        pe.wait_ge(s_acc, 4 * j + t - 3)
                    for i, (c0, cn_) in enumerate(SH_CHUNKS):
                        last = mm(PS[:, 4 + t, 0:E], sact[0:cn_, i, t * P:(t + 1) * P], down_sb[0:cn_, i, :],
                                  start=(i == 0), stop=(i == len(SH_CHUNKS) - 1))
                    last.then_inc(s_sp, 1)

            shared(0, first=True)
            with pe.Fori(1, TURNS) as j:
                shared(j)

        @block.scalar
        def _(act):
            a = nc.scalar.activation
            act.wait_ge(s_wm, 16 * 2)
            a(silu_c[:, :, :], cT[:, :, :], ACT.Silu).then_inc(s_silu, 1)
            act.wait_ge(s_rowp, 1)
            a(rows[:, :, :].rearrange("b (i k) f -> b i (k f)", i=2), PS[0:B, 6:8, :], ACT.Copy).then_inc(s_rowr, 1)
            act.wait_ge(s_cst, 16)
            act.wait_ge(s_w, 16 * N_W)
            eps = C("eps")
            with act.Fori(0, TURNS) as j:
                act.wait_ge(s_mv, j + 1)
                a(sd[:, :], mv[:, :, 1], ACT.Sqrt, bias=eps).then_inc(s_sd, 1)
                act.wait_ge(s_now, j + 1)
                for bb in range(BPG):
                    act.wait_ge(s_xnT, 4 * j + 2 * bb + 2)
                    for c in range(EC):
                        a(hT[:, c, bb * N:(bb + 1) * N], PS[:, bb, c * N:(c + 1) * N], ACT.Identity,
                          bias=mod_now[:, 0, c, bb:bb + 1], scale=mod_now[:, 1, c, bb:bb + 1]).then_inc(s_hT, 1)

                def squares(u):
                    act.wait_ge(s_cent, 4 * j + u + 1)
                    if u >= 2:
                        act.wait_ge(s_var, 4 * j + u - 1)
                    a(sq[:, u % 2, :], PS[:, 4 + u % 2, :], ACT.Square).then_inc(s_sq, 1)

                def deviation(u):
                    act.wait_ge(s_var, 4 * j + u + 1)
                    if u >= 2:
                        act.wait_ge(s_fin, 4 * j + u - 1)
                    a(qsd[:, u % 2, :], PS[:, 6 + u % 2, :], ACT.Sqrt, bias=eps).then_inc(s_qsd, 1)

                def q_scale(u):
                    if u >= 1:
                        act.wait_ge(s_fin, 4 * j + u)
                    a(scaled[:, :], PS[:, 4 + u % 2, :], ACT.Identity, scale=ln_col[:, 0:1]).then_inc(s_scale, 1)

                def q_high(u):
                    act.wait_ge(s_fin, 4 * j + u + 1)
                    a(q_hi[:, u, :], q_sum[:, :], ACT.Identity).then_inc(s_qh, 1)

                def k_high(f):
                    act.wait_ge(s_kk, 2 * j + f + 1)
                    a(k_hi[:, f, :], kk[:, f, :], ACT.Identity).then_inc(s_kh, 1)

                def copy_v(i):
                    act.wait_ge(s_v, 4 * j + 2 * i + 2)
                    hd = "p t h d -> p (t h) d"
                    ps = PS[:, i, :].rearrange("p (h d) -> p h d", d=D)
                    a(v_sb[:, 2 * i:2 * i + 2, :, :].rearrange(hd), ps, ACT.Identity)
                    a(va[:, 2 * i:2 * i + 2, :, 0, 0:D].rearrange(hd), ps, ACT.Identity).then_inc(s_vh, 1)

                squares(0)
                copy_v(0)
                deviation(0)
                q_scale(0)
                squares(1)
                copy_v(1)
                q_high(0)
                deviation(1)
                q_scale(1)
                squares(2)
                q_high(1)
                deviation(2)
                squares(3)
                deviation(3)
                k_high(0)
                k_high(1)

                def high(n):
                    act.wait_ge(s_s4, UNITS * j + n + 1)
                    if n >= A_RING:
                        act.wait_ge(s_av, UNITS * j + n - A_RING + 1)
                    a(a_hi[:, n % A_RING, :, :], s2[:, n % S_RING, :, :], ACT.Identity).then_inc(s_hi, 1)

                def square(n):
                    act.wait_ge(s_sc, UNITS * j + n + 1)
                    if n >= S_RING:
                        act.wait_ge(s_lo, UNITS * j + n - S_RING + 1)
                    a(s2[:, n % S_RING, :, :], PS[:, 2 * (n % 2):2 * (n % 2) + 2, 0:384], ACT.Square).then_inc(s_s2, 1)

                def copy_attended(n):
                    act.wait_ge(s_av, UNITS * j + n + 1)
                    if n >= 2:
                        act.wait_ge(s_back, UNITS * j + n - 1)
                    a(rows_av[:, n % 2, :, :].rearrange("p r n -> p (r n)"), PS[0:2 * (D + 1), 4 + n % 2, :], ACT.Copy)\
                        .then_inc(s_avc, 1)

                for n in range(UNITS + 3):
                    if n < UNITS:
                        square(n)
                    if 1 <= n < UNITS + 1:
                        high(n - 1)
                    if n >= 3:
                        copy_attended(n - 3)

                for t in range(TPG):
                    act.wait_ge(s_ot, 4 * j + t + 1)
                    if t >= 2:
                        act.wait_ge(s_ao, 4 * j + t - 1)
                    a(oT[:, t % 2, :, :].rearrange("p c n -> p (c n)"), PS[:, t % 2, 0:E], ACT.Copy).then_inc(s_oT, 1)
                for bb in range(BPG):
                    act.wait_ge(s_mv2, 2 * j + bb + 1)
                    a(sd[:, 2 * bb:2 * bb + 2], mv[:, 2 * bb:2 * bb + 2, 1], ACT.Sqrt, bias=eps).then_inc(s_sd2, 1)
                act.wait_ge(s_h2t, j + 1)
                a(h2T[:, :, :], PS[:, 4:6, :], ACT.Copy).then_inc(s_h2T, 1)
                act.wait_ge(s_lgp, j + 1)
                a(lg[:, bass.ds(j * TPG * NEXP, TPG * NEXP)], PS[:, 6, 0:TPG * NEXP], ACT.Copy).then_inc(s_lg, 1)

            act.wait_ge(s_ls, 1)
            a(ex[:, :, :], ex[:, :, :], ACT.Exp).then_inc(s_ex, 1)

            def silu(tile, slot, first=False):
                b = slot % 2
                act.wait_ge(s_m1, tile + 1)
                if not first:
                    act.wait_ge(s_m2, tile - 1)
                a(hx[:, b, :, :].rearrange("p i n -> p (i n)"), PS[0:IP, 4 + b, 0:IC * P], ACT.Silu).then_inc(s_hx, 1)

            def store(tile, slot):
                act.wait_ge(s_yb, tile + 1)
                act.dma_start(y_dram[bass.ds(tile * P, P), :], yb[:, slot, :]).then_inc(s_yd[slot], 16)

            silu(0, 0, first=True)
            silu(1, 1, first=True)
            silu(2, 2)
            store(0, 0)
            with act.Fori(0, SLOT_TILES // RING - 1) as q:
                for r in range(3, 3 + RING):
                    silu(RING * q + r, r % RING)
                    store(RING * q + r - 2, (r - 2) % RING)
            g = SLOT_TILES - 1
            silu(g, g % RING)
            for t in (g - 2, g - 1, g):
                store(t, t % RING)
            for slot in range(RING):
                act.wait_ge(s_yd[slot], 16 * (SLOT_TILES // RING))
            act.sem_inc(s_ystored, 1)

            def shared(j, first=False):
                for i, (c0, cn_) in enumerate(SH_CHUNKS):
                    n = 3 * j + i
                    act.wait_ge(s_gp, n + 1)
                    if i >= 2 or not first:
                        act.wait_ge(s_sa, n - 1)
                    a(sg[0:cn_, i % 2, :], PS[0:cn_, 2 * (i % 2), :], ACT.Silu).then_inc(s_sg, 1)

            shared(0, first=True)
            with act.Fori(1, TURNS) as j:
                shared(j)

        @block.vector
        def _(dve):
            v = nc.vector
            steps = [0]

            def link(ins):
                steps[0] += 1
                ins.then_inc(s_chain, 1)
                dve.wait_ge(s_chain, steps[0])

            dve.sem_inc(s_h2d, 16)
            dve.wait_ge(s_modp, 1)
            both = PS[:, 0, 0:2 * EC * B]
            v.tensor_copy(mod_col[:, 0, :, :].rearrange("p c b -> p (c b)"), both[:, 0:EC * B])
            v.tensor_scalar(mod_col[:, 1, :, :].rearrange("p c b -> p (c b)"), both[:, EC * B:2 * EC * B], 1.0, None,
                            ALU.add).then_inc(s_modc, 1)
            dve.wait_ge(s_x, 16)
            dve.wait_ge(s_cst, 16)
            dve.wait_ge(s_w, 16 * N_W)
            dve.wait_ge(s_modc, 1)
            v.memset(va[:, :, :, 0, D:D + 1].bitcast(F32).rearrange("p t h d -> p (t h) d"), 1.0)
            v.memset(va[:, :, :, 1, D:D + 1].bitcast(F32).rearrange("p t h d -> p (t h) d"), 0.0).then_inc(s_set, 1)

            PER = 24
            with dve.Fori(0, TURNS) as j:
                done = [0]

                def next_(ins):
                    done[0] += 1
                    ins.then_inc(s_turn, 1)
                    dve.wait_ge(s_turn, j * PER + done[0])

                def moments(ts):
                    for t in ts:
                        ins = v.bn_stats(st[:, t, :], x_all[:, bass.ds((TPG * j + t) * E, E)])
                    done[0] += 1
                    ins.then_inc(s_turn, 1)
                    then(dve, s_turn, j * PER + done[0])
                    for t in ts:
                        ins = v.bn_aggr(mv[:, t, :], st[:, t, :])
                    return ins

                moments(range(TPG)).then_inc(s_mv, 1)
                v.tensor_copy(mod_now[:, :, :, :].rearrange("p k c b -> p (k c) b"),
                              mod_col[:, :, :, :].rearrange("p k c b -> p (k c) b")[:, :, bass.ds(BPG * j, BPG)])\
                    .then_inc(s_now, 1)
                dve.wait_ge(s_sd, j + 1)
                next_(v.reciprocal(rstd[:, :], sd[:, :]))
                for t in range(TPG):
                    v.tensor_scalar(xn[:, t, :], x_all[:, bass.ds((TPG * j + t) * E, E)], mv[:, t, 0:1],
                                    rstd[:, t:t + 1], ALU.subtract, ALU.mult).then_inc(s_xn, 1)
                cos = C("cos").unsqueeze(1).broadcast_to([P, BPG, N])
                sin = C("sin").unsqueeze(1).broadcast_to([P, BPG, N])

                def two(ap):
                    return ap.rearrange("p (b n) -> p b n", b=BPG)

                def rope(u):
                    dve.wait_ge(s_proj, 4 * j + u + 1)
                    if u >= 2:
                        dve.wait_ge(s_cent, 4 * j + u - 1)
                    v.tensor_tensor(two(rc[:, u % 2, :]), two(PS[:, 2 + u % 2, :]), cos, ALU.mult)
                    v.tensor_tensor(two(rs[:, u % 2, :]), two(PS[:, 2 + u % 2, :]), sin, ALU.mult).then_inc(s_rope, 1)

                def q_shift(u):
                    dve.wait_ge(s_scale, 2 * j + u + 1)
                    if u >= 1:
                        dve.wait_ge(s_qh, 2 * j + u)
                        dve.wait_ge(s_ql, 2 * j + u)
                    v.scalar_tensor_tensor(out=q_sum[:, :], in0=qsd[:, u % 2, :], scalar=ln_col[:, 1:2],
                                           in1=scaled[:, :], op0=ALU.mult, op1=ALU.add).then_inc(s_fin, 1)

                def q_low(u):
                    dve.wait_ge(s_qh, 2 * j + u + 1)
                    v.tensor_tensor(q_lo[:, u, :], q_sum[:, :], q_hi[:, u, :].bitcast(F32), ALU.subtract)\
                        .then_inc(s_ql, 1)

                def k_norm(u):
                    dve.wait_ge(s_qsd, 4 * j + u + 1)
                    dve.wait_ge(s_fin, 4 * j + u)
                    next_(v.reciprocal(qrs[:, :], qsd[:, u % 2, :]))
                    v.tensor_tensor(kk[:, u - 2, :], PS[:, 4 + u % 2, :], qrs[:, :], ALU.mult).then_inc(s_fin, 1)

                rope(0)
                rope(1)
                rope(2)
                q_shift(0)
                rope(3)
                q_low(0)
                q_shift(1)
                q_low(1)
                k_norm(2)
                k_norm(3)

                def low(n):
                    dve.wait_ge(s_hi, UNITS * j + n + 1)
                    flat = "p r n -> p (r n)"
                    v.tensor_tensor(a_lo[:, n % A_RING, :, :].rearrange(flat), s2[:, n % S_RING, :, :].rearrange(flat),
                                    a_hi[:, n % A_RING, :, :].bitcast(F32).rearrange(flat), ALU.subtract)\
                        .then_inc(s_lo, 1)

                for n in range(UNITS):
                    dve.wait_ge(s_msk, UNITS * j + n + 1)
                    m = s2[:, n % S_RING, :, :].rearrange("p r n -> p (r n)")
                    v.tensor_tensor(m, m, m, ALU.mult).then_inc(s_s4, 1)
                    if n >= 1:
                        low(n - 1)
                    if n % 2 == 0 and n >= 6:
                        heads_norm(dve, j, n // 2 - 3, next_)
                low(UNITS - 1)
                for idx in range(UNITS // 2 - 3, UNITS // 2):
                    heads_norm(dve, j, idx, next_)

                for bb in range(BPG):
                    def row(kind):
                        return mod_row[:, bb, kind * E:(kind + 1) * E].unsqueeze(1).broadcast_to([P, 2, E])

                    def tiles(ap):
                        return ap.rearrange("p (t f) -> p t f", t=2)

                    xs = tiles(x_all[:, bass.ds((TPG * j + 2 * bb) * E, 2 * E)])
                    dve.wait_ge(s_ao, 4 * j + 2 * bb + 2)
                    if bb == 0:
                        dve.wait_ge(s_bc, 16 * j + 16)
                    next_(v.tensor_tensor(tiles(gated[:, bb, :]), tiles(PS[:, 2 + bb, :]), row(0), ALU.mult))
                    v.tensor_tensor(xs, tiles(gated[:, bb, :]), xs, ALU.add).then_inc(s_turn, 1)
                    done[0] += 1
                    then(dve, s_turn, j * PER + done[0])
                    moments((2 * bb, 2 * bb + 1)).then_inc(s_mv2, 1)
                    dve.wait_ge(s_sd2, 2 * j + bb + 1)
                    next_(v.reciprocal(rstd[:, 2 * bb:2 * bb + 2], sd[:, 2 * bb:2 * bb + 2]))
                    if bb == 0:
                        dve.wait_ge(s_h2d, 16 * j + 16)
                    for t in (2 * bb, 2 * bb + 1):
                        ins = v.tensor_scalar(h2[:, t, :], x_all[:, bass.ds((TPG * j + t) * E, E)], mv[:, t, 0:1],
                                              rstd[:, t:t + 1], ALU.subtract, ALU.mult)
                    hh = h2[:, 2 * bb:2 * bb + 2, :]
                    ins.then_inc(s_turn, 1)
                    done[0] += 1
                    dve.wait_ge(s_turn, j * PER + done[0])
                    next_(v.tensor_tensor(hh, hh, row(2), ALU.mult))
                    v.tensor_tensor(hh, hh, row(1), ALU.add).then_inc(s_h2, 1)
                dve.wait_ge(s_xr, 16)
                assert done[0] == PER, done[0]

            dve.wait_ge(s_lg, TURNS)
            dve.wait_ge(s_h2k, TURNS)
            v.memset(pr[:, :, NEXP:NEXP + 1], 8.0)
            v.memset(pr[:, :, NEXP + 1:NEXP + 2], 9.0)
            v.memset(cum[:, 0, :], 0.0)
            wide = [P, TILES, NEXP]
            lg3 = lg[:, :].rearrange("p (t e) -> p t e", t=TILES)
            link(v.tensor_reduce(mx[:, :], lg3, AX_X, ALU.max))
            v.tensor_tensor(ex[:, :, :], lg3, mx[:, :].unsqueeze(2).broadcast_to(wide), ALU.subtract).then_inc(s_ls, 1)
            dve.wait_ge(s_ex, 1)
            link(v.tensor_reduce(zs[:, :], ex[:, :, :], AX_X, ALU.add))
            link(v.reciprocal(mx[:, :], zs[:, :]))
            probs = pr[:, :, 0:NEXP]
            link(v.tensor_tensor(probs, ex[:, :, :], mx[:, :].unsqueeze(2).broadcast_to(wide), ALU.mult))
            for i in range(TILES):
                ins = v.max(p8[:, i, :], pr[:, i, 0:NEXP])
            link(ins)
            v.memset(p8[:, :, TOPK:TOPK + 1], 8.0)
            link(v.memset(p8[:, :, TOPK + 1:8], 9.0))
            for i in range(TILES):
                ins = v.match_replace(rep[:, i, :], p8[:, i, :], pr[:, i, :], -1.0)
            link(ins)
            v.tensor_scalar(mask[:, :, :], rep[:, :, 0:NEXP], -1.0, None, ALU.is_equal).then_inc(s_mask, 1)
            dve.wait_ge(s_mask, 1)
            for i in range(1, TILES):
                ins = v.tensor_tensor(cum[:, i, :], cum[:, i - 1, :], mask[:, i - 1, :], ALU.add)
                if i < TILES - 1:
                    link(ins)
            ins.then_inc(s_mask, 1)
            dve.wait_ge(s_n, 1)
            link(v.tensor_copy(n_col[:, :], PS[0:NEXP, 0, 0:1]))
            link(v.tensor_scalar(n_cmp[:, :], C("steps", NEXP), n_col[:, 0:1], None, ALU.is_lt))
            link(v.tensor_reduce(t_col[:, :], n_cmp[:, :], AX_X, ALU.add))
            v.tensor_copy(t_col16[:, :], t_col[:, :])
            v.tensor_scalar(t_wide[:, :], H("ones", NEXP), t_col[:, 0:1], float(P), ALU.mult, ALU.mult)\
                .then_inc(s_t, 1)
            dve.wait_ge(s_end, 1)
            link(v.tensor_copy(e_end[:, :], PS[0:NEXP, 3, 0:1]))
            v.tensor_scalar(e_cmp[:, :], H("tiles", NEXP), e_end[:, 0:1], None, ALU.is_ge).then_inc(s_ec, 1)
            dve.wait_ge(s_e, 1)
            link(v.tensor_scalar(e_row[:, :], PS[0:1, 4, 0:SLOT_TILES], float(NEXP - 1), None, ALU.min))
            v.tensor_copy(e_of[:, :], e_row[:, :]).then_inc(s_eo, 1)
            for half in range(2):
                tt = slice(8 * half, 8 * half + 8)
                ins = v.scalar_tensor_tensor(out=pos1[:, tt, :].rearrange("p t e -> p (t e)"), in0=PS[:, 1 + half, :],
                                             scalar=1.0, in1=mask[:, tt, :].rearrange("p t e -> p (t e)"),
                                             op0=ALU.add, op1=ALU.mult)
            link(ins)
            for i in range(TILES):
                ins = v.max(slot8[:, i, :], pos1[:, i, :])
            link(ins)
            v.tensor_scalar(slot_i[:, :], slot8[:, :, :].rearrange("p t k -> p (t k)"), -1.0, 0.0,
                            ALU.add, ALU.max).then_inc(s_slots, 1)
            dve.wait_ge(s_slots, 1)
            v.tensor_scalar(slot_g[:, :], slot_i[:, :], 7, None, ALU.arith_shift_right)
            link(v.tensor_scalar(slot_s[:, :], slot_i[:, :], P - 1, None, ALU.bitwise_and))
            v.tensor_copy(col_g[:, :], slot_g[:, :])
            link(v.tensor_copy(col_s[:, :], slot_s[:, :]))
            t0 = CST["token"][0]

            def one_hots(i, b, first=False):
                if not first:
                    dve.wait_ge(s_hotm, i - 1)
                for k in range(TOPK):
                    at = bass.ds(i * 8 + k, 1)
                    v.tensor_scalar(hot_s[:, b, k, :], H("slots"), col_s[:, at], None, ALU.is_equal)
                    ins = v.tensor_scalar(hot_g[:, b, k, :], H("tiles"), col_g[:, at], cs[:, bass.ds(i + t0, 1)],
                                          ALU.is_equal, ALU.mult)
                ins.then_inc(s_hot, 1)

            one_hots(0, 0, first=True)
            one_hots(1, 1, first=True)
            with dve.Fori(1, TILES // 2) as r:
                for b in range(2):
                    one_hots(2 * r + b, b)
            dve.wait_ge(s_hotm, TILES)
            v.tensor_copy(tok_of[:, :], PS[:, 3, 0:SLOT_TILES]).then_inc(s_tok, 1)

            def copy_x(tile, slot, first=False):
                b = slot % 2
                dve.wait_ge(s_xt, tile + 1)
                if not first:
                    dve.wait_ge(s_m1, tile - 1)
                v.tensor_copy(xgT[:, b, :, :].rearrange("p c n -> p (c n)"), PS[:, b, 0:E]).then_inc(s_xT, 1)

            def copy_y(tile, rnd, slot, first=False):
                b = slot % 2
                dve.wait_ge(s_m2, tile + 1)
                if not first:
                    dve.wait_ge(s_yd[slot], 16 * rnd)
                v.tensor_copy(yb[:, slot, :], PS[:, 6 + b, 0:E]).then_inc(s_yb, 1)

            copy_x(0, 0, first=True)
            copy_x(1, 1, first=True)
            for g in range(1, RING + 1):
                copy_x(g + 1, (g + 1) % RING)
                copy_y(g - 1, 0, g - 1, first=True)
            with dve.Fori(1, SLOT_TILES // RING - 1) as q:
                for r in range(1, 1 + RING):
                    copy_x(RING * q + r + 1, (r + 1) % RING)
                    copy_y(RING * q + r - 1, q, r - 1)
            g = SLOT_TILES - RING
            for r in range(1, 1 + RING):
                if g + r + 1 < SLOT_TILES:
                    copy_x(g + r + 1, (r + 1) % RING)
                copy_y(g + r - 1, g // RING, r - 1)

            link(v.tensor_tensor(comb[:, :, :], mask[:, :, :], probs, ALU.mult))
            link(v.tensor_reduce(zs[:, :], comb[:, :, :], AX_X, ALU.add))
            link(v.reciprocal(mx[:, :], zs[:, :]))
            link(v.tensor_tensor(comb[:, :, :], comb[:, :, :], mx[:, :].unsqueeze(2).broadcast_to(wide), ALU.mult))
            for k in range(TOPK):
                link(v.tensor_tensor(ex[:, :, :], pos1[:, :, :],
                                     slot8[:, :, k:k + 1].broadcast_to(wide), ALU.is_equal))
                link(v.tensor_tensor(ex[:, :, :], ex[:, :, :], comb[:, :, :], ALU.mult))
                link(v.tensor_reduce(wk[:, k, :], ex[:, :, :], AX_X, ALU.add))

            dve.wait_ge(s_gr, 16)
            gate_rows = gate_row[:, :, :].rearrange("p b f -> p (b f)")

            def combine(i, j, t, chain, first=False):
                b = t % 2
                rnd = 2 * j + t // 2
                dve.wait_ge(s_sp, i + 1)
                dve.wait_ge(s_yg[b], 16 * TOPK * (rnd + 1))
                if not first:
                    dve.wait_ge(s_out[b], 16 * rnd)
                for k in range(TOPK):
                    src = PS[:, 4 + t, 0:E] if k == 0 else acc[:, b, :]
                    ins = v.scalar_tensor_tensor(out=acc[:, b, :], in0=yg[:, b, k, :],
                                                 scalar=wk[:, k, bass.ds(i, 1)], in1=src,
                                                 op0=ALU.mult, op1=ALU.add)
                    if k < TOPK - 1:
                        chain(ins)
                ins.then_inc(s_acc, 1)
                dve.wait_ge(s_acc, i + 1)
                chain(v.tensor_tensor(acc[:, b, :], acc[:, b, :], gate_rows[:, bass.ds(rnd * E, E)], ALU.mult))
                v.tensor_tensor(acc[:, b, :], acc[:, b, :], x_all[:, bass.ds(i * E, E)], ALU.add)\
                    .then_inc(s_final, 1)

            def group(j, chain, first=False):
                for i, (c0, cn_) in enumerate(SH_CHUNKS):
                    n = 3 * j + i
                    dve.wait_ge(s_sg, n + 1)
                    if i == 0 and not first:
                        dve.wait_ge(s_sp, 4 * j)
                    v.tensor_tensor(sact[0:cn_, i, :], sg[0:cn_, i % 2, :], PS[0:cn_, 2 * (i % 2) + 1, :], ALU.mult)\
                        .then_inc(s_sa, 1)
                for t in range(TPG):
                    combine(4 * j + t, j, t, chain, first=first and t < 2)

            group(0, link, first=True)
            before = steps[0]
            per = TPG * TOPK
            with dve.Fori(1, TURNS) as j:
                count = [0]

                def linked(ins):
                    count[0] += 1
                    ins.then_inc(s_chain, 1)
                    dve.wait_ge(s_chain, j * per + before - per + count[0])

                group(j, linked)
                assert count[0] == per

        @block.gpsimd
        def _(pool):
            g = nc.gpsimd
            psteps = [0]

            def plink(ins):
                psteps[0] += 1
                ins.then_inc(s_pchain, 1)
                pool.wait_ge(s_pchain, psteps[0])

            pool.wait_ge(s_rowr, 1)
            gates = rows[:, 0:4:3, :]
            g.tensor_scalar(rows[:, 2, :], rows[:, 2, :], 1.0, None, ALU.add)
            plink(g.tensor_scalar(gate_sign[:, :, :], gates, 0.0, 2.0, ALU.is_ge, ALU.mult))
            plink(g.tensor_scalar(gate_sign[:, :, :], gate_sign[:, :, :], -1.0, None, ALU.add))
            plink(g.tensor_tensor(gate_size[:, :, :], gates, gate_sign[:, :, :], ALU.mult))
            plink(g.tensor_scalar(gate_size[:, :, :], gate_size[:, :, :], 0.25, None, ALU.max))
            g.tensor_tensor(gates, gate_sign[:, :, :], gate_size[:, :, :], ALU.mult).then_inc(s_rows, 1)
            pool.wait_ge(s_set, 1)
            with pool.Fori(0, TURNS) as j:
                for i in range(2):
                    then(pool, s_vh, 2 * j + i + 1)
                    hd = "p t h d -> p (t h) d"
                    g.tensor_tensor(va[:, 2 * i:2 * i + 2, :, 1, 0:D].rearrange(hd),
                                    v_sb[:, 2 * i:2 * i + 2, :, :].rearrange(hd),
                                    va[:, 2 * i:2 * i + 2, :, 0, 0:D].bitcast(F32).rearrange(hd), ALU.subtract)\
                        .then_inc(s_va, 1)
                for f in range(2):
                    then(pool, s_fin, 4 * j + 2 + f + 1)
                    g.tensor_scalar(kk[:, f, :], kk[:, f, :], ln_col[:, 0:1], ln_col[:, 1:2], ALU.mult, ALU.add)\
                        .then_inc(s_kk, 1)
                    then(pool, s_kh, 2 * j + f + 1)
                    g.tensor_tensor(k_lo[:, f, :], kk[:, f, :], k_hi[:, f, :].bitcast(F32), ALU.subtract)\
                        .then_inc(s_kl, 1)
                for n in range(UNITS):
                    then(pool, s_s2, UNITS * j + n + 1)
                    m = s2[:, n % S_RING, :, 0:2 * P].rearrange("p r (a n) -> p r a n", a=2)
                    g.affine_select(out=m, in_=m, pattern=[[0, 2], [0, 2], [1, P]], compare_op=ALU.is_ge, fill=0.0,
                                    base=0, channel_multiplier=-1).then_inc(s_msk, 1)
                then(pool, s_h2T, j + 1)
                g.tensor_copy(h2T_all[:, :, bass.ds(j * GROUP, GROUP)], h2T[:, :, :]).then_inc(s_h2k, 1)

            pool.wait_ge(s_tok, 1)
            pool.wait_ge(s_h2d, 16 * TURNS + 16)

            def gather(index, slot):
                g.indirect_dma_start(out=xg[:, slot, :], out_offset=None, in_=h2_dram,
                                     in_offset=bass.IndirectOffsetOnAxis(ap=index, axis=0)).then_inc(s_xg[slot], 16)

            for slot in range(RING):
                gather(tok_of[:, slot:slot + 1], slot)
            with pool.Fori(1, SLOT_TILES // RING) as r:
                for slot in range(RING):
                    tile = RING * r + slot
                    then(pool, s_xt, tile - RING + 1)
                    g.tensor_copy(ti[:, slot:slot + 1], tok_of[:, bass.ds(tile, 1)]).then_inc(s_ti, 1)
                    then(pool, s_ti, tile - RING + 1)
                    gather(ti[:, slot:slot + 1], slot)

            pool.wait_ge(s_ystored, 1)
            pool.wait_ge(s_slots, 1)
            idx = slot_i[:, :].bitcast(U32)

            def choices(i, b):
                g.tensor_copy(ki[:, b, :], idx[:, bass.ds(8 * i, TOPK)]).then_inc(s_ki, 1)
                then(pool, s_ki, i + 1)
                for k in range(TOPK):
                    g.indirect_dma_start(out=yg[:, b, k, :], out_offset=None, in_=y_dram,
                                         in_offset=bass.IndirectOffsetOnAxis(ap=ki[:, b, k:k + 1], axis=0))\
                        .then_inc(s_yg[b], 16)

            choices(0, 0)
            choices(1, 1)
            with pool.Fori(1, TILES // 2) as r:
                for b in range(2):
                    then(pool, s_acc, 2 * r + b - 1)
                    choices(2 * r + b, b)


def constants():
    import numpy as np
    cst = np.zeros((P, NCST), np.float32)

    def put(name, a):
        lo, _ = CST[name]
        a = np.asarray(a, np.float32)
        cst[0:a.shape[0], lo:lo + a.shape[1]] = a

    head = np.arange(P) // D
    same = (head[:, None] == head[None, :]).astype(np.float32)
    centre = np.eye(P, dtype=np.float32) - same / np.float32(D)
    swap = np.arange(P) ^ (D // 2)
    put("ident", np.eye(P))
    put("centre", centre)
    put("centre_swap", centre[swap])
    put("var", same / np.float32(D))
    inv = (np.float32(1.0) / np.float32(10000.0) ** (np.arange(0, D, 2, dtype=np.float32) / np.float32(D))).astype(np.float32)
    ang = np.arange(N, dtype=np.float32)[None, :] * inv[:, None]
    half = np.arange(P) % (D // 2)
    first = (np.arange(P) % D < D // 2)[:, None]
    put("cos", np.cos(ang)[half])
    put("sin", np.where(first, np.sin(ang)[half], -np.sin(ang)[half]))
    put("even", (head % 2 == 0)[:, None])
    put("odd", (head % 2 == 1)[:, None])
    put("eps", np.full((P, 1), EPS))
    put("token", np.arange(P)[:, None] + P * np.arange(TILES)[None, :])
    put("steps", np.tile(P * np.arange(TOK // P)[None, :], (P, 1)))
    hst = np.zeros((P, NHST), np.float16)

    def put16(name, a):
        lo, _ = HST[name]
        a = np.asarray(a, np.float16)
        hst[0:a.shape[0], lo:lo + a.shape[1]] = a

    put16("before", np.triu(np.ones((P, P)), 1))
    put16("ones", np.ones((P, P)))
    put16("exp_before", np.triu(np.ones((NEXP, NEXP)), 1))
    put16("exp_upto", np.triu(np.ones((NEXP, NEXP)), 0))
    put16("tiles", np.tile(np.arange(SLOT_TILES)[None, :], (P, 1)))
    put16("slots", np.tile(np.arange(P)[None, :], (P, 1)))
    return cst, hst


def kernel(L0_attn_x, L0_attn_w_qkv, L0_attn_w_out, L0_attn_ln_scale, L0_attn_ln_bias, L0_ffn_gate_w,
           L0_ffn_experts_w1, L0_ffn_experts_w2, L0_ffn_shared_gate_up, L0_ffn_shared_down, L0_c, L0_wmod):
    import numpy as np
    import concourse.bacc as bacc
    from concourse.bass_utils import run_bass_kernel_spmd

    def lay(a):
        return np.ascontiguousarray(a)

    cst, hst = constants()
    ln = np.stack([np.tile(np.asarray(L0_attn_ln_scale), P // D), np.tile(np.asarray(L0_attn_ln_bias), P // D)], axis=1)
    arrays = {
        "x": lay(L0_attn_x).reshape(TOK, E),
        "w_qkv": lay(L0_attn_w_qkv),
        "w_out": lay(L0_attn_w_out),
        "ln_cols": lay(ln),
        "gate_t": lay(np.asarray(L0_ffn_gate_w).T),
        "w1_t": lay(np.asarray(L0_ffn_experts_w1).transpose(0, 2, 1)),
        "w2_t": lay(np.asarray(L0_ffn_experts_w2).transpose(0, 2, 1)),
        "gu_t": lay(np.asarray(L0_ffn_shared_gate_up).T),
        "down_t": lay(np.asarray(L0_ffn_shared_down).T),
        "c_t": lay(np.asarray(L0_c).T),
        "wmod": lay(L0_wmod),
        "cst": cst,
        "hst": hst,
    }
    nc = bacc.Bacc("TRN2", target_bir_lowering=False, num_devices=1)
    args = [nc.dram_tensor(name, a.shape, mybir.dt.from_np(a.dtype), kind="ExternalInput").ap()
            for name, a in arrays.items()]
    out = nc.dram_tensor("out", (TOK, E), F32, kind="ExternalOutput").ap()
    build(nc, *args, out)
    r = run_bass_kernel_spmd(nc, [arrays], core_ids=[0])
    return r.results[0]["out"].reshape(B, N, E)
```

```python
from contextlib import ExitStack

import concourse.bass as bass
from concourse import mybir

ALU = mybir.AluOpType
ACT = mybir.ActivationFunctionType
F32 = mybir.dt.float32
F32R = mybir.dt.float32r
F16 = mybir.dt.float16
I32 = mybir.dt.int32
U32 = mybir.dt.uint32
AX_X = mybir.AxisListType.X

P = 128
B, N, E = 8, 256, 256
TOK = B * N
TILES = TOK // P
EC = E // P
HEADS, D = 16, 16
QK = 2 * E // P
GROUP = 512
TURNS = TOK // GROUP
S_RING, A_RING, K_RING = 4, 3, 2
SCALAR_HOTS, VECTOR_HOTS = 3, 1
UNITS = 16
ROUTE_PARTS = 4
HB = P // D
TPG = GROUP // P
BPG = GROUP // N
NEXP, INNER, TOPK = 64, 176, 6
IC = 2
IP = INNER // IC
ROUTED_TILES = (TOK * TOPK + NEXP * (P - 1)) // P
RING = 4
SLOT_TILES = -(-ROUTED_TILES // RING) * RING
SHARED = 352
SH_CHUNKS = [(0, 128), (128, 128), (256, 96)]
EPS = 1e-5

CST = {}
_at = 0
for _name, _n in (("ident", P), ("centre", P), ("centre_swap", P), ("var", P), ("cos", N), ("sin", N),
                  ("one", 1), ("eps", 1), ("token", TILES), ("steps", TOK // P)):
    CST[_name] = (_at, _at + _n)
    _at += _n
NCST = _at
HST = {}
_at = 0
for _name, _n in (("before", P), ("ones", P), ("exp_before", NEXP), ("exp_upto", NEXP),
                  ("tiles", SLOT_TILES), ("slots", P)):
    HST[_name] = (_at, _at + _n)
    _at += _n
NHST = _at


def build(nc, x, w_qkv, w_out, ln_cols, gate_t, w1_t, w2_t, gu_t, down_t, c_t, wmod, cst, hst, out):
    with ExitStack() as ctx:
        def sb(name, shape, dt=F32):
            return ctx.enter_context(nc.sbuf_tensor(name, shape, dt))

        def sem(name):
            return ctx.enter_context(nc.semaphore(name))

        rows_dram = nc.dram_tensor("modulation_rows", [B, 4 * E], F32, kind="Internal").ap()
        h2_dram = nc.dram_tensor("h2_rows", [TOK, E], F32, kind="Internal").ap()
        y_dram = nc.dram_tensor("expert_rows", [SLOT_TILES * P, E], F32, kind="Internal").ap()

        PS = ctx.enter_context(nc.psum_tensor("PS", [P, 8, 512], F32))

        cs = sb("cs", [P, NCST])
        hs = sb("hs", [P, NHST], F16)
        ln_col = sb("ln_col", [P, 2])
        wqkv_sb = sb("wqkv_sb", [P, EC, 3 * E])
        wout_sb = sb("wout_sb", [P, EC, E])
        gate_sb = sb("gate_sb", [P, EC, NEXP])
        mod_col = sb("mod_col", [P, 2, EC, B])
        x_all = sb("x_all", [P, TILES * E])
        h2T_all = sb("h2T_all", [P, EC, TOK])
        lg = sb("lg", [P, TILES * NEXP])
        mx = sb("mx", [P, TILES])
        zs = sb("zs", [P, TILES])
        mask = sb("mask", [P, TILES * NEXP], F16)
        cum = sb("cum", [P, (TILES + 1) * NEXP], F16)
        slot_i = sb("slot_i", [P, TILES * 8], I32)
        slot_g = sb("slot_g", [P, TILES * 8], I32)
        slot_s = sb("slot_s", [P, TILES * 8], I32)
        col_g = sb("col_g", [P, TILES * 8])
        col_s = sb("col_s", [P, TILES * 8])
        tok_of = sb("tok_of", [P, SLOT_TILES], U32)
        n_col = sb("n_col", [NEXP, 1])
        n_cmp = sb("n_cmp", [NEXP, TILES])
        t_col = sb("t_col", [NEXP, 1])
        t_col16 = sb("t_col16", [NEXP, 1], F16)
        t_wide = sb("t_wide", [NEXP, P], F16)
        e_end = sb("e_end", [NEXP, 1])
        e_cmp = sb("e_cmp", [NEXP, SLOT_TILES], F16)
        e_row = sb("e_row", [1, SLOT_TILES])
        e_of = sb("e_of", [1, SLOT_TILES], I32)
        wk = sb("wk", [P, TOPK, TILES])
        early_stack = ExitStack()

        def early(name, shape, dt=F32):
            return early_stack.enter_context(nc.sbuf_tensor(name, shape, dt))

        modulation_stack = ExitStack()

        def modulation(name, shape, dt=F32):
            return modulation_stack.enter_context(nc.sbuf_tensor(name, shape, dt))

        rows = modulation("rows", [B, 4, E])
        gate_size = modulation("gate_size", [B, 2, E])
        gate_sign = modulation("gate_sign", [B, 2, E])
        wmod_sb = modulation("wmod_sb", [P, EC, 6 * E])
        modulation_stack.close()
        h2 = early("h2", [P, TPG, E])
        gated = early("gated", [P, BPG, 2 * E])
        o_sb = gated[:, :, :].rearrange("p b (t f) -> p (b t) f", t=2)
        q_dev = gated[:, :, :]
        s2 = early("s2", [P, S_RING, 2, 384])
        cT = early("cT", [P, EC, B])
        silu_c = early("silu_c", [P, EC, B])
        mod_row = early("mod_row", [P, BPG, 4 * E])
        mod_now = early("mod_now", [P, 2, EC, BPG])
        st = early("st", [P, TPG, 6])
        mv = early("mv", [P, TPG, 2])
        sd = early("sd", [P, TPG])
        rstd = early("rstd", [P, TPG])
        st2 = early("st2", [P, TPG, 6])
        mv2 = early("mv2", [P, TPG, 2])
        sd2 = early("sd2", [P, TPG])
        rstd2 = early("rstd2", [P, TPG])
        xn = early("xn", [P, TPG, E])
        v_sb = xn[:, :, :].rearrange("p t (h d) -> p t h d", d=D)
        lmax = early("lmax", [P, TPG, NEXP + 2])
        top8 = early("top8", [P, TPG, 8])
        rest = early("rest", [P, TPG, NEXP + 2])
        hT = early("hT", [P, EC, GROUP])
        rc = early("rc", [P, 2, GROUP])
        rs = early("rs", [P, 2, GROUP])
        scaled = (rc[:, 0, :], rs[:, 0, :])
        sq = early("sq", [P, 2, GROUP])
        k_dev = early("k_dev", [P, 2, TPG * HB])
        k_rec = early("k_rec", [P, 2, TPG * HB])
        k_rec_wide = early("k_rec_wide", [P, 2, GROUP])
        q_sum = early("q_sum", [P, 2, GROUP])
        q_hi = early("q_hi", [P, 2, GROUP], F32R)
        q_lo = early("q_lo", [P, 2, GROUP], F32R)
        k_hi = early("k_hi", [P, 2, GROUP], F32R)
        k_lo = early("k_lo", [P, 2, GROUP], F32R)
        k_stack = early("k_stack", [P, K_RING, 2, 2, GROUP], F32R)
        q_stack = early("q_stack", [P, 4, 2, GROUP], F32R)
        kk = early("kk", [P, 2, GROUP])
        va = early("va", [P, TPG, HEADS, 2, D + 1], F32R)
        a_hi = early("a_hi", [P, A_RING, 2, 384], F32R)
        a_lo = early("a_lo", [P, A_RING, 2, 384], F32R)
        rows_av = early("rows_av", [2 * (D + 1), 2, 2, N])
        av = early("av", [P, 2 * 4, D + 1])
        rden = early("rden", [P, 2 * 4])
        oT = early("oT", [P, 2, EC, P])
        h2T = s2[:, 0:2, :, :].rearrange("p s r n -> p (s r n)")[:, 0:EC * GROUP].rearrange("p (c n) -> p c n", c=EC)
        early_stack.close()
        def late(name, shape, dt=F32):
            return ctx.enter_context(nc.sbuf_tensor(name, shape, dt))

        yg = late("yg", [P, TPG, TOPK, E])
        ex = late("ex", [P, TILES, NEXP])
        comb = late("comb", [P, TILES, NEXP])
        pos1 = late("pos1", [P, TILES, NEXP])
        slot8 = late("slot8", [P, TILES, 8])
        hot_s = late("hot_s", [P, 2, TOPK, P], F16)
        col_now = late("col_now", [P, 2, TOPK])
        apart = late("apart", [P, 2, SCALAR_HOTS, P], F16)
        hot_g = late("hot_g", [P, 2, TOPK, SLOT_TILES], F16)
        gu_sb = late("gu_sb", [P, EC, 2 * SHARED])
        down_sb = late("down_sb", [P, len(SH_CHUNKS), E])
        sg = late("sg", [P, 2, GROUP])
        sact = late("sact", [P, len(SH_CHUNKS), GROUP])
        ti = late("ti", [P, RING], U32)
        xg = late("xg", [P, RING, E])
        xgT = late("xgT", [P, 2, EC, P])
        w1b = late("w1b", [P, RING, EC, INNER])
        w2b = late("w2b", [IP, RING, IC, E])
        hx = late("hx", [IP, 2, IC, P])
        hx_hi = late("hx_hi", [IP, RING, IC, P], F32R)
        hx_lo = late("hx_lo", [IP, RING, IC, P], F32R)
        w2_hi = late("w2_hi", [IP, RING, IC, E], F32R)
        w2_lo = late("w2_lo", [IP, RING, IC, E], F32R)
        yb = late("yb", [P, RING, E])
        ki = late("ki", [P, TPG, TOPK], U32)
        acc = late("acc", [P, 2, E])
        gate_row = late("gate_row", [P, B, E])

        def C(name, rows_=P):
            a, b = CST[name]
            return cs[0:rows_, a:b]

        def H(name, rows_=P):
            a, b = HST[name]
            return hs[0:rows_, a:b]

        ident = C("ident")

        s_c = sem("c_loaded")
        s_wm = sem("first_modulation_weights_loaded")
        s_wr = sem("other_modulation_weights_loaded")
        s_wo = sem("later_weights_loaded")
        s_w = sem("weights_loaded")
        s_ws = sem("shared_weights_loaded")
        s_cst = sem("constants_loaded")
        s_x = sem("x_loaded")
        s_zero = sem("stacks_zeroed")
        s_set = sem("buffers_set")
        s_silu = sem("silu_c_ready")
        s_modp = sem("mod_product")
        s_modc = sem("mod_columns")
        s_rowp = sem("rows_product")
        s_rowr = sem("rows_product_read")
        s_rows = sem("rows_ready")
        s_rowd = sem("rows_stored_in_dram")
        s_bc = sem("rows_broadcast")
        s_gr = sem("gate_rows_broadcast")
        s_xr = sem("rest_of_x_loaded")
        s_chain = sem("vector_steps")
        s_turn = sem("vector_turn_steps")
        s_mv = sem("moments")
        s_sd = sem("deviation")
        s_xn = sem("normed")
        s_xnT = sem("normed_turned")
        s_now = sem("mod_now_ready")
        s_hT = sem("h_ready")
        s_proj = sem("qk_projected")
        s_rope = sem("rope_products")
        s_cent = sem("centred")
        s_sq = sem("squared")
        s_var = sem("variance")
        s_qsd = sem("head_deviation")
        s_rec = sem("k_deviation_reciprocals")
        s_centk = sem("centred_k_copied")
        s_wide = sem("reciprocals_turned")
        s_fin = sem("centred_read")
        s_scale = sem("q_scaled")
        s_qh = sem("q_high_ready")
        s_ql = sem("q_low_ready")
        s_kk = sem("k_ready")
        s_kh = sem("k_high_ready")
        s_kl = [sem(f"k_low_ready{i}") for i in range(2)]
        s_qst = [sem(f"q_stacked{i}") for i in range(4)]
        s_first = sem("first_heads_stacked_by_gpsimd")
        s_kst = [sem(f"k_stacked{i}") for i in range(4)]
        s_vh = sem("v_high_ready")
        s_hi = sem("weights_high")
        s_lo = sem("weights_low")
        s_off = sem("weights_low_off_the_diagonal")
        s_av4 = sem("attended_read")
        s_v = sem("v_projected")
        s_va = sem("v_copied")
        s_sc = sem("scores")
        s_s2 = sem("scores_squared")
        s_msk = sem("scores_masked")
        s_s4 = sem("scores_fourth")
        s_av = sem("attended")
        s_avc = sem("attended_copied")
        s_back = sem("attended_turned_back")
        s_on = sem("attention_normed")
        s_ot = sem("attention_turned")
        s_oT = sem("attention_turned_copied")
        s_ao = sem("attention_projected")
        s_gated = sem("attention_gated")
        s_res = sem("residual_updated")
        s_mv2 = sem("moments2")
        s_sd2 = sem("deviation2")
        s_h2n = sem("h2_normed")
        s_h2s = sem("h2_scaled")
        s_h2 = sem("h2_ready")
        s_h2d = sem("h2_stored")
        s_h2t = sem("h2_turned")
        s_h2T = sem("h2_turned_copied")
        s_h2k = sem("h2_turned_kept")
        s_lgp = sem("logits_product")
        s_lg = sem("logits_ready")
        s_ls = sem("logits_less_max")
        s_ex = sem("exp_ready")
        s_mask = sem("masks_ready")
        s_n = sem("expert_counts")
        s_t = sem("expert_tiles")
        s_pos = sem("positions")
        s_e = sem("expert_of_tile_sum")
        s_ec = sem("expert_compared")
        s_end = sem("expert_ends")
        s_eo = sem("expert_of_tile")
        s_hot = sem("one_hots")
        s_cols = sem("slot_columns_ready")
        s_pcol = sem("slot_column_copied")
        s_phot = sem("one_hots_of_gpsimd")
        s_apart = sem("distances_squared")
        s_ahot = sem("one_hots_of_scalar")
        s_hotm = sem("one_hots_used")
        s_tok = sem("token_of_slot")
        s_gp = sem("shared_gate_and_up")
        s_sg = sem("shared_gate_copied")
        s_sa = sem("shared_act")
        s_sp = sem("shared_down_product")
        s_ti = sem("tile_indices")
        s_xg = [sem(f"rows_gathered{i}") for i in range(RING)]
        s_w1 = [sem(f"w1_loaded{i}") for i in range(RING)]
        s_w2 = [sem(f"w2_loaded{i}") for i in range(RING)]
        s_yd = [sem(f"rows_stored{i}") for i in range(RING)]
        s_xt = sem("rows_turned")
        s_xT = sem("rows_turned_copied")
        s_m1 = sem("inner_product")
        s_w2h = sem("w2_high_ready")
        s_hx = sem("inner_silu")
        s_hxh = sem("inner_high_ready")
        s_parts = sem("outer_parts_ready")
        s_m2 = sem("outer_product")
        s_yb = sem("outer_copied")
        s_ystored = sem("all_rows_stored")
        s_slots = sem("slots_ready")
        s_ki = sem("choice_indices")
        s_yg = [sem(f"choices_gathered{i}") for i in range(TPG)]
        s_share = sem("choice_shares")
        s_acc = sem("choices_summed")
        s_final = sem("rows_final")
        s_out = [sem(f"out_stored{i}") for i in range(2)]
        s_wait = sem("waited")

        def then(eng, semaphore, value):
            eng.wait_ge(semaphore, value)
            eng.sem_inc(s_wait, 1)

        def lows_of(ops, n, columns):
            return ops.tensor_tensor(a_lo[:, n % A_RING, :, columns], s2[:, n % S_RING, :, columns],
                                     a_hi[:, n % A_RING, :, columns].bitcast(F32), ALU.subtract)

        def split_k(ops, f):
            ops.tensor_tensor(k_lo[:, f, :], kk[:, f, :], k_hi[:, f, :].bitcast(F32), ALU.subtract).then_inc(s_kl[f], 1)

        def k_place(i, head):
            return k_stack[:, i % K_RING, head // 4, :, :]

        def q_place(i, head):
            return q_stack[:, i, :, :]

        def part_of(queue, place, part, i, head, n, semaphore):
            row = 64 * (head // 4) + D * n
            queue.dma_start(place(i, head)[row:row + D, :, :].bitcast(F32),
                            part[head * D:(head + 1) * D, :, :].bitcast(F32)).then_inc(semaphore, 16)

        def stack(queue, place, parts, i, semaphore):
            for head in (i, i + 4):
                for n, part in enumerate(parts):
                    part_of(queue, place, part, i, head, n, semaphore)

        def add_residual(engine, ops, j):
            then(engine, s_gated, BPG * j + BPG)
            xs = x_all[:, bass.ds(TPG * j * E, TPG * E)]
            ops.tensor_tensor(xs, gated[:, :, :].rearrange("p b f -> p (b f)"), xs, ALU.add).then_inc(s_res, 1)

        def second_shift(engine, ops, j):
            def row(bb, kind):
                return mod_row[:, bb, kind * E:(kind + 1) * E].unsqueeze(1).broadcast_to([P, 2, E])

            then(engine, s_h2n, j + 1)
            for bb in range(BPG):
                hh = h2[:, 2 * bb:2 * bb + 2, :]
                ins = ops.tensor_tensor(hh, hh, row(bb, 2), ALU.mult)
            ins.then_inc(s_h2s, 1)
            then(engine, s_h2s, j + 1)
            for bb in range(BPG):
                hh = h2[:, 2 * bb:2 * bb + 2, :]
                ins = ops.tensor_tensor(hh, hh, row(bb, 1), ALU.add)
            ins.then_inc(s_h2, 1)

        def project_out(pe, t, j):
            pe.wait_ge(s_oT, 4 * j + t + 1)
            for c in range(EC):
                last = nc.tensor.matmul(PS[:, 4 + t // 2, (t % 2) * E:(t % 2 + 1) * E], oT[:, t % 2, c, :],
                                        wout_sb[:, c, :], start=(c == 0), stop=(c == EC - 1))
            last.then_inc(s_ao, 1)

        def heads_norm(dve, j, idx, next_):
            v = nc.vector
            bb, i, _ = unit(2 * idx)
            dve.wait_ge(s_back, UNITS * j + 2 * idx + 2)
            if idx >= 1:
                dve.wait_ge(s_on, 8 * j + idx)
            o = PS[:, 6 + idx % 2, 0:2 * 4 * 2 * (D + 1)].rearrange("p (m a d) -> p m d a", a=2, d=D + 1)
            v.tensor_reduce(av[:, :, :], o, AX_X, ALU.add).then_inc(s_av4, 1)
            dve.wait_ge(s_av4, 8 * j + idx + 1)
            next_(v.reciprocal(rden[:, :], av[:, :, D]))
            dst = o_sb[:, 2 * bb:2 * bb + 2, :].rearrange("p t (g i d) -> p t g i d", i=4, d=D)
            v.tensor_tensor(dst[:, :, :, i, :], av[:, :, 0:D].rearrange("p (t g) d -> p t g d", t=2),
                            rden[:, :].rearrange("p (t g) -> p t g", t=2).unsqueeze(3).broadcast_to([P, 2, 4, D]),
                            ALU.mult).then_inc(s_on, 1)

        def centred_in(u):
            return (4, 5, 2, 3)[u]

        def unit(n):
            return n // 2 % 2, n // 4, n % 2

        block = ctx.enter_context(nc.Block())

        @block.sync
        def _(sp):
            x_tiles = x_all[:, :].rearrange("p (t f) -> p t f", f=E)
            wmod_parts = wmod.rearrange("(c p) n -> p c n", p=P)
            sp.dma_start(cT[:, :, :], c_t.rearrange("(c p) b -> p c b", p=P)).then_inc(s_c, 16)
            sp.dma_start(x_tiles[:, 0:TPG, :], x[0:GROUP, :].rearrange("(t p) f -> p t f", p=P)).then_inc(s_x, 16)
            sp.dma_start(wmod_sb[:, :, 0:2 * E], wmod_parts[:, :, 0:2 * E]).then_inc(s_wm, 16)
            sp.dma_start(cs[:, :], cst).then_inc(s_cst, 16)
            sp.dma_start(wqkv_sb[:, :, :], w_qkv.rearrange("(c p) n -> p c n", p=P)).then_inc(s_w, 16)
            sp.dma_start(ln_col[:, :], ln_cols).then_inc(s_w, 16)
            sp.dma_start(wmod_sb[:, :, 2 * E:6 * E], wmod_parts[:, :, 2 * E:6 * E]).then_inc(s_wr, 16)
            sp.dma_start(wout_sb[:, :, :], w_out.rearrange("(c p) n -> p c n", p=P)).then_inc(s_wo, 16)
            sp.dma_start(gate_sb[:, :, :], gate_t.rearrange("(c p) n -> p c n", p=P)).then_inc(s_wo, 16)
            sp.dma_start(hs[:, :], hst).then_inc(s_wo, 16)
            sp.dma_start(x_tiles[:, TPG:TILES, :], x[GROUP:TOK, :].rearrange("(t p) f -> p t f", p=P))\
                .then_inc(s_xr, 16)

            def keep_h2(j):
                then(sp, s_h2, j + 1)
                sp.dma_start(h2_dram[bass.ds(j * GROUP, GROUP), :].rearrange("(t p) f -> p t f", p=P),
                             h2[:, :, :]).then_inc(s_h2d, 16)

            def broadcast_rows(j):
                sp.dma_start(mod_row[:, :, :].rearrange("p b f -> p (b f)"),
                             rows_dram[bass.ds(BPG * j, BPG), :].rearrange("b f -> (b f)").unsqueeze(0)
                             .broadcast_to([P, BPG * 4 * E])).then_inc(s_bc, 16)

            def turn(j, last_open):
                if last_open:
                    keep_h2(j - 1)
                    broadcast_rows(j)
                then(sp, s_kh, 2 * j + 2)
                for head in (0, 4):
                    for n in (0, 2):
                        part_of(sp, k_place, k_hi, 0, head, n, s_kst[0])
                then(sp, s_qh, 2 * j + 2)
                for n in (0, 1):
                    part_of(sp, q_place, q_hi, 0, 4, n, s_qst[0])
                then(sp, s_ql, 2 * j + 2)
                for head in (0, 4):
                    part_of(sp, q_place, q_lo, 0, head, 2, s_qst[0])
                for f in range(2):
                    then(sp, s_kl[f], j + 1)
                stack(sp, k_place, (k_hi, k_lo, k_hi), 1, s_kst[1])
                stack(sp, q_place, (q_hi, q_hi, q_lo), 1, s_qst[1])
                for i in (2, 3):
                    stack(sp, q_place, (q_hi, q_hi, q_lo), i, s_qst[i])
                    then(sp, s_sc, UNITS * j + 4 * (i - 1))
                    stack(sp, k_place, (k_hi, k_lo, k_hi), i, s_kst[i])

            sp.wait_ge(s_zero, 1)
            turn(0, False)
            sp.wait_ge(s_rows, 1)
            sp.dma_start(rows_dram.rearrange("b (k f) -> b k f", k=4), rows[:, :, :]).then_inc(s_rowd, 16)
            sp.wait_ge(s_rowd, 16)
            broadcast_rows(0)
            with sp.Fori(1, TURNS) as j:
                turn(j, True)
            keep_h2(TURNS - 1)
            sp.wait_ge(s_eo, 1)
            sp.wait_ge(s_h2d, 16 * TURNS + 16)
            sp.wait_ge(s_h2k, TURNS)

            sp.dma_start(gu_sb[:, :, :], gu_t.rearrange("(c p) n -> p c n", p=P)).then_inc(s_ws, 16)
            sp.dma_start(down_sb[:, 0:2, :], down_t[0:2 * P].rearrange("(c p) n -> p c n", p=P)).then_inc(s_ws, 16)
            sp.dma_start(down_sb[0:SHARED - 2 * P, 2, :], down_t[2 * P:SHARED]).then_inc(s_ws, 16)

            sp.dma_start(gate_row[:, :, :], rows_dram[:, 3 * E:4 * E].unsqueeze(0).broadcast_to([P, B, E]))\
                .then_inc(s_gr, 16)

            def load(tile, rnd, slot):
                e = sp.value_load(e_of[0:1, bass.ds(tile, 1)] if rnd is not None else e_of[0:1, tile:tile + 1],
                                  min_val=0, max_val=NEXP - 1)
                if rnd is not None:
                    then(sp, s_m1, tile - RING + 1)
                sp.dma_start(w1b[:, slot, :, :], w1_t[bass.ds(e, 1)].rearrange("a (c p) i -> p (a c) i", p=P))\
                    .then_inc(s_w1[slot], 16)
                if rnd is not None:
                    then(sp, s_parts, tile - RING + 1)
                sp.dma_start(w2b[:, slot, :, :], w2_t[bass.ds(e, 1)].rearrange("a (c p) h -> p (a c) h", p=IP))\
                    .then_inc(s_w2[slot], 16)

            for slot in range(RING):
                load(slot, None, slot)
            with sp.Fori(1, SLOT_TILES // RING) as r:
                for slot in range(RING):
                    load(r * RING + slot, r, slot)
            with sp.Fori(0, TILES // 2) as r:
                for b in range(2):
                    then(sp, s_final, 2 * r + b + 1)
                    sp.dma_start(out[bass.ds((2 * r + b) * P, P), :], acc[:, b, :]).then_inc(s_out[b], 16)
            for b in range(2):
                sp.wait_ge(s_out[b], 16 * (TILES // 2))

        @block.tensor
        def _(pe):
            mm = nc.tensor.matmul

            pe.wait_ge(s_silu, 1)
            pe.wait_ge(s_wm, 16)
            for kind in range(2):
                for c in range(EC):
                    at = (kind * EC + c) * B
                    for k in range(EC):
                        last = mm(PS[:, 0, at:at + B], wmod_sb[:, k, kind * E + c * P:kind * E + (c + 1) * P],
                                  silu_c[:, k, :], start=(k == 0), stop=(k == EC - 1))
            last.then_inc(s_modp, 1)
            pe.wait_ge(s_modc, 1)
            pe.wait_ge(s_cst, 16)

            def turn_normed(j):
                for t in range(TPG):
                    pe.wait_ge(s_xn, TPG * j + t + 1)
                    for c in range(EC):
                        last = nc.tensor.transpose(PS[:, t // 2, c * N + t % 2 * P:c * N + (t % 2 + 1) * P],
                                                   xn[:, t, c * P:(c + 1) * P], ident)
                    last.then_inc(s_xnT, 1)

            def finish(j, next_open):
                pe.wait_ge(s_h2, j + 1)
                if next_open:
                    pe.wait_ge(s_qsd, 4 * j + 8)
                for t in range(TPG):
                    for c in range(EC):
                        last = nc.tensor.transpose(PS[:, 6 + c, t * P:(t + 1) * P], h2[:, t, c * P:(c + 1) * P], ident)
                last.then_inc(s_h2t, 1)
                if next_open:
                    pe.wait_ge(s_fin, 4 * j + 5)
                pe.wait_ge(s_h2T, j + 1)
                for t in range(TPG):
                    for k in range(EC):
                        last = mm(PS[:, 4, t * NEXP:(t + 1) * NEXP], h2T[:, k, t * P:(t + 1) * P], gate_sb[:, k, :],
                                  start=(k == 0), stop=(k == EC - 1))
                last.then_inc(s_lgp, 1)

            def turn(j, last_open, more):
                def proj(u):
                    if u >= 2:
                        pe.wait_ge(s_rope, 4 * j + u - 1)
                    for k in range(EC):
                        last = mm(PS[:, 2 + u % 2, :], wqkv_sb[:, k, (u + 2) % 4 * P:((u + 2) % 4 + 1) * P], hT[:, k, :],
                                  start=(k == 0), stop=(k == EC - 1))
                    last.then_inc(s_proj, 1)

                def values(t):
                    for k in range(EC):
                        last = mm(PS[:, t // 2, (t % 2) * E:(t % 2 + 1) * E], hT[:, k, t * P:(t + 1) * P],
                                  wqkv_sb[:, k, 2 * E:3 * E], start=(k == 0), stop=(k == EC - 1))
                    last.then_inc(s_v, 1)

                def centre(u):
                    pe.wait_ge(s_rope, 4 * j + u + 1)
                    if u < 2 and last_open:
                        pe.wait_ge(s_gated, 2 * j - 1 + u)
                    mm(PS[:, centred_in(u), :], C("centre"), rc[:, u % 2, :], start=True, stop=False)
                    mm(PS[:, centred_in(u), :], C("centre_swap"), rs[:, u % 2, :], start=False, stop=True)\
                        .then_inc(s_cent, 1)

                def variance(u):
                    pe.wait_ge(s_sq, 4 * j + u + 1)
                    if u < 2:
                        for t in range(TPG):
                            last = mm(PS[:, 6 + u, t * HB:(t + 1) * HB], sq[:, u, t * P:(t + 1) * P],
                                      C("var")[:, 0:P:D], start=True, stop=True)
                        last.then_inc(s_var, 1)
                    else:
                        pe.wait_ge(s_fin, 4 * j + u - 1)
                        mm(PS[:, 6 + u % 2, :], C("var"), sq[:, u % 2, :], start=True, stop=True).then_inc(s_var, 1)

                def widen(u):
                    pe.wait_ge(s_rec, 2 * j + u + 1)
                    for t in range(TPG):
                        last = mm(PS[:, 6 + u, t * P:(t + 1) * P],
                                  k_rec_wide[:, u, t * P:(t + 1) * P], ident,
                                  start=True, stop=True)
                    last.then_inc(s_wide, 1)

                pe.wait_ge(s_hT, 4 * j + 4)
                proj(0)
                proj(1)
                centre(0)
                proj(2)
                variance(0)
                centre(1)
                proj(3)
                widen(0)
                variance(1)
                centre(2)
                widen(1)
                variance(2)
                centre(3)
                variance(3)
                for t in range(TPG):
                    values(t)
                if last_open:
                    finish(j - 1, True)
                else:
                    pe.wait_ge(s_wr, 16)
                    pe.wait_ge(s_qsd, 4)
                    for half in range(2):
                        for k in range(EC):
                            last = mm(PS[0:B, 6 + half, :], silu_c[:, k, :],
                                      wmod_sb[:, k, (2 + 2 * half) * E:(4 + 2 * half) * E],
                                      start=(k == 0), stop=(k == EC - 1))
                    last.then_inc(s_rowp, 1)
                    pe.wait_ge(s_wo, 16 * 3)

                def scores(n):
                    bb, i, f = unit(n)
                    if bb == 0 and f == 0:
                        pe.wait_ge(s_kst[i], 16 * (4 if i == 0 else 6) * (j + 1))
                        pe.wait_ge(s_qst[i], 16 * (4 if i == 0 else 6) * (j + 1))
                        if i == 0:
                            pe.wait_ge(s_first, 16 * 4 * (j + 1))
                    if n >= 2:
                        pe.wait_ge(s_s2, UNITS * j + n - 1)
                    at = bb * N
                    for r in range(2):
                        bank = PS[:, 2 * (n % 2) + r, :]
                        for key in range(2):
                            first = at + key * P
                            o = bank[:, P:2 * P] if key else bank.rearrange("p (a n) -> p a n", a=2)[:, :, 0:P]
                            last = mm(o, k_stack[:, i % K_RING, r, f, first:first + P], q_stack[:, i, f, first:at + N],
                                      start=True, stop=True)
                    last.then_inc(s_sc, 1)

                def attend(n):
                    bb, i, f = unit(n)
                    pe.wait_ge(s_lo, UNITS * j + n + 1)
                    pe.wait_ge(s_off, UNITS * j + n + 1)
                    if n >= 2:
                        pe.wait_ge(s_avc, UNITS * j + n - 1)
                    if n in (0, 2):
                        pe.wait_ge(s_va, 2 * j + 1 + n // 2)
                    if n == 0 and last_open:
                        pe.wait_ge(s_lg, j)
                        pe.wait_ge(s_h2k, j)
                    if n == 0 and not last_open:
                        pe.wait_ge(s_rowr, 1)
                    for r in range(2):
                        v0, v1 = (va[:, 2 * bb + m, 8 * f + i + 4 * r, :, :].rearrange("p a d -> p (a d)")
                                  for m in range(2))
                        o = PS[0:2 * (D + 1), 4 + n % 2, r * N:(r + 1) * N]
                        hi, lo = (a[:, n % A_RING, r, :] for a in (a_hi, a_lo))

                        def all_queries(a):
                            return bass.AP(a.tensor, a.offset, [list(a.ap[0]), [2 * P, 2], [1, P]])

                        mm(o, v0, all_queries(hi), start=True, stop=False)
                        mm(o[:, P:2 * P], v1, hi[:, P:2 * P], start=False, stop=False)
                        mm(o[:, P:2 * P], v1, lo[:, P:2 * P], start=False, stop=False)
                        last = mm(o, v0, all_queries(lo), start=False, stop=True)
                    last.then_inc(s_av, 1)

                def turn_back(n):
                    f = n % 2
                    then(pe, s_avc, UNITS * j + n + 1)
                    if n % 2 == 0 and n >= 4:
                        then(pe, s_av4, 8 * j + n // 2 - 1)
                    o = PS[:, 6 + n // 2 % 2, 0:2 * 4 * 2 * (D + 1)].rearrange("p (t h d) -> p t h d", t=2, h=4)
                    for r in range(2):
                        for t in range(2):
                            last = nc.tensor.transpose(o[:, t, 2 * f + r, :], rows_av[:, n % 2, r, t * P:(t + 1) * P],
                                                       C("ident", 2 * (D + 1))[:, 0:2 * (D + 1)])
                    last.then_inc(s_back, 1)

                pe.wait_ge(s_vh, 2 * j + 2)
                for n in range(UNITS + 4):
                    if n < UNITS:
                        scores(n)
                    if 3 <= n < UNITS + 3:
                        attend(n - 3)
                    if n >= 4:
                        turn_back(n - 4)

                for t in range(TPG):
                    if t % 2 == 0:
                        pe.wait_ge(s_on, 8 * j + 7 + t // 2)
                    if t >= 2:
                        pe.wait_ge(s_oT, 4 * j + t - 1)
                    for c in range(EC):
                        last = nc.tensor.transpose(PS[:, t % 2, c * P:(c + 1) * P], o_sb[:, t, c * P:(c + 1) * P], ident)
                    last.then_inc(s_ot, 1)
                    if t >= 1:
                        project_out(pe, t - 1, j)
                project_out(pe, TPG - 1, j)
                if more:
                    pe.wait_ge(s_oT, 4 * j + 4)
                    turn_normed(j + 1)

            turn_normed(0)
            pe.wait_ge(s_w, 16 * 2)
            turn(0, False, True)
            with pe.Fori(1, TURNS - 1) as j:
                turn(j, True, True)
            turn(TURNS - 1, True, False)
            finish(TURNS - 1, False)

            pe.wait_ge(s_mask, 1)
            mm(PS[0:NEXP, 0, 0:1], cum[:, TILES * NEXP:(TILES + 1) * NEXP], H("ones")[:, 0:1], start=True, stop=True)\
                .then_inc(s_n, 1)
            pe.wait_ge(s_t, 1)
            for half in range(2):
                tt = slice(8 * half * NEXP, (8 * half + 8) * NEXP)
                o = PS[:, 1 + half, :]
                mm(o, H("before"), mask[:, tt], start=True, stop=False)
                mm(o, H("ones"), cum[:, tt], start=False, stop=False)
                last = mm(o, t_wide[:, :], H("exp_before", NEXP).unsqueeze(1).broadcast_to([NEXP, 8, NEXP]),
                          start=False, stop=True)
            last.then_inc(s_pos, 1)
            mm(PS[0:NEXP, 3, 0:1], H("exp_upto", NEXP), t_col16[:, :], start=True, stop=True).then_inc(s_end, 1)
            pe.wait_ge(s_ec, 1)
            mm(PS[0:1, 4, 0:SLOT_TILES], H("ones", NEXP)[:, 0:1], e_cmp[:, :], start=True, stop=True).then_inc(s_e, 1)

            def collect(n, b, first=False, final=False):
                pe.wait_ge(s_hot, n + 1)
                pe.wait_ge(s_ahot, n + 1)
                pe.wait_ge(s_phot, n + 1)
                for k in range(TOPK):
                    last = mm(PS[:, 3, 0:SLOT_TILES], hot_s[:, b, k, :], hot_g[:, b, k, :],
                              start=(first and k == 0), stop=(final and k == TOPK - 1))
                last.then_inc(s_hotm, 1)

            collect(0, 0, first=True)
            collect(1, 1)
            with pe.Fori(1, TILES // 2 - 1) as r:
                for b in range(2):
                    collect(2 * r + b, b)
            collect(TILES - 2, 0)
            collect(TILES - 1, 1, final=True)

            def turn(tile, rnd, slot):
                pe.wait_ge(s_xg[slot], 16 * (rnd + 1))
                b = slot % 2
                for c in range(EC):
                    last = nc.tensor.transpose(PS[:, b, c * P:(c + 1) * P], xg[:, slot, c * P:(c + 1) * P], ident)
                last.then_inc(s_xt, 1)

            def inner(tile, rnd, slot):
                b = slot % 2
                pe.wait_ge(s_xT, tile + 1)
                pe.wait_ge(s_w1[slot], 16 * (rnd + 1))
                for i in range(IC):
                    for c in range(EC):
                        last = mm(PS[0:IP, 4 + b, i * P:(i + 1) * P], w1b[:, slot, c, i * IP:(i + 1) * IP],
                                  xgT[:, b, c, :], start=(c == 0), stop=(c == EC - 1))
                last.then_inc(s_m1, 1)

            def outer(tile, slot, first=False):
                b = slot % 2
                pe.wait_ge(s_parts, tile + 1)
                if not first:
                    pe.wait_ge(s_yb, tile - 1)
                products = [(h[:, slot, i, :], w[:, slot, i, :]) for i in range(IC)
                            for h, w in ((hx_hi, w2_hi), (hx_lo, w2_hi), (hx_hi, w2_lo))]
                for n, (h, w) in enumerate(products):
                    last = mm(PS[:, 6 + b, 0:E], h, w, start=(n == 0), stop=(n == len(products) - 1))
                last.then_inc(s_m2, 1)

            def step(g, q, r, **kw):
                turn(g + 1, q + (r + 1) // RING, (r + 1) % RING)
                inner(g, q + r // RING, r % RING)
                outer(g - 2, (r - 2) % RING, **kw)

            turn(0, 0, 0)
            turn(1, 0, 1)
            inner(0, 0, 0)
            turn(2, 0, 2)
            inner(1, 0, 1)
            step(2, 0, 2, first=True)
            step(3, 0, 3, first=True)
            LOOPS = SLOT_TILES // RING - 1
            with pe.Fori(1, LOOPS) as q:
                for r in range(RING):
                    step(RING * q + r, q, r)
            g = RING * LOOPS
            for r in range(RING - 1):
                step(g + r, LOOPS, r)
            inner(g + 3, LOOPS, 3)
            for t in (g + 1, g + 2, g + 3):
                outer(t, t % RING)

            pe.wait_ge(s_ws, 16 * 3)
            pe.wait_ge(s_h2k, TURNS)
            pe.wait_ge(s_yb, SLOT_TILES)

            def shared(j, first=False):
                for i, (c0, cn_) in enumerate(SH_CHUNKS):
                    n = 3 * j + i
                    if i >= 2 or not first:
                        pe.wait_ge(s_sa, n - 1)
                    for which in range(2):
                        w0 = which * SHARED + c0
                        for k in range(EC):
                            last = mm(PS[0:cn_, 2 * (i % 2) + which, :], gu_sb[:, k, w0:w0 + cn_],
                                      h2T_all[:, k, bass.ds(j * GROUP, GROUP)], start=(k == 0), stop=(k == EC - 1))
                    last.then_inc(s_gp, 1)
                pe.wait_ge(s_sa, 3 * j + 3)
                for t in range(TPG):
                    if not first:
                        pe.wait_ge(s_acc, 4 * j + t - 3)
                    for i, (c0, cn_) in enumerate(SH_CHUNKS):
                        last = mm(PS[:, 4 + t, 0:E], sact[0:cn_, i, t * P:(t + 1) * P], down_sb[0:cn_, i, :],
                                  start=(i == 0), stop=(i == len(SH_CHUNKS) - 1))
                    last.then_inc(s_sp, 1)

            shared(0, first=True)
            with pe.Fori(1, TURNS) as j:
                shared(j)

        @block.scalar
        def _(act):
            a = nc.scalar.activation
            act.wait_ge(s_c, 16)
            a(silu_c[:, :, :], cT[:, :, :], ACT.Silu).then_inc(s_silu, 1)
            act.wait_ge(s_cst, 16)
            eps = C("eps")

            def first_norm(j):
                act.wait_ge(s_mv, j + 1)
                a(sd[:, :], mv[:, :, 1], ACT.Sqrt, bias=eps).then_inc(s_sd, 1)
                act.wait_ge(s_now, j + 1)
                for bb in range(BPG):
                    act.wait_ge(s_xnT, 4 * j + 2 * bb + 2)
                    for c in range(EC):
                        a(hT[:, c, bb * N:(bb + 1) * N], PS[:, bb, c * N:(c + 1) * N], ACT.Identity,
                          bias=mod_now[:, 0, c, bb:bb + 1], scale=mod_now[:, 1, c, bb:bb + 1]).then_inc(s_hT, 1)

            def second_deviation(j):
                act.wait_ge(s_mv2, j + 1)
                a(sd2[:, :], mv2[:, :, 1], ACT.Sqrt, bias=eps).then_inc(s_sd2, 1)

            def finish(j, copy_v=None):
                act.wait_ge(s_h2t, j + 1)
                a(h2T[:, :, :], PS[:, 6:8, :], ACT.Copy).then_inc(s_h2T, 1)
                if copy_v:
                    copy_v(0)
                    copy_v(1)
                act.wait_ge(s_lgp, j + 1)
                a(lg[:, bass.ds(j * TPG * NEXP, TPG * NEXP)], PS[:, 4, 0:TPG * NEXP], ACT.Copy).then_inc(s_lg, 1)

            def keep(j):
                a(h2T_all[:, :, bass.ds(j * GROUP, GROUP)], PS[:, 6:8, :], ACT.Copy).then_inc(s_h2k, 1)

            def turn(j, last_open, more):
                def squares(u):
                    act.wait_ge(s_cent, 4 * j + u + 1)
                    if u >= 2:
                        act.wait_ge(s_var, 4 * j + u - 1)
                    a(sq[:, u % 2, :], PS[:, centred_in(u), :], ACT.Square).then_inc(s_sq, 1)
                    if u < 2:
                        a(kk[:, u, :], PS[:, 4 + u, :], ACT.Identity).then_inc(s_centk, 1)

                def deviation(u):
                    act.wait_ge(s_var, 4 * j + u + 1)
                    if u == 2 and last_open:
                        act.wait_ge(s_res, j)
                    if u < 2:
                        a(k_dev[:, u, :], PS[:, 6 + u, 0:TPG * HB], ACT.Sqrt, bias=eps).then_inc(s_qsd, 1)
                    else:
                        a(q_dev[:, u - 2, :], PS[:, 6 + u % 2, :], ACT.Sqrt, bias=eps).then_inc(s_qsd, 1)

                def q_scale(u):
                    a(scaled[u - 2], PS[:, centred_in(u), :], ACT.Identity, scale=ln_col[:, 0:1])\
                        .then_inc(s_scale, 1)

                def q_high(u):
                    act.wait_ge(s_fin, 4 * j + u + 1)
                    a(q_hi[:, u - 2, :], q_sum[:, u - 2, :], ACT.Identity).then_inc(s_qh, 1)

                def k_high(f):
                    act.wait_ge(s_kk, 2 * j + f + 1)
                    a(k_hi[:, f, :], kk[:, f, :], ACT.Identity).then_inc(s_kh, 1)

                def copy_v(i):
                    act.wait_ge(s_v, 4 * j + 2 * i + 2)
                    hd = "p t h d -> p (t h) d"
                    ps = PS[:, i, :].rearrange("p (h d) -> p h d", d=D)
                    a(v_sb[:, 2 * i:2 * i + 2, :, :].rearrange(hd), ps, ACT.Identity)
                    a(va[:, 2 * i:2 * i + 2, :, 0, 0:D].rearrange(hd), ps, ACT.Identity).then_inc(s_vh, 1)

                if last_open:
                    second_deviation(j - 1)
                else:
                    act.wait_ge(s_w, 16 * 2)
                squares(0)
                deviation(0)
                squares(1)
                deviation(1)
                squares(2)
                k_high(0)
                deviation(2)
                q_scale(2)
                squares(3)
                q_scale(3)
                k_high(1)
                q_high(2)
                deviation(3)
                q_high(3)
                if last_open:
                    finish(j - 1, copy_v)
                else:
                    copy_v(0)
                    copy_v(1)
                    act.wait_ge(s_rowp, 1)
                    a(rows[:, :, :].rearrange("b (i k) f -> b i (k f)", i=2), PS[0:B, 6:8, :], ACT.Copy)\
                        .then_inc(s_rowr, 1)

                def high(n):
                    act.wait_ge(s_s4, UNITS * j + n + 1)
                    if n >= A_RING:
                        act.wait_ge(s_av, UNITS * j + n - A_RING + 1)
                    a(a_hi[:, n % A_RING, :, :], s2[:, n % S_RING, :, :], ACT.Identity).then_inc(s_hi, 1)

                def square(n):
                    act.wait_ge(s_sc, UNITS * j + n + 1)
                    if n >= S_RING:
                        act.wait_ge(s_lo, UNITS * j + n - S_RING + 1)
                        act.wait_ge(s_off, UNITS * j + n - S_RING + 1)
                    a(s2[:, n % S_RING, :, :], PS[:, 2 * (n % 2):2 * (n % 2) + 2, 0:384], ACT.Square).then_inc(s_s2, 1)

                def copy_attended(n):
                    act.wait_ge(s_av, UNITS * j + n + 1)
                    if n >= 2:
                        act.wait_ge(s_back, UNITS * j + n - 1)
                    a(rows_av[:, n % 2, :, :].rearrange("p r n -> p (r n)"), PS[0:2 * (D + 1), 4 + n % 2, :], ACT.Copy)\
                        .then_inc(s_avc, 1)

                for n in range(UNITS + 3):
                    if n < UNITS:
                        square(n)
                    if 1 <= n < UNITS + 1:
                        high(n - 1)
                    if n == 1 and last_open:
                        keep(j - 1)
                    if n >= 3:
                        copy_attended(n - 3)

                for t in range(TPG):
                    act.wait_ge(s_ot, 4 * j + t + 1)
                    if t >= 2:
                        act.wait_ge(s_ao, 4 * j + t - 1)
                    a(oT[:, t % 2, :, :].rearrange("p c n -> p (c n)"), PS[:, t % 2, 0:E], ACT.Copy).then_inc(s_oT, 1)
                if more:
                    first_norm(j + 1)

            first_norm(0)
            turn(0, False, True)
            with act.Fori(1, TURNS - 1) as j:
                turn(j, True, True)
            turn(TURNS - 1, True, False)
            second_deviation(TURNS - 1)
            finish(TURNS - 1)
            keep(TURNS - 1)

            act.wait_ge(s_ls, 1)
            a(lg[:, :], lg[:, :], ACT.Exp).then_inc(s_ex, 1)

            act.wait_ge(s_cols, 1)

            def one_hots(i, b, first=False):
                if not first:
                    act.wait_ge(s_ahot, i - 1)
                for k in range(SCALAR_HOTS):
                    ins = a(apart[:, b, k, :], H("slots"), ACT.Square, scale=-1.0, bias=col_s[:, bass.ds(8 * i + k, 1)])
                ins.then_inc(s_apart, 1)
                act.wait_ge(s_apart, i + 1)
                if not first:
                    act.wait_ge(s_hotm, i - 1)
                a(hot_s[:, b, 0:SCALAR_HOTS, :], apart[:, b, :, :], ACT.Relu, scale=-2.0, bias=C("one"))\
                    .then_inc(s_ahot, 1)

            one_hots(0, 0, first=True)
            one_hots(1, 1, first=True)
            with act.Fori(1, TILES // 2) as r:
                for b in range(2):
                    one_hots(2 * r + b, b)

            def highs(tile, rnd, slot, first=False):
                b = slot % 2
                act.wait_ge(s_w2[slot], 16 * (rnd + 1))
                a(w2_hi[:, slot, :, :], w2b[:, slot, :, :], ACT.Identity).then_inc(s_w2h, 1)
                act.wait_ge(s_m1, tile + 1)
                if not first:
                    act.wait_ge(s_parts, tile - 1)
                a(hx[:, b, :, :].rearrange("p i n -> p (i n)"), PS[0:IP, 4 + b, 0:IC * P], ACT.Silu).then_inc(s_hx, 1)
                act.wait_ge(s_hx, tile + 1)
                a(hx_hi[:, slot, :, :], hx[:, b, :, :], ACT.Identity).then_inc(s_hxh, 1)

            def store(tile, slot):
                act.wait_ge(s_yb, tile + 1)
                act.dma_start(y_dram[bass.ds(tile * P, P), :], yb[:, slot, :]).then_inc(s_yd[slot], 16)

            for g in range(RING):
                highs(g, 0, g, first=g < 2)
            store(0, 0)
            with act.Fori(1, SLOT_TILES // RING) as q:
                for r in range(RING):
                    highs(RING * q + r, q, r)
                    store(RING * q + r - 3, (r - 3) % RING)
            for t in range(SLOT_TILES - 3, SLOT_TILES):
                store(t, t % RING)
            for slot in range(RING):
                act.wait_ge(s_yd[slot], 16 * (SLOT_TILES // RING))
            act.sem_inc(s_ystored, 1)

            def shared(j, first=False):
                for i, (c0, cn_) in enumerate(SH_CHUNKS):
                    n = 3 * j + i
                    act.wait_ge(s_gp, n + 1)
                    if i >= 2 or not first:
                        act.wait_ge(s_sa, n - 1)
                    a(sg[0:cn_, i % 2, :], PS[0:cn_, 2 * (i % 2), :], ACT.Silu).then_inc(s_sg, 1)

            shared(0, first=True)
            with act.Fori(1, TURNS) as j:
                shared(j)

        @block.vector
        def _(dve):
            v = nc.vector
            steps = [0]

            def link(ins):
                steps[0] += 1
                ins.then_inc(s_chain, 1)
                dve.wait_ge(s_chain, steps[0])

            dve.sem_inc(s_h2d, 16)
            dve.wait_ge(s_modp, 1)
            both = PS[:, 0, 0:2 * EC * B]
            v.tensor_copy(mod_col[:, 0, :, :].rearrange("p c b -> p (c b)"), both[:, 0:EC * B])
            v.tensor_scalar(mod_col[:, 1, :, :].rearrange("p c b -> p (c b)"), both[:, EC * B:2 * EC * B], 1.0, None,
                            ALU.add).then_inc(s_modc, 1)
            v.memset(va[:, :, :, 0, D:D + 1].bitcast(F32).rearrange("p t h d -> p (t h) d"), 1.0)
            v.memset(va[:, :, :, 1, D:D + 1].bitcast(F32).rearrange("p t h d -> p (t h) d"), 0.0).then_inc(s_set, 1)

            v.memset(cum[:, 0:NEXP], 0.0)
            v.memset(lmax[:, :, NEXP:NEXP + 1], 8.0)
            link(v.memset(lmax[:, :, NEXP + 1:NEXP + 2], 9.0))

            PER = 24
            total = [0]
            base = [0]

            def step(ins, apart=False):
                total[0] += 1
                ins.then_inc(s_turn, 1)
                if apart:
                    then(dve, s_turn, base[0] + total[0])
                else:
                    dve.wait_ge(s_turn, base[0] + total[0])

            def moments(j, stats, out_):
                for t in range(TPG):
                    ins = v.bn_stats(stats[:, t, :], x_all[:, bass.ds((TPG * j + t) * E, E)])
                step(ins, apart=True)
                for t in range(TPG):
                    ins = v.bn_aggr(out_[:, t, :], stats[:, t, :])
                return ins

            def first_norm(j):
                moments(j, st, mv).then_inc(s_mv, 1)
                v.tensor_copy(mod_now[:, :, :, :].rearrange("p k c b -> p (k c) b"),
                              mod_col[:, :, :, :].rearrange("p k c b -> p (k c) b")[:, :, bass.ds(BPG * j, BPG)])\
                    .then_inc(s_now, 1)
                dve.wait_ge(s_sd, j + 1)
                step(v.reciprocal(rstd[:, :], sd[:, :]))
                for t in range(TPG):
                    v.tensor_scalar(xn[:, t, :], x_all[:, bass.ds((TPG * j + t) * E, E)], mv[:, t, 0:1],
                                    rstd[:, t:t + 1], ALU.subtract, ALU.mult).then_inc(s_xn, 1)

            def row(bb, kind):
                return mod_row[:, bb, kind * E:(kind + 1) * E].unsqueeze(1).broadcast_to([P, 2, E])

            def tiles(ap):
                return ap.rearrange("p (t f) -> p t f", f=E)

            def gate_attention(j):
                dve.wait_ge(s_ao, 4 * j + 4)
                dve.wait_ge(s_bc, 16 * j + 16)
                for bb in range(BPG):
                    ins = v.tensor_tensor(tiles(gated[:, bb, :]), tiles(PS[:, 4 + bb, :]), row(bb, 0), ALU.mult)
                    ins.then_inc(s_gated, 1)

            def second_moments(j):
                then(dve, s_res, j + 1)
                moments(j, st2, mv2).then_inc(s_mv2, 1)

            def second_norm(j):
                dve.wait_ge(s_sd2, j + 1)
                step(v.reciprocal(rstd2[:, :], sd2[:, :]))
                dve.wait_ge(s_h2d, 16 * j + 16)
                for t in range(TPG):
                    ins = v.tensor_scalar(h2[:, t, :], x_all[:, bass.ds((TPG * j + t) * E, E)], mv2[:, t, 0:1],
                                          rstd2[:, t:t + 1], ALU.subtract, ALU.mult)
                ins.then_inc(s_h2n, 1)

            def route(j, part):
                group = bass.ds(j * TPG, TPG)
                logits = lg[:, bass.ds(j * TPG * NEXP, TPG * NEXP)].rearrange("p (t e) -> p t e", e=NEXP)
                chose = mask[:, bass.ds(j * TPG * NEXP, TPG * NEXP)].rearrange("p (t e) -> p t e", e=NEXP)
                if part == 0:
                    dve.wait_ge(s_lg, j + 1)
                    step(v.tensor_reduce(mx[:, group], logits, AX_X, ALU.max))
                    step(v.tensor_tensor(lmax[:, :, 0:NEXP], logits,
                                         mx[:, group].unsqueeze(2).broadcast_to([P, TPG, NEXP]), ALU.subtract),
                         apart=True)
                elif part == 1:
                    for t in range(TPG):
                        ins = v.max(top8[:, t, :], lmax[:, t, 0:NEXP])
                    step(ins)
                    v.memset(top8[:, :, TOPK:TOPK + 1], 8.0)
                    step(v.memset(top8[:, :, TOPK + 1:8], 9.0), apart=True)
                elif part == 2:
                    for t in range(TPG):
                        ins = v.match_replace(rest[:, t, :], top8[:, t, :], lmax[:, t, :], 1.0)
                    step(ins)
                    step(v.tensor_scalar(chose, rest[:, :, 0:NEXP], 1.0, None, ALU.is_equal))
                else:
                    for t in range(TPG):
                        at, to = (bass.ds((TPG * j + n) * NEXP, NEXP) for n in (t, t + 1))
                        step(v.tensor_tensor(cum[:, to], cum[:, at], mask[:, at], ALU.add))

            def modulation_rows():
                dve.wait_ge(s_rowr, 1)
                gates = rows[:, 0:4:3, :]
                v.tensor_scalar(rows[:, 2, :], rows[:, 2, :], 1.0, None, ALU.add)
                v.tensor_scalar(gate_size[:, :, :], gates, -1.0, None, ALU.mult)
                link(v.tensor_scalar(gate_sign[:, :, :], gates, 0.0, 2.0, ALU.is_ge, ALU.mult))
                link(v.tensor_tensor(gate_size[:, :, :], gates, gate_size[:, :, :], ALU.max))
                v.tensor_scalar(gate_size[:, :, :], gate_size[:, :, :], 0.25, None, ALU.max)
                link(v.tensor_scalar(gate_sign[:, :, :], gate_sign[:, :, :], -1.0, None, ALU.add))
                v.tensor_tensor(gates, gate_sign[:, :, :], gate_size[:, :, :], ALU.mult).then_inc(s_rows, 1)

            def turn(j, last_open, more):
                cos = C("cos").unsqueeze(1).broadcast_to([P, BPG, N])
                sin = C("sin").unsqueeze(1).broadcast_to([P, BPG, N])

                def two(ap):
                    return ap.rearrange("p (b n) -> p b n", b=BPG)

                def rope(u):
                    dve.wait_ge(s_proj, 4 * j + u + 1)
                    if u >= 2:
                        dve.wait_ge(s_cent, 4 * j + u - 1)
                    v.tensor_tensor(two(rc[:, u % 2, :]), two(PS[:, 2 + u % 2, :]), cos, ALU.mult)
                    v.tensor_tensor(two(rs[:, u % 2, :]), two(PS[:, 2 + u % 2, :]), sin, ALU.mult).then_inc(s_rope, 1)

                def q_shift(u):
                    dve.wait_ge(s_scale, 2 * j + u - 1)
                    dve.wait_ge(s_qsd, 4 * j + u + 1)
                    v.scalar_tensor_tensor(out=q_sum[:, u - 2, :], in0=q_dev[:, u - 2, :], scalar=ln_col[:, 1:2],
                                           in1=scaled[u - 2], op0=ALU.mult, op1=ALU.add).then_inc(s_fin, 1)

                def q_low(u):
                    dve.wait_ge(s_qh, 2 * j + u - 1)
                    v.tensor_tensor(q_lo[:, u - 2, :], q_sum[:, u - 2, :], q_hi[:, u - 2, :].bitcast(F32), ALU.subtract)\
                        .then_inc(s_ql, 1)

                def k_reciprocal(u):
                    dve.wait_ge(s_qsd, 4 * j + u + 1)
                    step(v.reciprocal(k_rec[:, u, :], k_dev[:, u, :]))
                    v.tensor_copy(k_rec_wide[:, u, :].rearrange("p (h d) -> p h d", d=D),
                                  k_rec[:, u, :].unsqueeze(2).broadcast_to([P, TPG * HB, D])).then_inc(s_rec, 1)

                def k_norm(u):
                    dve.wait_ge(s_centk, 2 * j + u + 1)
                    dve.wait_ge(s_wide, 2 * j + u + 1)
                    v.tensor_tensor(kk[:, u, :], PS[:, 6 + u, :], kk[:, u, :], ALU.mult).then_inc(s_fin, 1)

                if last_open:
                    gate_attention(j - 1)
                rope(0)
                if last_open:
                    second_moments(j - 1)
                rope(1)
                if last_open:
                    second_norm(j - 1)
                rope(2)
                k_reciprocal(0)
                rope(3)
                k_norm(0)
                k_reciprocal(1)
                k_norm(1)
                q_shift(2)
                dve.wait_ge(s_kh, 2 * j + 2)
                split_k(v, 1)
                q_low(2)
                q_shift(3)
                q_low(3)
                if not last_open:
                    modulation_rows()

                def low(n):
                    dve.wait_ge(s_hi, UNITS * j + n + 1)
                    lows_of(v, n, slice(0, 2 * P)).then_inc(s_lo, 1)

                for n in range(UNITS):
                    dve.wait_ge(s_msk, UNITS * j + n + 1)
                    m = s2[:, n % S_RING, :, :].rearrange("p r n -> p (r n)")
                    v.tensor_tensor(m, m, m, ALU.mult).then_inc(s_s4, 1)
                    if n >= 1:
                        low(n - 1)
                    if last_open and 1 <= n <= ROUTE_PARTS:
                        route(j - 1, n - 1)
                    if n % 2 == 0 and n >= 6:
                        heads_norm(dve, j, n // 2 - 3, step)
                low(UNITS - 1)
                for idx in range(UNITS // 2 - 3, UNITS // 2):
                    heads_norm(dve, j, idx, step)
                if more:
                    first_norm(j + 1)

            dve.wait_ge(s_x, 16)
            first_norm(0)
            dve.wait_ge(s_cst, 16)
            dve.wait_ge(s_w, 16 * 2)
            dve.wait_ge(s_xr, 16)
            turn(0, False, True)
            start, total[0] = total[0], 0
            with dve.Fori(1, TURNS - 1) as j:
                base[0] = j * PER + (start - PER)
                turn(j, True, True)
                assert total[0] == PER, total[0]
            base[0] = start + (TURNS - 2) * PER
            total[0] = 0
            turn(TURNS - 1, True, False)
            gate_attention(TURNS - 1)
            add_residual(dve, v, TURNS - 1)
            second_moments(TURNS - 1)
            second_norm(TURNS - 1)
            second_shift(dve, v, TURNS - 1)

            dve.wait_ge(s_wo, 16 * 3)
            for part in range(ROUTE_PARTS):
                route(TURNS - 1, part)
            dve.sem_inc(s_mask, 1)
            dve.wait_ge(s_h2k, TURNS)
            wide = [P, TILES, NEXP]
            dve.wait_ge(s_n, 1)
            link(v.tensor_copy(n_col[:, :], PS[0:NEXP, 0, 0:1]))
            link(v.tensor_scalar(n_cmp[:, :], C("steps", NEXP), n_col[:, 0:1], None, ALU.is_lt))
            link(v.tensor_reduce(t_col[:, :], n_cmp[:, :], AX_X, ALU.add))
            v.tensor_copy(t_col16[:, :], t_col[:, :])
            v.tensor_scalar(t_wide[:, :], H("ones", NEXP), t_col[:, 0:1], float(P), ALU.mult, ALU.mult)\
                .then_inc(s_t, 1)
            dve.wait_ge(s_end, 1)
            link(v.tensor_copy(e_end[:, :], PS[0:NEXP, 3, 0:1]))
            v.tensor_scalar(e_cmp[:, :], H("tiles", NEXP), e_end[:, 0:1], None, ALU.is_ge).then_inc(s_ec, 1)
            dve.wait_ge(s_e, 1)
            link(v.tensor_scalar(e_row[:, :], PS[0:1, 4, 0:SLOT_TILES], float(NEXP - 1), None, ALU.min))
            v.tensor_copy(e_of[:, :], e_row[:, :]).then_inc(s_eo, 1)
            dve.wait_ge(s_pos, 1)
            for half in range(2):
                tt = slice(8 * half, 8 * half + 8)
                te = slice(8 * half * NEXP, (8 * half + 8) * NEXP)
                ins = v.scalar_tensor_tensor(out=pos1[:, tt, :].rearrange("p t e -> p (t e)"), in0=PS[:, 1 + half, :],
                                             scalar=1.0, in1=mask[:, te],
                                             op0=ALU.add, op1=ALU.mult)
            link(ins)
            for i in range(TILES):
                ins = v.max(slot8[:, i, :], pos1[:, i, :])
            link(ins)
            v.tensor_scalar(slot_i[:, :], slot8[:, :, :].rearrange("p t k -> p (t k)"), -1.0, 0.0,
                            ALU.add, ALU.max).then_inc(s_slots, 1)
            dve.wait_ge(s_slots, 1)
            v.tensor_scalar(slot_g[:, :], slot_i[:, :], 7, None, ALU.arith_shift_right)
            link(v.tensor_scalar(slot_s[:, :], slot_i[:, :], P - 1, None, ALU.bitwise_and))
            v.tensor_copy(col_g[:, :], slot_g[:, :])
            link(v.tensor_copy(col_s[:, :], slot_s[:, :]))
            dve.sem_inc(s_cols, 1)
            t0 = CST["token"][0]

            def one_hots(i, b, first=False):
                if not first:
                    dve.wait_ge(s_hotm, i - 1)
                for k in range(SCALAR_HOTS, SCALAR_HOTS + VECTOR_HOTS):
                    v.tensor_scalar(hot_s[:, b, k, :], H("slots"), col_s[:, bass.ds(i * 8 + k, 1)], None, ALU.is_equal)
                for k in range(TOPK):
                    at = bass.ds(i * 8 + k, 1)
                    ins = v.tensor_scalar(hot_g[:, b, k, :], H("tiles"), col_g[:, at], cs[:, bass.ds(i + t0, 1)],
                                          ALU.is_equal, ALU.mult)
                ins.then_inc(s_hot, 1)

            one_hots(0, 0, first=True)
            one_hots(1, 1, first=True)
            with dve.Fori(1, TILES // 2) as r:
                for b in range(2):
                    one_hots(2 * r + b, b)
            dve.wait_ge(s_hotm, TILES)
            v.tensor_copy(tok_of[:, :], PS[:, 3, 0:SLOT_TILES]).then_inc(s_tok, 1)

            def copy_x(tile, slot, first=False):
                b = slot % 2
                dve.wait_ge(s_xt, tile + 1)
                if not first:
                    dve.wait_ge(s_m1, tile - 1)
                v.tensor_copy(xgT[:, b, :, :].rearrange("p c n -> p (c n)"), PS[:, b, 0:E]).then_inc(s_xT, 1)

            def copy_y(tile, rnd, slot, first=False):
                b = slot % 2
                dve.wait_ge(s_m2, tile + 1)
                if not first:
                    dve.wait_ge(s_yd[slot], 16 * rnd)
                v.tensor_copy(yb[:, slot, :], PS[:, 6 + b, 0:E]).then_inc(s_yb, 1)

            def share(step):
                if step == 1:
                    dve.wait_ge(s_ex, 1)
                    v.tensor_tensor(comb[:, :, :].rearrange("p t e -> p (t e)"), mask[:, :], lg[:, :], ALU.mult)\
                        .then_inc(s_share, 1)
                elif step == 2:
                    v.tensor_reduce(zs[:, :], comb[:, :, :], AX_X, ALU.add).then_inc(s_share, 1)
                elif step == 3:
                    v.reciprocal(mx[:, :], zs[:, :]).then_inc(s_share, 1)
                else:
                    v.tensor_tensor(comb[:, :, :], comb[:, :, :], mx[:, :].unsqueeze(2).broadcast_to(wide), ALU.mult)\
                        .then_inc(s_share, 1)

            def lows(tile, slot, between=None):
                dve.wait_ge(s_w2h, tile + 1)
                v.tensor_tensor(w2_lo[:, slot, :, :], w2b[:, slot, :, :], w2_hi[:, slot, :, :].bitcast(F32), ALU.subtract)
                if between is not None:
                    copy_y(*between)
                dve.wait_ge(s_hxh, tile + 1)
                v.tensor_tensor(hx_lo[:, slot, :, :], hx[:, slot % 2, :, :], hx_hi[:, slot, :, :].bitcast(F32),
                                ALU.subtract).then_inc(s_parts, 1)

            copy_x(0, 0, first=True)
            for g in range(RING + 2):
                copy_x(g + 1, (g + 1) % RING, first=g == 0)
                lows(g, g % RING, (g - 2, 0, g - 2, True) if g >= 2 else None)
                if g >= 3:
                    dve.wait_ge(s_share, g - 2)
                if g >= 2:
                    share(g - 1)
            with dve.Fori(1, SLOT_TILES // RING - 1) as q:
                for r in range(2, 2 + RING):
                    copy_x(RING * q + r + 1, (r + 1) % RING)
                    lows(RING * q + r, r % RING, (RING * q + r - 2, q, r - 2))
            LAST = SLOT_TILES // RING - 1
            copy_x(SLOT_TILES - 1, RING - 1)
            for r in (2, 3):
                lows(RING * LAST + r, r, (RING * LAST + r - 2, LAST, r - 2))
            dve.wait_ge(s_share, RING)
            for r in (2, 3):
                copy_y(RING * LAST + r, LAST, r)

            def gated_up(n, i, wait=None):
                dve.wait_ge(s_sg, n + 1)
                if wait is not None:
                    dve.wait_ge(s_sp, wait)
                v.tensor_tensor(sact[0:SH_CHUNKS[i][1], i, :], sg[0:SH_CHUNKS[i][1], i % 2, :],
                                PS[0:SH_CHUNKS[i][1], 2 * (i % 2) + 1, :], ALU.mult).then_inc(s_sa, 1)

            def weight(k):
                link(v.tensor_tensor(ex[:, :, :], pos1[:, :, :],
                                     slot8[:, :, k:k + 1].broadcast_to(wide), ALU.is_equal))
                link(v.tensor_tensor(ex[:, :, :], ex[:, :, :], comb[:, :, :], ALU.mult))
                link(v.tensor_reduce(wk[:, k, :], ex[:, :, :], AX_X, ALU.add))

            for k in range(TOPK):
                weight(k)
                if 1 <= k <= len(SH_CHUNKS):
                    gated_up(k - 1, k - 1)

            dve.wait_ge(s_gr, 16)
            gate_rows = gate_row[:, :, :].rearrange("p b f -> p (b f)")

            def combine(i, j, t, chain, first=False):
                b = t % 2
                rnd = 2 * j + t // 2
                dve.wait_ge(s_sp, i + 1)
                dve.wait_ge(s_yg[t], 16 * TOPK * (j + 1))
                if not first:
                    dve.wait_ge(s_out[b], 16 * rnd)
                for k in range(TOPK):
                    src = PS[:, 4 + t, 0:E] if k == 0 else acc[:, b, :]
                    ins = v.scalar_tensor_tensor(out=acc[:, b, :], in0=yg[:, t, k, :],
                                                 scalar=wk[:, k, bass.ds(i, 1)], in1=src,
                                                 op0=ALU.mult, op1=ALU.add)
                    if k < TOPK - 1:
                        chain(ins)
                ins.then_inc(s_acc, 1)
                dve.wait_ge(s_acc, i + 1)
                chain(v.tensor_tensor(acc[:, b, :], acc[:, b, :], gate_rows[:, bass.ds(rnd * E, E)], ALU.mult))
                v.tensor_tensor(acc[:, b, :], acc[:, b, :], x_all[:, bass.ds(i * E, E)], ALU.add)\
                    .then_inc(s_final, 1)

            def group(j, chain, first=False, more=True):
                for t in range(TPG):
                    combine(TPG * j + t, j, t, chain, first=first and t < 2)
                    if more and t < len(SH_CHUNKS):
                        gated_up(3 * j + 3 + t, t, wait=4 * j + 4 if t == 0 else None)

            group(0, link, first=True)
            before = steps[0]
            per = TPG * TOPK
            with dve.Fori(1, TURNS - 1) as j:
                count = [0]

                def linked(ins):
                    count[0] += 1
                    ins.then_inc(s_chain, 1)
                    dve.wait_ge(s_chain, j * per + before - per + count[0])

                group(j, linked)
                assert count[0] == per
            steps[0] = before + (TURNS - 2) * per
            group(TURNS - 1, link, more=False)

        @block.gpsimd
        def _(pool):
            g = nc.gpsimd
            g.memset(k_stack[:, :, :, :, :].bitcast(F32).rearrange("p s r f n -> p (s r f n)"), 0.0)
            g.memset(q_stack[:, :, :, :].bitcast(F32).rearrange("p i f n -> p (i f n)"), 0.0).then_inc(s_zero, 1)
            pool.wait_ge(s_zero, 1)
            pool.wait_ge(s_set, 1)

            def turn(j, last_open):
                if last_open:
                    add_residual(pool, g, j - 1)
                    second_shift(pool, g, j - 1)

                def v_low(f):
                    then(pool, s_vh, 2 * j + f + 1)
                    hd = "p t h d -> p (t h) d"
                    g.tensor_tensor(va[:, 2 * f:2 * f + 2, :, 1, 0:D].rearrange(hd),
                                    v_sb[:, 2 * f:2 * f + 2, :, :].rearrange(hd),
                                    va[:, 2 * f:2 * f + 2, :, 0, 0:D].bitcast(F32).rearrange(hd), ALU.subtract)\
                        .then_inc(s_va, 1)

                def k_low(f):
                    then(pool, s_fin, 4 * j + f + 1)
                    g.tensor_scalar(kk[:, f, :], kk[:, f, :], ln_col[:, 0:1], ln_col[:, 1:2], ALU.mult, ALU.add)\
                        .then_inc(s_kk, 1)
                    if f == 0:
                        then(pool, s_kh, 2 * j + 1)
                        split_k(g, 0)

                k_low(0)
                k_low(1)
                for f in range(2):
                    then(pool, s_kl[f], j + 1)
                for head in (0, 4):
                    part_of(g, k_place, k_lo, 0, head, 1, s_first)
                then(pool, s_qh, 2 * j + 2)
                for n in (0, 1):
                    part_of(g, q_place, q_hi, 0, 0, n, s_first)
                v_low(0)

                def low(n):
                    then(pool, s_hi, UNITS * j + n + 1)
                    lows_of(g, n, slice(2 * P, 3 * P)).then_inc(s_off, 1)

                for n in range(UNITS):
                    then(pool, s_s2, UNITS * j + n + 1)
                    m = s2[:, n % S_RING, :, 0:2 * P].rearrange("p r (a n) -> p r a n", a=2)
                    g.affine_select(out=m, in_=m, pattern=[[0, 2], [0, 2], [1, P]], compare_op=ALU.is_ge, fill=0.0,
                                    base=0, channel_multiplier=-1).then_inc(s_msk, 1)
                    if n == 1:
                        v_low(1)
                    if n >= 1:
                        low(n - 1)
                low(UNITS - 1)

            turn(0, False)
            with pool.Fori(1, TURNS) as j:
                turn(j, True)

            pool.wait_ge(s_lg, TURNS)
            pool.wait_ge(s_mask, 1)
            lg3 = lg[:, :].rearrange("p (t e) -> p t e", e=NEXP)
            g.tensor_tensor(lg3, lg3, mx[:, :].unsqueeze(2).broadcast_to([P, TILES, NEXP]), ALU.subtract)\
                .then_inc(s_ls, 1)

            pool.wait_ge(s_cols, 1)

            def one_hots(i, b, first=False):
                if not first:
                    then(pool, s_hotm, i - 1)
                g.tensor_copy(col_now[:, b, :], col_s[:, bass.ds(8 * i, TOPK)]).then_inc(s_pcol, 1)
                then(pool, s_pcol, i + 1)
                for k in range(SCALAR_HOTS + VECTOR_HOTS, TOPK):
                    ins = g.tensor_scalar(hot_s[:, b, k, :], H("slots"), col_now[:, b, k:k + 1], None, ALU.is_equal)
                ins.then_inc(s_phot, 1)

            one_hots(0, 0, first=True)
            one_hots(1, 1, first=True)
            with pool.Fori(1, TILES // 2) as r:
                for b in range(2):
                    one_hots(2 * r + b, b)

            pool.wait_ge(s_tok, 1)
            pool.wait_ge(s_h2d, 16 * TURNS + 16)

            def gather(index, slot):
                g.indirect_dma_start(out=xg[:, slot, :], out_offset=None, in_=h2_dram,
                                     in_offset=bass.IndirectOffsetOnAxis(ap=index, axis=0)).then_inc(s_xg[slot], 16)

            for slot in range(RING):
                gather(tok_of[:, slot:slot + 1], slot)
            with pool.Fori(1, SLOT_TILES // RING) as r:
                for slot in range(RING):
                    tile = RING * r + slot
                    then(pool, s_xt, tile - RING + 1)
                    g.tensor_copy(ti[:, slot:slot + 1], tok_of[:, bass.ds(tile, 1)]).then_inc(s_ti, 1)
                    then(pool, s_ti, tile - RING + 1)
                    gather(ti[:, slot:slot + 1], slot)

            pool.wait_ge(s_ystored, 1)
            pool.wait_ge(s_slots, 1)
            idx = slot_i[:, :].bitcast(U32)

            def choices(i, b):
                g.tensor_copy(ki[:, b, :], idx[:, bass.ds(8 * i, TOPK)]).then_inc(s_ki, 1)
                then(pool, s_ki, i + 1)
                for k in range(TOPK):
                    g.indirect_dma_start(out=yg[:, b, k, :], out_offset=None, in_=y_dram,
                                         in_offset=bass.IndirectOffsetOnAxis(ap=ki[:, b, k:k + 1], axis=0))\
                        .then_inc(s_yg[b], 16)

            for t in range(TPG):
                choices(t, t)
            with pool.Fori(1, TURNS) as j:
                for t in range(TPG):
                    i = TPG * j + t
                    then(pool, s_acc, i - TPG + 1)
                    choices(i, t)


def constants():
    import numpy as np
    cst = np.zeros((P, NCST), np.float32)

    def put(name, a):
        lo, _ = CST[name]
        a = np.asarray(a, np.float32)
        cst[0:a.shape[0], lo:lo + a.shape[1]] = a

    head = np.arange(P) // D
    same = (head[:, None] == head[None, :]).astype(np.float32)
    centre = np.eye(P, dtype=np.float32) - same / np.float32(D)
    swap = np.arange(P) ^ (D // 2)
    put("ident", np.eye(P))
    put("centre", centre)
    put("centre_swap", centre[swap])
    put("var", same / np.float32(D))
    inv = (np.float32(1.0) / np.float32(10000.0) ** (np.arange(0, D, 2, dtype=np.float32) / np.float32(D))).astype(np.float32)
    ang = np.arange(N, dtype=np.float32)[None, :] * inv[:, None]
    half = np.arange(P) % (D // 2)
    first = (np.arange(P) % D < D // 2)[:, None]
    put("cos", np.cos(ang)[half])
    put("sin", np.where(first, np.sin(ang)[half], -np.sin(ang)[half]))
    put("one", np.ones((P, 1)))
    put("eps", np.full((P, 1), EPS))
    put("token", np.arange(P)[:, None] + P * np.arange(TILES)[None, :])
    put("steps", np.tile(P * np.arange(TOK // P)[None, :], (P, 1)))
    hst = np.zeros((P, NHST), np.float16)

    def put16(name, a):
        lo, _ = HST[name]
        a = np.asarray(a, np.float16)
        hst[0:a.shape[0], lo:lo + a.shape[1]] = a

    put16("before", np.triu(np.ones((P, P)), 1))
    put16("ones", np.ones((P, P)))
    put16("exp_before", np.triu(np.ones((NEXP, NEXP)), 1))
    put16("exp_upto", np.triu(np.ones((NEXP, NEXP)), 0))
    put16("tiles", np.tile(np.arange(SLOT_TILES)[None, :], (P, 1)))
    put16("slots", np.tile(np.arange(P)[None, :], (P, 1)))
    return cst, hst


def kernel(L0_attn_x, L0_attn_w_qkv, L0_attn_w_out, L0_attn_ln_scale, L0_attn_ln_bias, L0_ffn_gate_w,
           L0_ffn_experts_w1, L0_ffn_experts_w2, L0_ffn_shared_gate_up, L0_ffn_shared_down, L0_c, L0_wmod):
    import numpy as np
    import concourse.bacc as bacc
    from concourse.bass_utils import run_bass_kernel_spmd

    def lay(a):
        return np.ascontiguousarray(a)

    cst, hst = constants()
    ln = np.stack([np.tile(np.asarray(L0_attn_ln_scale), P // D), np.tile(np.asarray(L0_attn_ln_bias), P // D)], axis=1)
    arrays = {
        "x": lay(L0_attn_x).reshape(TOK, E),
        "w_qkv": lay(L0_attn_w_qkv),
        "w_out": lay(L0_attn_w_out),
        "ln_cols": lay(ln),
        "gate_t": lay(np.asarray(L0_ffn_gate_w).T),
        "w1_t": lay(np.asarray(L0_ffn_experts_w1).transpose(0, 2, 1)),
        "w2_t": lay(np.asarray(L0_ffn_experts_w2).transpose(0, 2, 1)),
        "gu_t": lay(np.asarray(L0_ffn_shared_gate_up).T),
        "down_t": lay(np.asarray(L0_ffn_shared_down).T),
        "c_t": lay(np.asarray(L0_c).T),
        "wmod": lay(L0_wmod),
        "cst": cst,
        "hst": hst,
    }
    nc = bacc.Bacc("TRN2", target_bir_lowering=False, num_devices=1)
    args = [nc.dram_tensor(name, a.shape, mybir.dt.from_np(a.dtype), kind="ExternalInput").ap()
            for name, a in arrays.items()]
    out = nc.dram_tensor("out", (TOK, E), F32, kind="ExternalOutput").ap()
    build(nc, *args, out)
    r = run_bass_kernel_spmd(nc, [arrays], core_ids=[0])
    return r.results[0]["out"].reshape(B, N, E)
```
